# Optimizing a Trainium2 kernel written in Bass

```python
import numpy as np
import jax
import jax.numpy as jnp

def _softmax(x, axis=-1):
    return jax.nn.softmax(x, axis=axis)

def _gelu(x):
    return jax.nn.gelu(x, approximate=True)

def _silu(x):
    return jax.nn.silu(x)

def _sigmoid(x):
    return jax.nn.sigmoid(x)

def _layernorm(x, axis=-1, eps=1e-05):
    m = jnp.mean(x, axis=axis, keepdims=True)
    v = jnp.var(x, axis=axis, keepdims=True)
    return (x - m) / jnp.sqrt(v + eps)

def _scatter_add(tgt, idx, src, axis=0):
    return tgt.at[idx].add(src)

def _segment_sum(src, seg, n):
    return jax.ops.segment_sum(src, seg, n)
kernel_name = 'mk_gps_d1_gnn_r8_0a5db4'

def setup_inputs(seed: int=0):
    np.random.seed(seed)
    _w = jnp.asarray

    def _rec_inputs():
        import jax
        import jax.numpy as jnp
        _gk = jax.random.key(seed)
        x = -0.0002117 + 1 * jax.random.normal(jax.random.fold_in(_gk, 1), (1250, 1024), jnp.float32)
        src = jax.random.randint(jax.random.fold_in(_gk, 2), (40000,), 0, 1250, jnp.int32)
        dst = jnp.minimum((1250 * jax.random.uniform(jax.random.fold_in(_gk, 3), (40000,)) ** 2.0).astype(jnp.int32), 9999)
        _o = jnp.argsort(dst, stable=True)
        src = src[_o]
        dst = dst[_o]
        return (x, src, dst)
    x, src, dst = _rec_inputs()

    def _L0_gnn_setup():
        import jax, jax.numpy as jnp
        import numpy as np
        N_NODES = 3125
        N_EDGES = 50000
        D = 1024

        def _sage_layer(h, edge_src, edge_dst, deg_inv, W_self, W_neigh, b):
            msg = h[edge_src]
            agg = jax.ops.segment_sum(msg, edge_dst, num_segments=h.shape[0])
            mean = agg * deg_inv[:, None]
            return h @ W_self + mean @ W_neigh + b
        key = jax.random.key(seed)
        ks = jax.random.split(key, 8)
        s = 1.0 / np.sqrt(D)
        return {'x': jax.random.normal(ks[0], (N_NODES, D), dtype=jnp.float32), 'edge_src': jax.random.randint(ks[1], (N_EDGES,), 0, N_NODES, dtype=jnp.int32), 'edge_dst': jax.random.randint(ks[2], (N_EDGES,), 0, N_NODES, dtype=jnp.int32), 'W_self0': jax.random.normal(ks[3], (D, D), dtype=jnp.float32) * s, 'W_neigh0': jax.random.normal(ks[4], (D, D), dtype=jnp.float32) * s, 'b0': jnp.zeros((D,), dtype=jnp.float32), 'W_self1': jax.random.normal(ks[5], (D, D), dtype=jnp.float32) * s, 'W_neigh1': jax.random.normal(ks[6], (D, D), dtype=jnp.float32) * s, 'b1': jnp.zeros((D,), dtype=jnp.float32)}
    _L0_gnn_all = _L0_gnn_setup()
    _L0_gnn_in = {k: v for k, v in _L0_gnn_all.items() if k in ('W_self0', 'W_neigh0', 'b0', 'W_self1', 'W_neigh1', 'b1')}
    del _L0_gnn_all

    def _L0_mix_setup():
        import jax, jax.numpy as jnp
        import numpy as np
        B, L, D, P = (4, 512, 1024, 256)
        EPS = 1e-08

        def _feature_map(x):
            return jax.nn.elu(x) + 1.0
        key = jax.random.key(seed)
        kx, kq, kk, kv, kp = jax.random.split(key, 5)
        x = jax.random.normal(kx, (B, L, D), dtype=jnp.float32)
        scale = 1.0 / np.sqrt(D)
        Wq = jax.random.uniform(kq, (D, D), jnp.float32, -scale, scale)
        Wk = jax.random.uniform(kk, (D, D), jnp.float32, -scale, scale)
        Wv = jax.random.uniform(kv, (D, D), jnp.float32, -scale, scale)
        g = jax.random.normal(kp, (D, P), dtype=jnp.float32)
        proj, _ = jnp.linalg.qr(g, mode='reduced')
        return {'x': x, 'Wq': Wq, 'Wk': Wk, 'Wv': Wv, 'proj': proj}
    _L0_mix_all = _L0_mix_setup()
    _L0_mix_in = {k: v for k, v in _L0_mix_all.items() if k in ('Wq', 'Wk', 'Wv', 'proj')}
    del _L0_mix_all

    def _L0_ffn_setup():
        import jax, jax.numpy as jnp
        import numpy as np
        N_HEADS = 16
        NUM_EXPERTS = 4
        TOP_K = 2
        D_MODEL = 1024
        GATE_HID = 128
        key = jax.random.key(seed)
        ks = jax.random.split(key, 12)
        B, T, C, E = (2, 1024, D_MODEL, NUM_EXPERTS)
        s = 1.0 / np.sqrt(C)
        return {'hidden_states': jax.random.normal(ks[0], (B, T, C), jnp.float32), 'Wq': jax.random.normal(ks[1], (E, C, C), jnp.float32) * s, 'bq': jnp.zeros((E, C), jnp.float32), 'Wk': jax.random.normal(ks[2], (E, C, C), jnp.float32) * s, 'bk': jnp.zeros((E, C), jnp.float32), 'Wv': jax.random.normal(ks[3], (E, C, C), jnp.float32) * s, 'bv': jnp.zeros((E, C), jnp.float32), 'Wg1': jax.random.normal(ks[4], (C, GATE_HID), jnp.float32) * s, 'bg1': jnp.zeros((GATE_HID,), jnp.float32), 'Wg2': jax.random.normal(ks[5], (GATE_HID, E), jnp.float32) / np.sqrt(GATE_HID), 'bg2': jnp.zeros((E,), jnp.float32), 'Wo': jax.random.normal(ks[6], (C, C), jnp.float32) * s, 'bo': jnp.zeros((C,), jnp.float32)}
    _L0_ffn_all = _L0_ffn_setup()
    _L0_ffn_in = {k: v for k, v in _L0_ffn_all.items() if k in ('Wq', 'bq', 'Wk', 'bk', 'Wv', 'bv', 'Wg1', 'bg1', 'Wg2', 'bg2', 'Wo', 'bo')}
    del _L0_ffn_all
    return {'x': x, 'src': src, 'dst': dst, 'L0_gnn_W_self0': _L0_gnn_in['W_self0'], 'L0_gnn_W_neigh0': _L0_gnn_in['W_neigh0'], 'L0_gnn_b0': _L0_gnn_in['b0'], 'L0_gnn_W_self1': _L0_gnn_in['W_self1'], 'L0_gnn_W_neigh1': _L0_gnn_in['W_neigh1'], 'L0_gnn_b1': _L0_gnn_in['b1'], 'L0_mix_Wq': _L0_mix_in['Wq'], 'L0_mix_Wk': _L0_mix_in['Wk'], 'L0_mix_Wv': _L0_mix_in['Wv'], 'L0_mix_proj': _L0_mix_in['proj'], 'L0_ffn_Wq': _L0_ffn_in['Wq'], 'L0_ffn_bq': _L0_ffn_in['bq'], 'L0_ffn_Wk': _L0_ffn_in['Wk'], 'L0_ffn_bk': _L0_ffn_in['bk'], 'L0_ffn_Wv': _L0_ffn_in['Wv'], 'L0_ffn_bv': _L0_ffn_in['bv'], 'L0_ffn_Wg1': _L0_ffn_in['Wg1'], 'L0_ffn_bg1': _L0_ffn_in['bg1'], 'L0_ffn_Wg2': _L0_ffn_in['Wg2'], 'L0_ffn_bg2': _L0_ffn_in['bg2'], 'L0_ffn_Wo': _L0_ffn_in['Wo'], 'L0_ffn_bo': _L0_ffn_in['bo']}

def reference(x, src, dst, L0_gnn_W_self0, L0_gnn_W_neigh0, L0_gnn_b0, L0_gnn_W_self1, L0_gnn_W_neigh1, L0_gnn_b1, L0_mix_Wq, L0_mix_Wk, L0_mix_Wv, L0_mix_proj, L0_ffn_Wq, L0_ffn_bq, L0_ffn_Wk, L0_ffn_bk, L0_ffn_Wv, L0_ffn_bv, L0_ffn_Wg1, L0_ffn_bg1, L0_ffn_Wg2, L0_ffn_bg2, L0_ffn_Wo, L0_ffn_bo):
    import jax
    import jax.numpy as jnp

    def _L0_gnn_ref(x, edge_src, edge_dst, W_self0, W_neigh0, b0, W_self1, W_neigh1, b1):
        import jax, jax.numpy as jnp
        import numpy as np
        N_NODES = 3125
        N_EDGES = 50000
        D = 1024

        def _sage_layer(h, edge_src, edge_dst, deg_inv, W_self, W_neigh, b):
            msg = h[edge_src]
            agg = jax.ops.segment_sum(msg, edge_dst, num_segments=h.shape[0])
            mean = agg * deg_inv[:, None]
            return h @ W_self + mean @ W_neigh + b
        N = x.shape[0]
        deg = jax.ops.segment_sum(jnp.ones_like(edge_dst, dtype=x.dtype), edge_dst, num_segments=N)
        deg_inv = 1.0 / jnp.maximum(deg, 1.0)
        h = jax.nn.relu(_sage_layer(x, edge_src, edge_dst, deg_inv, W_self0, W_neigh0, b0))
        out = _sage_layer(h, edge_src, edge_dst, deg_inv, W_self1, W_neigh1, b1)
        return out

    def _L0_mix_ref(x, Wq, Wk, Wv, proj):
        import jax, jax.numpy as jnp
        import numpy as np
        B, L, D, P = (4, 512, 1024, 256)
        EPS = 1e-08

        def _feature_map(x):
            return jax.nn.elu(x) + 1.0
        q = jnp.einsum('bld,ed->ble', x, Wq)
        k = jnp.einsum('bld,ed->ble', x, Wk)
        v = jnp.einsum('bld,ed->ble', x, Wv)
        q_prime = _feature_map(q @ proj)
        k_prime = _feature_map(k @ proj)
        kv = jnp.einsum('blp,bld->bpd', k_prime, v)
        num = jnp.einsum('blp,bpd->bld', q_prime, kv)
        z = 1.0 / (jnp.sum(q_prime, axis=-1, keepdims=True) + EPS)
        return num * z

    def _L0_ffn_ref(hidden_states, Wq, bq, Wk, bk, Wv, bv, Wg1, bg1, Wg2, bg2, Wo, bo):
        import jax, jax.numpy as jnp
        import numpy as np
        N_HEADS = 16
        NUM_EXPERTS = 4
        TOP_K = 2
        D_MODEL = 1024
        GATE_HID = 128
        B, T, C = hidden_states.shape
        H = N_HEADS
        D = C // H
        pooled = hidden_states.mean(axis=1)
        logits = jax.nn.relu(pooled @ Wg1 + bg1) @ Wg2 + bg2
        vals, idx = jax.lax.top_k(logits, TOP_K)
        sm = jax.nn.softmax(vals, axis=-1)
        weights = jnp.zeros_like(logits).at[jnp.arange(B)[:, None], idx].set(sm)

        def moe_proj(W, b):
            Wc = jnp.einsum('be,ecd->bcd', weights, W)
            bc = weights @ b
            return jnp.einsum('btc,bcd->btd', hidden_states, Wc) + bc[:, None, :]
        q = moe_proj(Wq, bq).reshape(B, T, H, D)
        k = moe_proj(Wk, bk).reshape(B, T, H, D)
        v = moe_proj(Wv, bv).reshape(B, T, H, D)
        scores = jnp.einsum('bthd,bshd->bhts', q, k) / np.sqrt(D).astype(np.float32)
        attn = jax.nn.softmax(scores, axis=-1)
        out = jnp.einsum('bhts,bshd->bthd', attn, v).reshape(B, T, C)
        return out @ Wo + bo
    xn = _layernorm(x, axis=-1)
    x = x + _L0_gnn_ref(xn, src, dst, L0_gnn_W_self0, L0_gnn_W_neigh0, L0_gnn_b0, L0_gnn_W_self1, L0_gnn_W_neigh1, L0_gnn_b1) + _L0_mix_ref(xn[None], L0_mix_Wq, L0_mix_Wk, L0_mix_Wv, L0_mix_proj)[0]
    x = x + _L0_ffn_ref(_layernorm(x, axis=-1)[None], L0_ffn_Wq, L0_ffn_bq, L0_ffn_Wk, L0_ffn_bk, L0_ffn_Wv, L0_ffn_bv, L0_ffn_Wg1, L0_ffn_bg1, L0_ffn_Wg2, L0_ffn_bg2, L0_ffn_Wo, L0_ffn_bo)[0]
    return x

_drawn_inputs = setup_inputs


def setup_inputs(seed=0):
    import zlib

    import numpy as np

    out = dict(_drawn_inputs(seed))
    spreads = {'L0_gnn_b0': (0.0, 0.8),
     'L0_gnn_b1': (0.0, 0.8),
     'L0_ffn_bq': (0.0, 2.0),
     'L0_ffn_bk': (0.0, 2.0),
     'L0_ffn_bv': (0.0, 2.0),
     'L0_ffn_bg1': (0.0, 2.0),
     'L0_ffn_bg2': (0.0, 2.0),
     'L0_ffn_bo': (0.0, 0.8)}
    factors = {'L0_gnn_W_neigh0': 8.0, 'L0_ffn_Wq': 64.0, 'L0_ffn_Wk': 64.0, 'L0_ffn_Wg1': 2.721}
    for name, (base, spread) in spreads.items():
        noise = np.random.default_rng([zlib.crc32(name.encode()), seed]).standard_normal(out[name].shape)
        drawn = base * np.exp(spread * noise) if base else spread * noise
        out[name] = jnp.asarray(drawn.astype(out[name].dtype))
    for name, factor in factors.items():
        out[name] = (out[name] * factor).astype(out[name].dtype)
    return out
```

```python
import concourse.bass as bass
from concourse import mybir
from contextlib import ExitStack


class Count:

    def __init__(self):
        self.n, self.turn, self.per = 0, None, 0

    def add(self):
        self.n += 1
        return self.n if self.turn is None else self.turn * self.per + self.n

    def enter(self, turn, per):
        self.turn, self.per, self.start = turn, per, self.n

    def leave(self, turns):
        assert self.n - self.start == self.per, (self.n - self.start, self.per)
        self.turn, self.n = None, self.start + self.per * turns


def gps_layer_kernel(nc, x, src, dst, W_self0, W_neigh0, b0, W_self1, W_neigh1, b1,
                     mWq, mWk, mWv, proj, fWq, fbq, fWk, fbk, fWv, fbv, Wg1, bg1, Wg2, bg2,
                     Wo, bo, out, adj, base, y0hi, y0lo, s0T, y1hi, y1lo, x2d, qhi, qlo, khi, klo,
                     degrow):
    f32, f32r = mybir.dt.float32, mybir.dt.float32r
    bf16, f16, i32 = mybir.dt.bfloat16, mybir.dt.float16, mybir.dt.int32
    u32 = mybir.dt.uint32
    ALU, ACT, AX = mybir.AluOpType, mybir.ActivationFunctionType, mybir.AxisListType
    ds = bass.ds

    R, D = x.shape
    T = 125
    NT = R // T
    KB = D // 128
    E = src.shape[0]
    ET = E // T
    GE = 4
    NG = ET // GE
    PF_ = proj.shape[1]
    PB = PF_ // 128
    DW = 32
    NW = -(-R // DW)
    AW = NW * DW
    KW = NT * DW
    NE = fWq.shape[0]
    H, HD = 16, 64
    WQ = 256
    NQ = D // WQ
    CH = [(0, 418), (418, 416), (834, 416)]
    CM = CH[0][1]
    SCH = [(0, 512), (512, 512), (1024, R - 1024)]
    SCALE = 0.125
    FAST_MAX = 4096.0
    assert R == NT * T and E == ET * T and ET == NG * GE and NW % 2 == 0

    ctx = ExitStack()
    with ctx:
        def sb(name, shape, dt=f32):
            return ctx.enter_context(nc.sbuf_tensor(name, shape, dt))

        def sem(name):
            return ctx.enter_context(nc.semaphore(name))

        ident = sb("ident", [128, 128])
        ones = sb("ones", [128, 128])
        onesr = sb("onesr", [128, 2], f32r)
        b0c = sb("b0c", [128, KB])
        deginvB = sb("deginvB", [128, R])
        deginv = sb("deginv", [T, NT])
        degmax = sb("degmax", [1, 2])
        slow = sb("slow", [1, 1], i32)
        st6 = sb("st6", [T, 2, 6])
        mv = sb("mv", [T, 8])
        zcol = sb("zcol", [T, 2])
        qkb = sb("qkb", [128, 2 * KB])
        pooled = sb("pooled", [128, NT, KB])
        pool8 = sb("pool8", [128, KB])
        gate = sb("gate", [1, 64])
        gidx = sb("gidx", [1, 8], u32)
        gidxf = sb("gidxf", [1, 8])
        hid = sb("hid", [128, 1])
        wsel = sb("wsel", [128, 2])
        w4 = sb("w4", [NE, 128])
        iot4 = sb("iot4", [1, NE])
        att_m = sb("att_m", [T, 2, 4])
        att_r = sb("att_r", [T, 2, 2])

        ARENA = 203136
        base_at = nc.sbuf_base
        base_at += -base_at % 32
        arena = sb("arena", [128, ARENA // 4])

        def at(name, shape, dt, offset):
            return nc.alloc_sbuf_tensor_at(name, shape, dt, offset=base_at + offset)

        XTh = at("XTh", [128, KB, R], f32r, 0)
        XTl = at("XTl", [128, KB, R], f32r, 40000)
        o = 80000
        Wst = at("Wst", [128, 2, KB // 2, WQ], f32, o)
        o += 8192
        Wh = [at(f"Wh{i}", [128, KB, WQ], f32r, o + 8192 * i) for i in range(2)]
        Wl = [at(f"Wl{i}", [128, KB, WQ], f32r, o + 16384 + 8192 * i) for i in range(2)]
        o += 32768
        G0 = o
        adj_sb = at("adj_sb", [T, NT, AW], f32, 0)
        raw = at("raw", [NG, 2, GE * T], i32, 51200)
        ef = at("ef", [NG, 6, GE * T], f32, 55200+32)
        dhi_i = at("dhi_i", [NG, GE * T], i32, 67232)
        slo = at("slo", [T, ET], f32, 69248)
        key = at("key", [T, ET], f32, 70528)
        iot = at("iot", [128, KW], f16, 71776 + 32)
        tk = at("tk", [128, NW], f32, 72448)
        iotw = at("iotw", [128, NW], f32, 72608)
        pcol = at("pcol", [128, 2], f32, 72768)
        ohs = at("ohs", [T, GE, 128], bf16, 72800)
        ohk = at("ohk", [T, GE, KW], bf16, 73824)
        zw = at("zw", [T, 128], bf16, 76384)
        gmm = at("gmm", [NG, 2], f32, 76640)
        cond = at("cond", [NG, 3, NW], f32, 76672)
        bnd = at("bnd", [NW, 2], f32, 77152+32)
        brow = at("brow", [1, 4, NW], f32, 77216)
        bint = at("bint", [1, 2, NW], i32, 77856)
        degp = at("degp", [T, 2, R], f32, G0 + 36864)
        Mqh = at("Mqh", [128, KB, PF_], f32r, G0)
        Mql = at("Mql", [128, KB, PF_], f32r, G0 + 8192)
        Mkh = at("Mkh", [128, KB, PF_], f32r, G0 + 16384)
        Mkl = at("Mkl", [128, KB, PF_], f32r, G0 + 24576)
        L = G0 + 32768
        prh = at("prh", [128, KB, PF_], f32r, L)
        prl = at("prl", [128, KB, PF_], f32r, L + 8192)
        prf = at("prf", [128, KB, PF_], f32, L + 16384)
        xs = at("xs", [T, 2, D], f32, L)
        xn = at("xn", [T, 2, D], f32, L + 8192)
        xnh = [at(f"xnh{i}", [T, D], f32r, L + 16384 + 4096 * i) for i in range(2)]
        xnl = [at(f"xnl{i}", [T, D], f32r, L + 24576 + 4096 * i) for i in range(2)]
        kph = at("kph", [T, 2, PF_], f32r, L + 32768)
        kpl = at("kpl", [T, 2, PF_], f32r, L + 34816)
        qph = at("qph", [128, PB, R], f32r, L)
        qpl = at("qpl", [128, PB, R], f32r, L + 10016)
        GTh = at("GTh", [128, KB, PF_], f32r, L + 20032)
        GTl = at("GTl", [128, KB, PF_], f32r, L + 28224)
        elm = at("elm", [128, 2, CM], f32, L + 36864)
        elf = at("elf", [128, 2, CM], f32, L + 40224)
        kvh = at("kvh", [128, PB, D], f32r, G0 + 16384)
        kvl = at("kvl", [128, PB, D], f32r, G0 + 24576)
        xr = at("xr", [T, 2, D], f32, G0)
        bt2 = at("bt2", [T, 2, 512], f32, G0 + 8192)
        b1B = at("b1B", [T, D], f32, G0 + 12288)
        ot1 = [at(f"ot1{c}", [128, 4, CM], f32, G0 + 50048 + 6720 * c) for c in range(2)]
        ot2 = [at(f"ot2{c}", [128, 4, CM], f32, G0 + 16384 + 6720 * c) for c in range(2)]
        bs = at("bs", [T, 4, WQ], f32, G0 + 30720)
        adjr = at("adjr", [T, NT, R], f32r, G0)
        y0sh = [at(f"y0sh{i}", [T, NT, 128], f32r, G0 + 50016 + 10240 * i) for i in range(2)]
        y0sl = [at(f"y0sl{i}", [T, NT, 128], f32r, G0 + 55136 + 10240 * i) for i in range(2)]
        s0c = at("s0c", [128, 2, CM], f32, G0 + 70528)
        zt = at("zt", [128, 2, CM], f32, G0 + 73888)
        y1l = at("y1l", [T, NT, D], f32r, 80000)
        adt = [at(f"adt{i}", [T, NT, T], f32r, G0 + 5024 * i) for i in range(2)]
        b2 = at("b2", [T, 2, D], f32, G0 + 10048)
        x2s = at("x2s", [T, 2, D], f32, G0 + 18240)
        x2n = at("x2n", [T, 2, D], f32, G0 + 26432)
        V0 = G0 + 40960
        y1h = at("y1h", [T, NT, D], f32r, V0)
        wg1 = at("wg1", [128, KB, 128], f32, G0 + 34816)
        wg2 = at("wg2", [128, NE], f32, G0 + 38912)
        bgr = at("bgr", [1, 8], f32, G0 + 38944)
        bg1c = at("bg1c", [128, 1], f32, G0 + 38976)
        wst2 = at("wst2", [128, 2, 2, KB // 2, WQ], f32, G0)
        b3 = at("b3", [NE, 3, D], f32, V0)
        bvB = at("bvB", [T, D], f32, G0 + 30720)
        v = at("v", [T, NT, D], f32, V0)
        QS = [at(f"QS{i}", [128, R], f32r, 5024 * i) for i in range(2)]
        KH = [at(f"KH{i}", [128, R], f32r, 10048 + 5024 * i) for i in range(2)]
        KL = [at(f"KL{i}", [128, R], f32r, 20096 + 5024 * i) for i in range(2)]
        Pt = [at(f"Pt{i}", [T, R], f32, 30144 + 5024 * i) for i in range(2)]
        PT = [at(f"PT{i}", [T, NT, T], f32, 40192 + 5024 * i) for i in range(2)]
        ao = at("ao", [T, NT, D], f32, G0)
        x2r = at("x2r", [T, 4, WQ], f32, V0)
        ot = at("ot", [T, 4, WQ], f32, V0 + 4096)
        boB = at("boB", [T, D], f32, V0 + 8192)

        ps = ctx.enter_context(nc.psum_tensor("ps", [128, 8 * 512], f32))

        def bank(i, p=128, n=512, c=0):
            return ps[0:p, 512 * i + c:512 * i + c + n]

        names = ["Mq", "Mk", "GT", "QP", "KV", "NUM", "S0", "Y0", "HT", "Y1", "S1", "X2", "Q", "K", "V", "O"]
        tiles = [KB, KB, 4, PB * 3, 4 * PB, 2 * NT, 3 * KB, 4 * NT, 3 * KB, 4 * NT, 4 * NT, 2 * NT, 3 * KB, 3 * KB,
                 4 * NT, 4 * NT]
        split = {"Mq", "Mk", "GT", "KV", "Y0", "Y1", "Q", "K"}
        N, HI, STORED = {}, {}, {}
        n = h = 0
        st = 16
        for name, m in zip(names, tiles):
            N[name], HI[name], STORED[name] = n, h, st
            n += m
            h += m if name in split else 0
            if name in ("S0", "S1", "O"):
                st += 16 * (m // 4)
            if name in ("Y0", "Y1", "Q", "K"):
                st += 32 * (m // 4)
        END, ST_END = n, st
        ORDER = ["Mq", "Mk", "KV", "S0", "Y0", "Y1", "S1", "Q", "K", "V", "O"]
        SIZE = dict(zip(names, tiles))

        def slot_free(ph, u, i):
            k = ORDER.index(ph)
            before = 0 if k == 0 else N[ORDER[k - 1]] + SIZE[ORDER[k - 1]] * (3 + u) // 4
            same = N[ph] + SIZE[ph] * (1 + u) // 4
            if isinstance(i, int):
                return (before, same)[i]
            return i * (same - before) + before
        WRDY = {k: 4 * i for i, k in enumerate(["Mq", "Mk", "S0", "Y0", "Y1", "S1", "Q", "K", "V", "O"])}

        s_const = sem("s_const")
        s_edges = sem("s_edges")
        s_small = sem("s_small")
        s_passed = sem("s_passed")
        s_gw = sem("s_gw")
        s_eb = sem("s_eb")
        s_w = [sem(f"s_w{k}") for k in range(2)]
        s_we = [sem(f"s_we{k}") for k in range(2)]
        s_wv = sem("s_wv")
        s_gp = sem("s_gp")
        s_wready = sem("s_wready")
        s_acc = sem("s_acc")
        s_hi = sem("s_hi")
        s_done = sem("s_done")
        s_st = [sem(f"s_st{k}") for k in range(4)]
        s_dve = sem("s_dve")
        s_act = sem("s_act")
        s_proj = sem("s_proj")
        s_idx = sem("s_idx")
        s_idxT = sem("s_idxT")
        s_bnd = sem("s_bnd")
        s_oh = sem("s_oh")
        s_ohfree = sem("s_ohfree")
        s_win = sem("s_win")
        s_winev = sem("s_winev")
        s_degp = sem("s_degp")
        s_deg = sem("s_deg")
        s_dinv = sem("s_dinv")
        s_adj = sem("s_adj")
        s_row = sem("s_row")
        s_x = [sem(f"s_x{k}") for k in range(2)]
        s_xn = sem("s_xn")
        s_xh = sem("s_xh")
        s_xl = sem("s_xl")
        s_T = sem("s_T")
        s_Thi = sem("s_Thi")
        s_Tlo = sem("s_Tlo")
        s_kp = sem("s_kp")
        s_G = sem("s_G")
        s_elm = sem("s_elm")
        s_ele = sem("s_ele")
        s_elf = sem("s_elf")
        s_elh = sem("s_elh")
        s_ell = sem("s_ell")
        s_wt = sem("s_wt")
        s_wthi = sem("s_wthi")
        s_wtlo = sem("s_wtlo")
        s_z = sem("s_z")
        s_xr = [sem(f"s_xr{k}") for k in range(2)]
        s_bt = [sem(f"s_bt{k}") for k in range(2)]
        s_b1 = sem("s_b1")
        s_adjr = sem("s_adjr")
        s_y0 = [sem(f"s_y0{k}") for k in range(2)]
        s_s0 = [sem(f"s_s0{k}") for k in range(2)]
        s_zt = sem("s_zt")
        s_hh = sem("s_hh")
        s_bs = [sem(f"s_bs{k}") for k in range(4)]
        s_y1h = sem("s_y1h")
        s_y1l = sem("s_y1l")
        s_at = [sem(f"s_at{k}") for k in range(2)]
        s_b2 = [sem(f"s_b2{k}") for k in range(2)]
        s_x2 = [sem(f"s_x2{k}") for k in range(2)]
        s_x2n = sem("s_x2n")
        s_pool = sem("s_pool")
        s_gmm = sem("s_gmm")
        s_ghid = sem("s_ghid")
        s_gate = sem("s_gate")
        s_qk = [sem(f"s_qk{k}") for k in range(2)]
        s_s = sem("s_s")
        s_mx = sem("s_mx")
        s_exp = sem("s_exp")
        s_pt = sem("s_pt")
        s_ta = sem("s_ta")
        s_tb = sem("s_tb")
        s_pv = sem("s_pv")
        s_ev = sem("s_ev")
        s_x2r = [sem(f"s_x2r{k}") for k in range(4)]
        s_bo = sem("s_bo")

        block = ctx.enter_context(nc.Block())

        xt = x.rearrange("(t p) c -> t p c", p=T)

        def wait_apart(eng, sem_, value):
            eng.wait_ge(sem_, value)
            if not isinstance(value, int):
                eng.sem_inc(s_passed, 1)

        @block.sync
        def _(sp):
            for k in range(4):
                sp.sem_inc(s_st[k], 16)
            sp.dma_start(raw[:, 0, :], src.rearrange("(p e) -> p e", p=NG)).then_inc(s_edges, 16)
            sp.dma_start(raw[:, 1, :], dst.rearrange("(p e) -> p e", p=NG)).then_inc(s_edges, 16)
            sp.dma_start(prf[:, :, :], proj.rearrange("(k p) n -> p k n", p=128)).then_inc(s_proj, 16)
            with nc.allow_non_contiguous_dma(reason="one small column layout"):
                sp.dma_start(b0c[:, :], b0.rearrange("(k p) -> p k", p=128)).then_inc(s_small, 16)
            sp.wait_ge(s_winev, 2 + NW)
            sp.dma_start(adj.rearrange("(b p) d -> p b d", p=T), adj_sb[:, :, :]).then_inc(s_adj, 16)
            sp.wait_ge(s_dinv, 1)
            sp.dma_start(degrow.rearrange("(a n) -> a n", a=1), deginvB[0:1, :]).then_inc(s_row, 16)
            sp.wait_ge(s_row, 16)
            with nc.allow_non_contiguous_dma(reason="one small column layout"):
                sp.dma_start(deginv[:, :], degrow.rearrange("(t p) -> p t", p=T)).then_inc(s_row, 16)
            sp.wait_ge(s_acc, N["GT"])
            sp.wait_ge(s_done, 4 + N["GT"])
            for t in range(NT):
                if t >= 2:
                    sp.wait_ge(s_xn, t - 1)
                sp.dma_start(xs[:, t % 2, :], xt[t, :, :]).then_inc(s_x[t % 2], 16)
            sp.wait_ge(s_acc, N["KV"])
            sp.dma_start(b1B[:, :], b1.partition_broadcast(T)).then_inc(s_b1, 16)
            for t in range(NT + 1):
                if t < NT:
                    if t >= 2:
                        sp.wait_ge(s_done, 4 + N["NUM"] + 2 * (t - 1))
                    sp.dma_start(xr[:, t % 2, :], xt[t, :, :]).then_inc(s_xr[t % 2], 16)
                if t >= 1:
                    for c in range(2):
                        sp.wait_ge(s_done, 4 + N["NUM"] + 2 * (t - 1) + c + 1)
                        sp.dma_start(base[(t - 1) * T:t * T, 512 * c:512 * c + 512], bt2[:, c, :])\
                          .then_inc(s_bt[c], 16)
            sp.wait_ge(s_bt[0], 16 * NT)
            sp.wait_ge(s_bt[1], 16 * NT)
            sp.wait_ge(s_adj, 16)
            sp.dma_start(adjr[:, :, :].bitcast(f32), adj.rearrange("(b p) d -> p b d", p=T)[:, :, 0:R])\
              .then_inc(s_adjr, 16)

            def store_cols(ph, outs, tb, per_quarter_blocks=2):
                with sp.Fori(0, 2) as i:
                    for j in range(12):
                        u, b, c = j // 6, j // 3 % 2, j % 3
                        c0, cn = CH[c]
                        slot = (N[ph] + j) % 4
                        sp.wait_ge(s_done, i * 12 + (4 + N[ph] + j + 1))
                        for o_, t_ in zip(outs, tb):
                            dst_ = o_[ds(i * 512 + (2 * u + b) * 128, 128), c0:c0 + cn]
                            sp.dma_start(dst_, t_[:, slot, 0:cn]).then_inc(s_st[slot], 16)

            def store_rows(ph, outs, tb):
                with sp.Fori(0, 2) as i:
                    for j in range(2 * NT):
                        u, t = j // NT, j % NT
                        slot = (N[ph] + j) % 4
                        sp.wait_ge(s_done, i * (2 * NT) + (4 + N[ph] + j + 1))
                        for o_, t_ in zip(outs, tb):
                            sp.dma_start(o_[t * T:(t + 1) * T, ds(i * 512 + u * WQ, WQ)], t_[0:T, slot, 0:WQ])\
                              .then_inc(s_st[slot], 16)

            def stored(ph_next):
                for k in range(4):
                    sp.wait_ge(s_st[k], STORED[ph_next])

            store_cols("S0", [s0T], [ot1[0]])
            store_rows("Y0", [y0hi, y0lo], ot1)
            stored("HT")
            y0v = [a.rearrange("(s p) c -> p s c", p=T) for a in (y0hi, y0lo)]
            for blk in range(KB):
                if blk >= 2:
                    sp.wait_ge(s_acc, N["HT"] + 3 * (blk - 1))
                for a_, d_ in zip(y0v, (y0sh, y0sl)):
                    sp.dma_start(d_[blk % 2][:, :, :].bitcast(f32), a_[:, :, blk * 128:(blk + 1) * 128])\
                      .then_inc(s_y0[blk % 2], 16)
                for c, (c0, cn) in enumerate(CH):
                    m = 3 * blk + c
                    if m >= 2:
                        sp.wait_ge(s_zt, m - 1)
                    sp.dma_start(s0c[:, m % 2, 0:cn], s0T[blk * 128:(blk + 1) * 128, c0:c0 + cn])\
                      .then_inc(s_s0[m % 2], 16)
            store_rows("Y1", [y1hi, y1lo], ot2)
            stored("S1")
            y1v = [a.rearrange("(s p) c -> p s c", p=T) for a in (y1hi, y1lo)]
            sp.dma_start(y1h[:, :, :].bitcast(f32), y1v[0]).then_inc(s_y1h, 16)
            store_rows("S1", [base], [ot2[0]])
            stored("X2")
            sp.wait_ge(s_acc, N["X2"])
            sp.dma_start(y1l[:, :, :].bitcast(f32), y1v[1]).then_inc(s_y1l, 16)
            adv = adj.rearrange("(b p) d -> p b d", p=T)
            for t in range(NT + 1):
                if t < NT:
                    if t >= 2:
                        sp.wait_ge(s_acc, N["X2"] + 2 * (t - 1))
                    sp.dma_start(adt[t % 2][:, :, :].bitcast(f32), adv[:, :, t * T:(t + 1) * T])\
                      .then_inc(s_at[t % 2], 16)
                    if t >= 2:
                        sp.wait_ge(s_done, 4 + N["X2"] + 2 * (t - 1))
                    sp.dma_start(b2[:, t % 2, :], base[t * T:(t + 1) * T, :]).then_inc(s_b2[t % 2], 16)
                if t >= 1:
                    sp.wait_ge(s_done, 4 + N["X2"] + 2 * t)
                    sp.dma_start(x2d[(t - 1) * T:t * T, :], x2s[:, (t - 1) % 2, :]).then_inc(s_x2[(t - 1) % 2], 16)
                if t == 0:
                    sp.dma_start(wg1[:, :, :], Wg1.rearrange("(k p) n -> p k n", p=128)).then_inc(s_gw, 16)
                    sp.dma_start(wg2[:, :], Wg2).then_inc(s_gw, 16)
                    sp.dma_start(bgr[:, 0:NE], bg2.rearrange("(a n) -> a n", a=1)).then_inc(s_gw, 16)
                    with nc.allow_non_contiguous_dma(reason="one small column layout"):
                        sp.dma_start(bg1c[:, :], bg1.rearrange("(p a) -> p a", a=1)).then_inc(s_gw, 16)
            sp.wait_ge(s_acc, N["Q"])
            for k_, b_ in enumerate((fbq, fbk, fbv)):
                sp.dma_start(b3[:, k_, :], b_).then_inc(s_eb, 16)
            store_cols("Q", [qhi, qlo], ot2)
            store_cols("K", [khi, klo], ot2)
            stored("V")

            def head_stacks(hh, slot):
                for d_, a_, b_ in ((QS, qhi, qlo), (KH, khi, khi), (KL, klo, klo)):
                    sp.dma_start(d_[slot][0:HD, :].bitcast(f32), a_[ds(hh, HD), :] if not isinstance(hh, int)
                                 else a_[hh:hh + HD, :]).then_inc(s_qk[slot], 16)
                    sp.dma_start(d_[slot][HD:128, :].bitcast(f32), b_[ds(hh, HD), :] if not isinstance(hh, int)
                                 else b_[hh:hh + HD, :]).then_inc(s_qk[slot], 16)

            sp.wait_ge(s_acc, N["O"])
            head_stacks(0, 0)
            head_stacks(HD, 1)
            with sp.Fori(0, H // 2 - 1) as i:
                for u in range(2):
                    sp.wait_ge(s_s, i * (2 * NT) + NT * (u + 1))
                    head_stacks(sp.snap(i * 128 + (2 + u) * HD), u)
            sp.wait_ge(s_pv, H * NT)
            sp.dma_start(boB[:, :], bo.partition_broadcast(T)).then_inc(s_bo, 16)
            store_rows("O", [out], [ot])
            for k in range(4):
                sp.wait_ge(s_st[k], ST_END)
            sp.wait_ge(s_x2[0], 16 * (NT // 2))
            sp.wait_ge(s_x2[1], 16 * (NT // 2))

        @block.gpsimd
        def _(g):
            g.sem_inc(s_wready, 2)
            g.memset(ident[:, :], 0.0).then_inc(s_gp, 1)
            g.memset(ones[:, :], 1.0).then_inc(s_const, 1)
            g.wait_ge(s_gp, 1)
            g.affine_select(out=ident[:, :], in_=ident[:, :], compare_op=ALU.not_equal, fill=1.0,
                            base=0, pattern=[[-1, 128]], channel_multiplier=1).then_inc(s_const, 1)
            imp = dict(allow_small_or_imprecise_dtypes=True)
            g.iota(iot[:, :], pattern=[[1, KW]], base=0, channel_multiplier=0, **imp).then_inc(s_const, 1)
            g.iota(tk[:, :], pattern=[[KW, NW]], base=0, channel_multiplier=0, **imp).then_inc(s_const, 1)
            g.iota(iotw[:, :], pattern=[[1, NW]], base=0, channel_multiplier=0, **imp).then_inc(s_const, 1)
            g.iota(iot4[:, :], pattern=[[1, NE]], base=0, channel_multiplier=0, **imp).then_inc(s_const, 1)
            g.iota(pcol[:, 0:1], pattern=[[0, 1]], base=NG, channel_multiplier=-1, **imp).then_inc(s_const, 1)
            g.iota(pcol[:, 1:2], pattern=[[0, 1]], base=1, channel_multiplier=1, **imp).then_inc(s_const, 1)

            gp = [1]

            def split_half(w, u, kh, hi_value):
                g.tensor_copy(Wh[u][:, 4 * kh:4 * kh + 4, :], w).then_inc(s_gp, 1)
                g.wait_ge(s_gp, hi_value)
                g.tensor_sub(Wl[u][:, 4 * kh:4 * kh + 4, :], w, Wh[u][:, 4 * kh:4 * kh + 4, :].bitcast(f32))\
                 .then_inc(s_wready, 1)

            def cols_(i, u):
                c0 = i * 512 + u * WQ
                return slice(c0, c0 + WQ) if isinstance(i, int) else ds(c0, WQ)

            def quarters(ph, w, loads):
                wv = w.rearrange("(k p) n -> p k n", p=128)
                with (ExitStack() if ph == "Mq" else g.Fori(0, 2)) as turn:
                    for i, u in [(0, 0), (0, 1), (1, 0), (1, 1)] if ph == "Mq" else [(turn, 0), (turn, 1)]:
                        g.wait_ge(s_wready, i * 4 + (2 * (WRDY[ph] + u) + 2))
                        for kh in range(2):
                            g.dma_start(Wst[:, kh, :, :], wv[:, 4 * kh:4 * kh + 4, cols_(i, u)])\
                             .then_inc(s_w[kh], 16)
                        for kh in range(2):
                            wait_apart(g, s_w[kh], i * 32 + 16 * (loads + u + 1))
                            if kh == 0:
                                free = slot_free(ph, u, i)
                                if not isinstance(free, int) or free > 0:
                                    wait_apart(g, s_acc, free)
                            split_half(Wst[:, kh, :, :], u, kh, i * 4 + (gp[0] + 2 * u + kh + 1))
                gp[0] += 8

            quarters("Mq", mWq, 0)
            quarters("Mk", mWk, 4)
            for t in range(NT):
                g.wait_ge(s_xh, t + 1)
                if t >= 2:
                    g.wait_ge(s_G, t - 1)
                g.tensor_sub(xnl[t % 2][:, :], xn[:, t % 2, :], xnh[t % 2][:, :].bitcast(f32)).then_inc(s_xl, 1)
            wst_rows = Wst[:, :, :, :].rearrange("p a b c -> p (a b c)").rearrange("p (e n) -> p e n", e=2)
            g.wait_ge(s_wready, 2 * WRDY["S0"] + 2)
            for j in range(4):
                if j:
                    g.wait_ge(s_wt, 4 * j)
                g.dma_start(wst_rows, mWv[j * WQ:(j + 1) * WQ, :].rearrange("(e p) n -> p e n", p=128))\
                 .then_inc(s_wv, 16)
            g.wait_ge(s_wt, 16)
            quarters("S0", W_self0, 8)
            quarters("Y0", W_neigh0, 12)
            quarters("Y1", W_neigh1, 16)
            quarters("S1", W_self1, 20)
            g.wait_ge(s_gate, 1)
            e1 = g.value_load(gidx[0:1, 0:1], min_val=0, max_val=NE - 1)
            e2 = g.value_load(gidx[0:1, 1:2], min_val=0, max_val=NE - 1)

            def expert_quarters(ph, w, first):
                wv = w.rearrange("e (k p) n -> p e k n", p=128)
                with g.Fori(0, 2) as i:
                    for u in range(2):
                        g.wait_ge(s_wready, i * 4 + (2 * (WRDY[ph] + u) + 2))
                        for kh in range(2):
                            for a, e in enumerate((e1, e2)):
                                g.dma_start(wst2[:, kh, a, :, :],
                                            wv[:, ds(e, 1), 4 * kh:4 * kh + 4, ds(i * 512 + u * WQ, WQ)]
                                            .rearrange("p e k n -> p (e k) n")).then_inc(s_we[kh], 16)
                        for kh in range(2):
                            c = gp[0] + 5 * (2 * u + kh) - 0
                            sa, sb_ = wst2[:, kh, 0, :, :], wst2[:, kh, 1, :, :]
                            wait_apart(g, s_we[kh], i * 64 + 32 * (first + u + 1))
                            g.tensor_scalar(sa, sa, wsel[:, 0:1], None, ALU.mult).then_inc(s_gp, 1)
                            g.tensor_scalar(sb_, sb_, wsel[:, 1:2], None, ALU.mult).then_inc(s_gp, 1)
                            wait_apart(g, s_gp, i * 16 + (gp[0] + 4 * (2 * u + kh) + 2))
                            g.tensor_add(sa, sa, sb_).then_inc(s_gp, 1)
                            wait_apart(g, s_gp, i * 16 + (gp[0] + 4 * (2 * u + kh) + 3))
                            if kh == 0:
                                wait_apart(g, s_acc, slot_free(ph, u, i))
                            split_half(sa, u, kh, i * 16 + (gp[0] + 4 * (2 * u + kh) + 4))
                gp[0] += 32

            expert_quarters("Q", fWq, 0)
            expert_quarters("K", fWk, 4)
            expert_quarters("V", fWv, 8)
            quarters("O", Wo, 24)

        @block.scalar
        def _(act):
            act.sem_inc(s_winev, 2)
            act.sem_inc(s_ta, 1)
            own = Count()

            def order(ins):
                ins.then_inc(s_act, 1)
                act.wait_ge(s_act, own.add())

            def highs(ph, loops, per, dst_of, bias_of=None, p=128, cols=None, slots=0, uses=0):
                with act.Fori(0, loops) as i:
                    for j in range(per):
                        slot = (N[ph] + j) % 4
                        n_ = cols(j)
                        wait_apart(act, s_acc, i * per + (N[ph] + j + 1))
                        if uses:
                            wait_apart(act, s_st[slot], i * (uses * per // 4) + (STORED[ph] + uses * (j // 4)))
                        b_ = bias_of(i, j) if bias_of else 0.0
                        act.activation(dst_of(i, j).bitcast(f32r) if uses else dst_of(i, j), bank(slot, p, n_),
                                       ACT.Identity if bias_of else ACT.Copy, bias=b_).then_inc(s_hi, 1)

            highs("Mq", 2, 4, lambda i, j: Mqh[:, ds(i * 4 + j, 1), :].rearrange("p a n -> p (a n)"), cols=lambda j: PF_)
            highs("Mk", 2, 4, lambda i, j: Mkh[:, ds(i * 4 + j, 1), :].rearrange("p a n -> p (a n)"), cols=lambda j: PF_)
            with act.Fori(0, NW // 2) as i:
                for u in range(2):
                    wait_apart(act, s_win, i * 2 + (u + 1))
                    act.copy(adj_sb[:, :, ds(i * (2 * DW) + u * DW, DW)],
                             bank(4 + u, T, KW).rearrange("p (b d) -> p b d", d=DW)).then_inc(s_winev, 1)

            def transposed_hi(t, m):
                for b in range(2):
                    act.wait_ge(s_T, m(b))
                    act.copy(XTh[:, 4 * b:4 * b + 4, t], bank(4 + b, 128, 4 * T).rearrange("p (k n) -> p k n", n=T))\
                       .then_inc(s_Thi, 1)

            def feature_exp(m, p, n_):
                act.wait_ge(s_elm, m + 1)
                act.activation(elm[0:p, m % 2, 0:n_], elm[0:p, m % 2, 0:n_], ACT.Exp).then_inc(s_ele, 1)

            act.wait_ge(s_adj, 16)
            act.wait_ge(s_degp, 1)
            for t in range(NT + 1):
                if t < NT:
                    act.wait_ge(s_xn, t + 1)
                    if t >= 2:
                        act.wait_ge(s_G, t - 1)
                    act.copy(xnh[t % 2][:, :], xn[:, t % 2, :]).then_inc(s_xh, 1)
                    transposed_hi(slice(t * T, (t + 1) * T), lambda b: 2 * t + b + 1)
                if t >= 1:
                    m = t - 1
                    feature_exp(m, T, PF_)
                    act.wait_ge(s_elf, m + 1)
                    if m >= 2:
                        act.wait_ge(s_G, m - 1)
                    act.copy(kph[:, m % 2, :], elf[0:T, m % 2, 0:PF_]).then_inc(s_elh, 1)
            act.wait_ge(s_acc, N["GT"] + 4)
            for j in range(4):
                act.copy(GTh[:, 2 * j:2 * j + 2, :].rearrange("p a n -> p (a n)"), bank(j)).then_inc(s_hi, 1)
            for j in range(PB * 3):
                c0, cn = CH[j % 3]
                feature_exp(NT + j, 128, cn)
                act.wait_ge(s_elf, NT + j + 1)
                act.copy(qph[:, j // 3, c0:c0 + cn], elf[:, (NT + j) % 2, 0:cn]).then_inc(s_elh, 1)
            for j in range(4):
                for b in range(4):
                    act.wait_ge(s_wt, 4 * j + b + 1)
                    if b == 0:
                        act.wait_ge(s_acc, slot_free("KV", j % 2, j // 2))
                    act.copy(Wh[j % 2][:, 2 * b:2 * b + 2, :].rearrange("p a n -> p (a n)"), bank(4 + b))\
                       .then_inc(s_wthi, 1)
                for b in range(PB):
                    m = PB * j + b
                    act.wait_ge(s_acc, N["KV"] + m + 1)
                    act.copy(kvh[:, b, j * WQ:(j + 1) * WQ], bank((N["KV"] + m) % 4, 128, WQ)).then_inc(s_hi, 1)
            highs("Y0", 2, 2 * NT, lambda i, j: ot1[0][0:T, (N["Y0"] + j) % 4, 0:WQ], p=T, cols=lambda j: WQ, uses=32)
            for m in range(3 * KB):
                c0, cn = CH[m % 3]
                act.wait_ge(s_zt, m + 1)
                act.copy(XTh[:, m // 3, c0:c0 + cn], zt[:, m % 2, 0:cn]).then_inc(s_hh, 1)
            highs("Y1", 2, 2 * NT, lambda i, j: ot2[0][0:T, (N["Y1"] + j) % 4, 0:WQ], p=T, cols=lambda j: WQ, uses=32)
            with act.Fori(0, 2) as i:
                for j in range(2 * NT):
                    slot, u, t = (N["S1"] + j) % 4, j // NT, j % NT
                    act.wait_ge(s_done, i * (2 * NT) + (N["S1"] + j + 1))
                    act.dma_start(bs[:, slot, :], base[t * T:(t + 1) * T, ds(i * 512 + u * WQ, WQ)])\
                       .then_inc(s_bs[slot], 16)

            for t in range(NT):
                transposed_hi(slice(t * T, (t + 1) * T), lambda b: 2 * (NT + t) + b + 1)
            act.wait_ge(s_gmm, 1)
            act.wait_ge(s_gw, 16 * 4)
            act.activation(hid[:, :], bank(6, 128, 1), ACT.Relu, bias=bg1c[:, 0:1]).then_inc(s_ghid, 1)
            act.wait_ge(s_pool, 2)
            act.activation(gate[:, 33:34], gate[:, 32:33], ACT.Exp).then_inc(s_ghid, 1)
            for k in range(2):
                act.wait_ge(s_x2[k], 16 * (NT // 2))
            for a, ph in enumerate(("Q", "K")):
                highs(ph, 2, 12, lambda i, j: ot2[0][:, (N[ph] + j) % 4, 0:CH[j % 3][1]],
                      bias_of=lambda i, j: qkb[:, ds(i * 4 + (KB * a + j // 3), 1)], cols=lambda j: CH[j % 3][1], uses=32)

            def exps(m, i, first):
                n = lambda k, c: i * (2 * NT * k) + (m * k + c) if not first else m * k + c
                s = m % 2
                act.wait_ge(s_mx, n(1, 1))
                act.activation(Pt[s][:, :], ps[0:T, 1536 * s:1536 * s + R], ACT.Exp, bias=att_m[:, s, 2:3],
                               scale=SCALE, accum_out=att_r[:, s, 0:1]).then_inc(s_exp, 1)
                for c, b0_, nb in ((0, 0, 4), (2, 8, 2)):
                    act.wait_ge(s_pt, n(3, c + 1))
                    act.copy(PT[s][:, b0_:b0_ + nb, :], bank(6 + (3 * m + c) % 2, T, nb * T)
                             .rearrange("p (b n) -> p b n", n=T)).then_inc(s_ta, 1)

            with act.Fori(0, H // 2) as i:
                for m in range(2 * NT):
                    exps(m, i, False)
            for t in range(NT):
                transposed_hi(slice(t * T, (t + 1) * T), lambda b: 2 * (2 * NT + t) + b + 1)
            with act.Fori(0, 2) as i:
                for j in range(2 * NT):
                    slot, u, t = (N["O"] + j) % 4, j // NT, j % NT
                    act.wait_ge(s_done, i * (2 * NT) + (N["O"] + j + 1))
                    act.dma_start(x2r[:, slot, :], x2d[t * T:(t + 1) * T, ds(i * 512 + u * WQ, WQ)])\
                       .then_inc(s_x2r[slot], 16)

        @block.vector
        def _(dve):
            v_ = nc.vector
            dve.sem_inc(s_done, 4)
            dve.sem_inc(s_tb, 1)
            own = Count()

            def order(ins):
                ins.then_inc(s_dve, 1)
                dve.wait_ge(s_dve, own.add())

            def flat(a):
                return a.rearrange("p a n -> p (a n)")

            v_.memset(zw[:, :], 0.0).then_inc(s_const, 1)
            dve.wait_ge(s_const, 9)
            v_.tensor_copy(onesr[:, :], ones[:, 0:2]).then_inc(s_const, 1)
            dve.wait_ge(s_proj, 16)
            order(v_.tensor_copy(prh[:, :, :], prf[:, :, :]))
            v_.tensor_sub(prl[:, :, :], prf[:, :, :], prh[:, :, :].bitcast(f32)).then_inc(s_proj, 1)

            dve.wait_ge(s_edges, 32)
            sf, df, hf, bf_, slf, kf = (ef[:, k, :] for k in range(6))
            v_.tensor_copy(sf, raw[:, 0, :]).then_inc(s_dve, 1); own.add()
            v_.tensor_copy(df, raw[:, 1, :]).then_inc(s_dve, 1); own.add()
            order(v_.tensor_scalar(dhi_i[:, :], raw[:, 1, :], 5, None, ALU.logical_shift_right))
            order(v_.tensor_copy(hf, dhi_i[:, :]))
            order(v_.tensor_scalar(bf_, sf, float(T), None, ALU.is_ge))
            for b in range(2, NT):
                order(v_.scalar_tensor_tensor(bf_, sf, float(T * b), bf_, ALU.is_ge, ALU.add))
            v_.scalar_tensor_tensor(slf, bf_, -float(T), sf, ALU.mult, ALU.add).then_inc(s_idx, 1)
            order(v_.scalar_tensor_tensor(kf, bf_, float(DW), df, ALU.mult, ALU.add))
            v_.scalar_tensor_tensor(kf, hf, float(KW - DW), kf, ALU.mult, ALU.add).then_inc(s_idx, 1)
            order(v_.tensor_reduce(gmm[:, 0:1], hf, AX.X, ALU.min))
            order(v_.tensor_reduce(gmm[:, 1:2], hf, AX.X, ALU.max))
            order(v_.tensor_scalar(cond[:, 0, :], iotw[0:NG, :], gmm[:, 0:1], None, ALU.is_ge))
            order(v_.scalar_tensor_tensor(cond[:, 0, :], iotw[0:NG, :], gmm[:, 1:2], cond[:, 0, :], ALU.is_le, ALU.mult))
            v_.tensor_scalar(cond[:, 1, :], cond[:, 0, :], pcol[0:NG, 0:1], None, ALU.mult).then_inc(s_idx, 1)
            v_.tensor_scalar(cond[:, 2, :], cond[:, 0, :], pcol[0:NG, 1:2], None, ALU.mult).then_inc(s_idx, 1)
            def lows(ph, loops, per, hi_of, lo_of, bias_of=None, p=128, cols=None):
                with dve.Fori(0, loops) as i:
                    for j in range(per):
                        slot = (N[ph] + j) % 4
                        dve.wait_ge(s_hi, i * per + (HI[ph] + j + 1))
                        a = bank(slot, p, cols(j))
                        if bias_of:
                            ins = v_.scalar_tensor_tensor(lo_of(i, j), a, bias_of(i, j), hi_of(i, j), ALU.add, ALU.subtract)
                        else:
                            ins = v_.tensor_sub(lo_of(i, j), a, hi_of(i, j))
                        ins.then_inc(s_done, 1)

            for ph, mh, ml in (("Mq", Mqh, Mql), ("Mk", Mkh, Mkl)):
                lows(ph, 2, 4, lambda i, j: flat(mh[:, ds(i * 4 + j, 1), :]).bitcast(f32),
                     lambda i, j: flat(ml[:, ds(i * 4 + j, 1), :]), cols=lambda j: PF_)

            dve.wait_ge(s_idxT, 1)
            v_.tensor_copy(slo[:, :].rearrange("e (p g) -> e g p", g=GE),
                           bank(4, T, ET).rearrange("e (g p) -> e g p", g=GE)).then_inc(s_dve, 1); own.add()
            dve.wait_ge(s_idxT, 2)
            v_.tensor_copy(key[:, :].rearrange("e (p g) -> e g p", g=GE),
                           bank(5, T, ET).rearrange("e (g p) -> e g p", g=GE)).then_inc(s_dve, 1); own.add()
            dve.wait_ge(s_idxT, 3)
            v_.tensor_reduce(bnd[:, 0:1], bank(6, NW, NG), AX.X, ALU.max).then_inc(s_idx, 1)
            v_.tensor_reduce(bnd[:, 1:2], bank(6, NW, NG, NG), AX.X, ALU.max).then_inc(s_idx, 1)
            dve.wait_ge(s_idxT, 4)
            order(v_.tensor_scalar(brow[:, 0, :], bank(7, 1, NW), -1.0, float(NG), ALU.mult, ALU.add))
            order(v_.tensor_sub(brow[:, 1, :], bank(7, 1, NW, NW), brow[:, 0, :]))
            order(v_.tensor_scalar(brow[:, 2, :], brow[:, 0, :], float(NG - 1), None, ALU.min))
            order(v_.tensor_scalar(brow[:, 3, :], brow[:, 1, :], 1.0, None, ALU.max))
            order(v_.tensor_copy(bint[:, :, :], brow[:, 2:4, :]))
            v_.memset(degmax[:, :], 0.0).then_inc(s_bnd, 1)

            tot = dve.alloc_register("groups_dve")
            dve.reg_mov(tot, 0)
            at_tile = dve.alloc_register("first_tile_dve")
            with dve.Fori(0, NW) as w:
                lo = dve.value_load(bint[0:1, 0, ds(w, 1)], min_val=0, max_val=NG - 1)
                cnt = dve.value_load(bint[0:1, 1, ds(w, 1)], min_val=1, max_val=NG)
                before = dve.snap(tot, min_val=0, max_val=NW * NG)
                dve.reg_mov(at_tile, lo * GE)
                with dve.Fori(0, cnt) as k:
                    col = dve.snap(at_tile, min_val=0, max_val=ET - GE)
                    for m in range(GE):
                        dve.wait_ge(s_ohfree, (before + k) * GE + (m + 1))
                        v_.tensor_scalar(ohk[:, m, :], iot[0:T, :], tk[0:T, ds(w, 1)], key[:, ds(col + m, 1)],
                                         ALU.add, ALU.is_equal).then_inc(s_oh, 1)
                        v_.tensor_scalar(ohs[:, m, :], iot[0:T, 0:128], slo[:, ds(col + m, 1)], None, ALU.is_equal)\
                          .then_inc(s_oh, 1)
                    dve.reg_add(at_tile, at_tile, GE)
                dve.reg_add(tot, tot, cnt)

            dve.wait_ge(s_winev, 2 + NW)
            v_.tensor_reduce(degp[:, 0, :], adj_sb[:, :, 0:R].rearrange("p b d -> p d b"), AX.X, ALU.add)\
              .then_inc(s_degp, 1)
            for c, (c0, cn) in enumerate(CH):
                dve.wait_ge(s_deg, c + 1)
                order(v_.tensor_scalar(deginvB[:, c0:c0 + cn], bank((6, 7, 4)[c], 128, cn), 1.0, None, ALU.max))
            order(v_.reciprocal(deginvB[:, :], deginvB[:, :]))
            order(v_.tensor_reduce(degmax[:, 0:1], deginvB[0:1, :], AX.X, ALU.min))
            order(v_.tensor_scalar(degmax[:, 1:2], degmax[:, 0:1], 1.0 / FAST_MAX, None, ALU.is_lt))
            v_.tensor_copy(slow[:, :], degmax[:, 1:2]).then_inc(s_dinv, 1)

            def normalise(src_, dst_, done):
                for c in range(2):
                    v_.bn_stats(st6[:, c, :], src_[:, 512 * c:512 * c + 512]).then_inc(s_dve, 1)
                    last = own.add()
                dve.wait_ge(s_dve, last)
                order(v_.bn_aggr(mv[:, 0:2], st6[:, :, :].rearrange("p a b -> p (a b)")))
                order(v_.tensor_scalar(mv[:, 2:3], mv[:, 1:2], 1e-5, None, ALU.add))
                order(v_.tensor_scalar(mv[:, 3:4].bitcast(i32), mv[:, 2:3].bitcast(i32), 1, None,
                                       ALU.logical_shift_right))
                order(v_.tensor_copy(mv[:, 4:5], mv[:, 3:4].bitcast(i32)))
                order(v_.tensor_scalar(mv[:, 4:5], mv[:, 4:5], float(0x1FC00000), None, ALU.add))
                order(v_.tensor_copy(mv[:, 3:4].bitcast(i32), mv[:, 4:5]))
                for _ in range(4):
                    order(v_.reciprocal(mv[:, 4:5], mv[:, 3:4]))
                    order(v_.scalar_tensor_tensor(mv[:, 4:5], mv[:, 4:5], mv[:, 2:3], mv[:, 3:4], ALU.mult, ALU.add))
                    order(v_.tensor_scalar(mv[:, 3:4], mv[:, 4:5], 0.5, None, ALU.mult))
                order(v_.reciprocal(mv[:, 5:6], mv[:, 3:4]))
                v_.tensor_scalar(dst_, src_, mv[:, 0:1], mv[:, 5:6], ALU.subtract, ALU.mult).then_inc(done, 1)

            def transposed_lo(t, m, sums=None):
                for b in range(2):
                    dve.wait_ge(s_Thi, m(b))
                    a = bank(4 + b, 128, 4 * T).rearrange("p (k n) -> p k n", n=T)
                    if sums is not None:
                        v_.tensor_reduce(pooled[:, sums, 4 * b:4 * b + 4], a, AX.X, ALU.add).then_inc(s_dve, 1)
                        own.add()
                    v_.tensor_sub(XTl[:, 4 * b:4 * b + 4, t], a, XTh[:, 4 * b:4 * b + 4, t].bitcast(f32))\
                      .then_inc(s_Tlo, 1)

            def feature(m, a, p, n_, full, hi_, lo_):
                s = m % 2
                dve.wait_ge(*full)
                v_.tensor_scalar(elm[0:p, s, 0:n_], a, 0.0, None, ALU.min).then_inc(s_elm, 1)
                dve.wait_ge(s_ele, m + 1)
                ins = v_.scalar_tensor_tensor(elf[0:p, s, 0:n_], a, 0.0, elm[0:p, s, 0:n_], ALU.max, ALU.add)
                ins.then_inc(s_elf, 1)
                dve.wait_ge(s_elh, m + 1)
                v_.tensor_sub(lo_, elf[0:p, s, 0:n_], hi_.bitcast(f32)).then_inc(s_ell, 1)

            for t in range(NT + 1):
                if t < NT:
                    dve.wait_ge(s_x[t % 2], 16 * (t // 2 + 1))
                    if t >= 2:
                        dve.wait_ge(s_T, 2 * (t - 1))
                        dve.wait_ge(s_xl, t - 1)
                    normalise(xs[:, t % 2, :], xn[:, t % 2, :], s_xn)
                    if t == 0:
                        dve.wait_ge(s_adj, 16)
                    transposed_lo(slice(t * T, (t + 1) * T), lambda b: 2 * t + b + 1)
                if t >= 1:
                    m = t - 1
                    feature(m, bank(6 + m % 2, T, PF_), T, PF_, (s_kp, m + 1), kph[:, m % 2, :], kpl[:, m % 2, :])
            for j in range(4):
                dve.wait_ge(s_hi, HI["GT"] + j + 1)
                v_.tensor_sub(flat(GTl[:, 2 * j:2 * j + 2, :]), bank(j), flat(GTh[:, 2 * j:2 * j + 2, :]).bitcast(f32))\
                  .then_inc(s_done, 1)
            for j in range(PB * 3):
                c0, cn = CH[j % 3]
                feature(NT + j, bank((N["QP"] + j) % 4, 128, cn), 128, cn, (s_acc, N["QP"] + j + 1),
                        qph[:, j // 3, c0:c0 + cn], qpl[:, j // 3, c0:c0 + cn])
                dve.wait_ge(s_elf, NT + j + 1)
                dve.sem_inc(s_done, 1)
            for j in range(4):
                for b in range(4):
                    dve.wait_ge(s_wthi, 4 * j + b + 1)
                    v_.tensor_sub(flat(Wl[j % 2][:, 2 * b:2 * b + 2, :]), bank(4 + b),
                                  flat(Wh[j % 2][:, 2 * b:2 * b + 2, :]).bitcast(f32)).then_inc(s_wtlo, 1)
                for b in range(PB):
                    m = PB * j + b
                    dve.wait_ge(s_hi, HI["KV"] + m + 1)
                    v_.tensor_sub(kvl[:, b, j * WQ:(j + 1) * WQ], bank((N["KV"] + m) % 4, 128, WQ),
                                  kvh[:, b, j * WQ:(j + 1) * WQ].bitcast(f32)).then_inc(s_done, 1)
            dve.wait_ge(s_b1, 16)
            for t in range(NT):
                dve.wait_ge(s_xr[t % 2], 16 * (t // 2 + 1))
                order(v_.tensor_add(xr[:, t % 2, :], xr[:, t % 2, :], b1B[:, :]))
                dve.wait_ge(s_z, t + 1)
                order(v_.tensor_scalar(zcol[:, 0:1], bank(4 + t % 2, T, 1), 1e-8, None, ALU.add))
                order(v_.reciprocal(zcol[:, 1:2], zcol[:, 0:1]))
                for c in range(2):
                    m = N["NUM"] + 2 * t + c
                    dve.wait_ge(s_acc, m + 1)
                    if t:
                        dve.wait_ge(s_bt[c], 16 * t)
                    v_.scalar_tensor_tensor(bt2[:, c, :], bank(m % 4, T, 512), zcol[:, 1:2],
                                            xr[:, t % 2, 512 * c:512 * c + 512], ALU.mult, ALU.add).then_inc(s_done, 1)
            with dve.Fori(0, 2) as i:
                for j in range(12):
                    slot, cn = (N["S0"] + j) % 4, CH[j % 3][1]
                    dve.wait_ge(s_acc, i * 12 + (N["S0"] + j + 1))
                    dve.wait_ge(s_st[slot], i * 48 + (STORED["S0"] + 16 * (j // 4)))
                    v_.tensor_copy(ot1[0][:, slot, 0:cn], bank(slot, 128, cn)).then_inc(s_done, 1)
            lows("Y0", 2, 2 * NT, lambda i, j: ot1[0][0:T, (N["Y0"] + j) % 4, 0:WQ],
                 lambda i, j: ot1[1][0:T, (N["Y0"] + j) % 4, 0:WQ].bitcast(f32r), p=T, cols=lambda j: WQ)
            for m in range(3 * KB):
                c0, cn = CH[m % 3]
                z = zt[:, m % 2, 0:cn]
                dve.wait_ge(s_acc, N["HT"] + m + 1)
                order(v_.tensor_mul(z, bank((N["HT"] + m) % 4, 128, cn), deginvB[:, c0:c0 + cn]))
                dve.wait_ge(s_s0[m % 2], 16 * (m // 2 + 1))
                order(v_.tensor_add(z, z, s0c[:, m % 2, 0:cn]))
                v_.tensor_scalar(z, z, b0c[:, m // 3:m // 3 + 1], 0.0, ALU.add, ALU.max).then_inc(s_zt, 1)
                dve.wait_ge(s_hh, m + 1)
                v_.tensor_sub(XTl[:, m // 3, c0:c0 + cn], z, XTh[:, m // 3, c0:c0 + cn].bitcast(f32)).then_inc(s_done, 1)
            lows("Y1", 2, 2 * NT, lambda i, j: ot2[0][0:T, (N["Y1"] + j) % 4, 0:WQ],
                 lambda i, j: ot2[1][0:T, (N["Y1"] + j) % 4, 0:WQ].bitcast(f32r), p=T, cols=lambda j: WQ)
            with dve.Fori(0, 2) as i:
                for j in range(2 * NT):
                    slot = (N["S1"] + j) % 4
                    dve.wait_ge(s_acc, i * (2 * NT) + (N["S1"] + j + 1))
                    dve.wait_ge(s_bs[slot], i * 80 + 16 * (j // 4 + 1))
                    dve.wait_ge(s_st[slot], i * 80 + (STORED["S1"] + 16 * (j // 4)))
                    v_.tensor_add(ot2[0][0:T, slot, 0:WQ], bank(slot, T, WQ), bs[:, slot, :]).then_inc(s_done, 1)
            dve.wait_ge(s_row, 32)
            for t in range(NT + 1):
                if t < NT:
                    s = t % 2
                    dve.wait_ge(s_b2[s], 16 * (t // 2 + 1))
                    if t >= 2:
                        dve.wait_ge(s_x2[s], 16 * (t // 2))
                        dve.wait_ge(s_T, 2 * (NT + t - 1))
                    for c in range(2):
                        m = N["X2"] + 2 * t + c
                        dve.wait_ge(s_acc, m + 1)
                        v_.scalar_tensor_tensor(x2s[:, s, 512 * c:512 * c + 512], bank(m % 4, T, 512), deginv[:, t:t + 1],
                                                b2[:, s, 512 * c:512 * c + 512], ALU.mult, ALU.add).then_inc(s_done, 1)
                    dve.wait_ge(s_done, 4 + N["X2"] + 2 * t + 2)
                    normalise(x2s[:, s, :], x2n[:, s, :], s_x2n)
                if t >= 1:
                    transposed_lo(slice((t - 1) * T, t * T), lambda b: 2 * (NT + t - 1) + b + 1, sums=t - 1)
            dve.wait_ge(s_dve, own.n)
            order(v_.tensor_reduce(pool8[:, :], pooled[:, :, :].rearrange("p t k -> p k t"), AX.X, ALU.add))
            v_.tensor_scalar(pool8[:, :], pool8[:, :], 1.0 / R, None, ALU.mult).then_inc(s_pool, 1)
            order(v_.memset(gate[:, :], -3.0e38))
            dve.wait_ge(s_gw, 16 * 4)
            dve.wait_ge(s_gmm, 2)
            order(v_.tensor_add(gate[:, 0:NE], bank(7, 1, NE), bgr[:, 0:NE]))
            order(v_.max(gate[:, 8:16], gate[:, 0:8]))
            order(v_.max_index(gidx[:, :], gate[:, 8:16], gate[:, 0:8]))
            order(v_.tensor_copy(gidxf[:, :], gidx[:, :]))
            v_.tensor_sub(gate[:, 32:33], gate[:, 9:10], gate[:, 8:9]).then_inc(s_pool, 1)
            dve.wait_ge(s_ghid, 2)
            order(v_.tensor_scalar(gate[:, 34:35], gate[:, 33:34], 1.0, None, ALU.add))
            order(v_.reciprocal(gate[:, 40:41], gate[:, 34:35]))
            order(v_.tensor_mul(gate[:, 41:42], gate[:, 33:34], gate[:, 40:41]))
            for e in range(2):
                order(v_.tensor_scalar(gate[:, 44 + 4 * e:48 + 4 * e], iot4[:, :], gidxf[:, e:e + 1],
                                       gate[:, 40 + e:41 + e], ALU.is_equal, ALU.mult))
            v_.tensor_add(gate[:, 52:56], gate[:, 44:48], gate[:, 48:52]).then_inc(s_pool, 1)
            dve.wait_ge(s_gmm, 3)
            order(v_.tensor_copy(w4[:, :], bank(6, NE, 128)))
            v_.tensor_copy(wsel[:, :], bank(7, 128, 2)).then_inc(s_gate, 1)
            dve.wait_ge(s_gmm, 4)
            for c in range(2):
                order(v_.tensor_copy(bvB[:, 512 * c:512 * c + 512], bank(4 + c, T, 512)))
            v_.tensor_copy(qkb[:, :], bank(6, 128, 2 * KB)).then_inc(s_gate, 1)
            for a, ph in enumerate(("Q", "K")):
                lows(ph, 2, 12, lambda i, j: ot2[0][:, (N[ph] + j) % 4, 0:CH[j % 3][1]],
                     lambda i, j: ot2[1][:, (N[ph] + j) % 4, 0:CH[j % 3][1]].bitcast(f32r),
                     bias_of=lambda i, j: qkb[:, ds(i * 4 + (KB * a + j // 3), 1)], cols=lambda j: CH[j % 3][1])
            with dve.Fori(0, 2) as i:
                for j in range(2 * NT):
                    slot, u, t = (N["V"] + j) % 4, j // NT, j % NT
                    dve.wait_ge(s_acc, i * (2 * NT) + (N["V"] + j + 1))
                    v_.tensor_add(v[:, t, ds(i * 512 + u * WQ, WQ)], bank(slot, T, WQ), bvB[:, ds(i * 512 + u * WQ, WQ)])\
                      .then_inc(s_done, 1)

            def top(m, val):
                s = m % 2
                dve.wait_ge(s_s, val(1, 1))
                v_.tensor_reduce(att_m[:, s, 0:1], ps[0:T, 1536 * s:1536 * s + 1024], AX.X, ALU.max).then_inc(s_dve, 1)
                return own.add()

            def rest(m):
                s = m % 2
                order(v_.tensor_reduce(att_m[:, s, 1:2], ps[0:T, 1536 * s + 1024:1536 * s + R], AX.X, ALU.max))
                v_.tensor_scalar(att_m[:, s, 2:3], att_m[:, s, 0:1], att_m[:, s, 1:2], -SCALE, ALU.max, ALU.mult)\
                  .then_inc(s_mx, 1)

            def step(m, i, ahead):
                s = m % 2

                def val(k, c, m_=m):
                    return m_ * k + c + 7 * 2 * NT * k if i is None else i * (2 * NT * k) + (m_ * k + c)
                dve.wait_ge(s_pt, val(3, 2))
                v_.tensor_copy(PT[s][:, 4:8, :], bank(6 + (3 * m + 1) % 2, T, 4 * T).rearrange("p (b n) -> p b n", n=T))\
                  .then_inc(s_tb, 1)
                if ahead:
                    top(m, lambda k, c: val(k, c, m + 2))
                dve.wait_ge(s_pv, val(1, 1))
                order(v_.reciprocal(att_r[:, s, 1:2], att_r[:, s, 0:1]))
                hcol = (14 + m // NT) * HD if i is None else None
                dst_ = ao[:, m % NT, hcol:hcol + HD] if i is None else ao[:, m % NT, ds(i * 128 + (m // NT) * HD, HD)]
                v_.tensor_scalar(dst_, ps[0:T, 1536 * s + 1280:1536 * s + 1280 + HD], att_r[:, s, 1:2], None, ALU.mult)\
                  .then_inc(s_ev, 1)
                if ahead:
                    rest(m)

            for m in range(2):
                top(m, lambda k, c: m + 1)
                rest(m)
            with dve.Fori(0, H // 2 - 1) as i:
                own.enter(i, 3 * 2 * NT)
                for m in range(2 * NT):
                    step(m, i, True)
            own.leave(H // 2 - 1)
            for m in range(2 * NT):
                step(m, None, m + 2 < 2 * NT)
            for t in range(NT):
                transposed_lo(slice(t * T, (t + 1) * T), lambda b: 2 * (2 * NT + t) + b + 1)
            dve.wait_ge(s_bo, 16)
            with dve.Fori(0, 2) as i:
                own.enter(i, 2 * NT)
                for j in range(2 * NT):
                    slot, u, t = (N["O"] + j) % 4, j // NT, j % NT
                    dve.wait_ge(s_acc, i * (2 * NT) + (N["O"] + j + 1))
                    dve.wait_ge(s_x2r[slot], i * 80 + 16 * (j // 4 + 1))
                    dve.wait_ge(s_st[slot], i * 80 + (STORED["O"] + 16 * (j // 4)))
                    order(v_.tensor_add(ot[:, slot, :], bank(slot, T, WQ), x2r[:, slot, :]))
                    v_.tensor_add(ot[:, slot, :], ot[:, slot, :], boB[:, ds(i * 512 + u * WQ, WQ)]).then_inc(s_done, 1)
            own.leave(2)

        @block.tensor
        def _(pe):
            mm, tr = nc.tensor.matmul, nc.tensor.transpose
            pe.sem_inc(s_ohfree, GE)
            pe.wait_ge(s_const, 10)

            def three(dst_, ah, al, bh, bl, start, stop):
                mm(dst_, ah, bh, start=start, stop=False)
                mm(dst_, ah, bl, start=False, stop=False)
                return mm(dst_, al, bh, start=False, stop=stop)

            def wait_weights(i, ph, u):
                pe.wait_ge(s_wready, i * 4 + (2 * (WRDY[ph] + u + 1) + 2))

            def weights_stationary(ph, bh, bl, chunks):
                per = 4 * len(chunks)
                with pe.Fori(0, 2) as i:
                    for u in range(2):
                        wait_weights(i, ph, u)
                        for b in range(2):
                            for c, (c0, cn) in enumerate(chunks):
                                j = (2 * u + b) * len(chunks) + c
                                slot = (N[ph] + j) % 4
                                pe.wait_ge(s_done, i * per + (N[ph] + j + 1))
                                for k in range(KB):
                                    ins = three(bank(slot, 128, cn), Wh[u][:, k, b * 128:(b + 1) * 128],
                                                Wl[u][:, k, b * 128:(b + 1) * 128], bh[:, k, c0:c0 + cn],
                                                bl[:, k, c0:c0 + cn], k == 0, k == KB - 1)
                                ins.then_inc(s_acc, 1)

            def weights_moving(ph, ah, al, rows, count, wait):
                per = 2 * count
                with pe.Fori(0, 2) as i:
                    for u in range(2):
                        if wait:
                            wait_weights(i, ph, u)
                        for t in range(count):
                            j = u * count + t
                            slot = (N[ph] + j) % 4
                            pe.wait_ge(s_done, i * per + (N[ph] + j + 1))
                            for k in range(KB):
                                ins = three(bank(slot, rows, WQ), ah[:, k, t * rows:(t + 1) * rows],
                                            al[:, k, t * rows:(t + 1) * rows], Wh[u][:, k, :], Wl[u][:, k, :],
                                            k == 0, k == KB - 1)
                            ins.then_inc(s_acc, 1)

            pe.wait_ge(s_proj, 17)
            for ph in ("Mq", "Mk"):
                weights_stationary(ph, prh, prl, [(0, PF_)])

            for a in range(2):
                pe.wait_ge(s_idx, a + 1)
                for e in range(GE):
                    ins = tr(bank(4 + a, T, NG, e * NG), ef[:, 4 + a, e * T:(e + 1) * T], ident[0:NG, 0:NG])
                ins.then_inc(s_idxT, 1)
            pe.wait_ge(s_idx, 4)
            for a in range(2):
                ins = tr(bank(6, NW, NG, a * NG), cond[:, 1 + a, :], ident[0:NG, 0:NG])
            ins.then_inc(s_idxT, 1)
            pe.wait_ge(s_idx, 6)
            for a in range(2):
                ins = tr(bank(7, 1, NW, a * NW), bnd[:, a:a + 1], ident[0:NW, 0:NW])
            ins.then_inc(s_idxT, 1)
            pe.wait_ge(s_bnd, 1)
            tot = pe.alloc_register("groups_pe")
            pe.reg_mov(tot, 0)
            with pe.Fori(0, NW // 2) as i:
                for u in range(2):
                    w = pe.snap(i * 2 + u)
                    cnt = pe.value_load(bint[0:1, 1, ds(w, 1)], min_val=1, max_val=NG)
                    before = pe.snap(tot, min_val=0, max_val=NW * NG)
                    pe.wait_ge(s_winev, i * 2 + (u + 1))
                    acc = bank(4 + u, 128, KW)
                    mm(acc, zw[:, :], iot[0:T, :], start=True, stop=False)
                    with pe.Fori(0, cnt) as k:
                        for m in range(GE):
                            pe.wait_ge(s_oh, (before + k) * (2 * GE) + (2 * m + 2))
                            mm(acc, ohs[:, m, :], ohk[:, m, :], start=False, stop=False).then_inc(s_ohfree, 1)
                    mm(acc, zw[:, :], iot[0:T, :], start=False, stop=True).then_inc(s_win, 1)
                    pe.reg_add(tot, tot, cnt)
            pe.wait_ge(s_degp, 1)
            for c, (c0, cn) in enumerate(CH):
                mm(bank((6, 7, 4)[c], 128, cn), ones[0:T, :], degp[:, 0, c0:c0 + cn], start=True, stop=True)\
                    .then_inc(s_deg, 1)
            pe.wait_ge(s_dinv, 1)
            slow_ = pe.value_load(slow[0:1, 0:1], min_val=0, max_val=1)

            def transposes(src_, sem_):
                for b in range(2):
                    for k in range(4):
                        c0 = (4 * b + k) * 128
                        ins = tr(bank(4 + b, 128, T, k * T), src_[:, c0:c0 + 128], ident[0:T, 0:T])
                    ins.then_inc(sem_, 1)

            pe.wait_ge(s_done, 4 + N["GT"])
            for t in range(NT + 2):
                if t < NT:
                    pe.wait_ge(s_xn, t + 1)
                    if t:
                        pe.wait_ge(s_Tlo, 2 * t)
                    transposes(xn[:, t % 2, :], s_T)
                if 1 <= t <= NT:
                    m = t - 1
                    pe.wait_ge(s_Tlo, 2 * m + 2)
                    if m >= 2:
                        pe.wait_ge(s_elf, m - 1)
                    for k in range(KB):
                        ins = three(bank(6 + m % 2, T, PF_), XTh[:, k, m * T:t * T], XTl[:, k, m * T:t * T],
                                    Mkh[:, k, :], Mkl[:, k, :], k == 0, k == KB - 1)
                    ins.then_inc(s_kp, 1)
                if t >= 2:
                    m = t - 2
                    pe.wait_ge(s_ell, m + 1)
                    pe.wait_ge(s_xl, m + 1)
                    for k in range(KB):
                        dst_ = bank(k // 2, 128, PF_, PF_ * (k % 2))
                        ah, al = (a[m % 2][:, k * 128:(k + 1) * 128] for a in (xnh, xnl))
                        bh, bl = kph[:, m % 2, :], kpl[:, m % 2, :]
                        mm(dst_, ah, bh, start=m == 0 and k % 2 == 0, stop=False, skip_group_check=True)
                        mm(dst_, ah, bl, start=False, stop=False, skip_group_check=True)
                        ins = mm(dst_, al, bh, start=False, stop=m == NT - 1, skip_group_check=True)
                        if m == NT - 1 and k % 2:
                            ins.then_inc(s_acc, 1)
                            if k == KB - 1:
                                pe.wait_ge(s_acc, N["GT"] + 4)
                                pe.sem_inc(s_G, 1)
                    if m < NT - 1:
                        ins.then_inc(s_G, 1)
            for j in range(PB * 3):
                n_ = N["QP"] + j
                c0, cn = CH[j % 3]
                pb = j // 3
                pe.wait_ge(s_done, n_ + 1)
                for k in range(KB):
                    ins = three(bank(n_ % 4, 128, cn), Mqh[:, k, pb * 128:(pb + 1) * 128],
                                Mql[:, k, pb * 128:(pb + 1) * 128], XTh[:, k, c0:c0 + cn], XTl[:, k, c0:c0 + cn],
                                k == 0, k == KB - 1)
                ins.then_inc(s_acc, 1)
            wst_rows = Wst[:, :, :, :].rearrange("p a b c -> p (a b c)").rearrange("p (e n) -> p e n", e=2)
            pe.wait_ge(s_elf, NT)
            pe.wait_ge(s_Tlo, 2 * NT)
            for j in range(4):
                pe.wait_ge(s_wv, 16 * (j + 1))
                for b in range(4):
                    if j:
                        pe.wait_ge(s_wtlo, 4 * (j - 1) + b + 1)
                    for k in range(2):
                        for e in range(2):
                            c0 = (2 * b + k) * 128
                            ins = tr(bank(4 + b, 128, 128, k * WQ + e * 128), wst_rows[:, e, c0:c0 + 128], ident[:, :])
                    ins.then_inc(s_wt, 1)
                pe.wait_ge(s_wtlo, 4 * j + 4)
                for b in range(PB):
                    n_ = N["KV"] + PB * j + b
                    pe.wait_ge(s_done, n_ + 1)
                    for k in range(KB):
                        ins = three(bank(n_ % 4, 128, WQ), GTh[:, k, b * 128:(b + 1) * 128],
                                    GTl[:, k, b * 128:(b + 1) * 128], Wh[j % 2][:, k, :], Wl[j % 2][:, k, :],
                                    k == 0, k == KB - 1)
                    ins.then_inc(s_acc, 1)
            pe.wait_ge(s_ell, NT + PB * 3)
            pe.wait_ge(s_done, 4 + N["NUM"])
            for t in range(NT):
                rows = slice(t * T, (t + 1) * T)
                if t >= 2:
                    pe.wait_ge(s_done, 4 + N["NUM"] + 2 * (t - 2) + 1)
                for b in range(PB):
                    mm(bank(4 + t % 2, T, 2), qph[:, b, rows], onesr[:, :], start=b == 0, stop=False)
                    ins = mm(bank(4 + t % 2, T, 2), qpl[:, b, rows], onesr[:, :], start=False, stop=b == PB - 1)
                ins.then_inc(s_z, 1)
                for c in range(2):
                    n_ = N["NUM"] + 2 * t + c
                    pe.wait_ge(s_done, n_ + 1)
                    for b in range(PB):
                        ins = three(bank(n_ % 4, T, 512), qph[:, b, rows], qpl[:, b, rows],
                                    kvh[:, b, 512 * c:512 * c + 512], kvl[:, b, 512 * c:512 * c + 512],
                                    b == 0, b == PB - 1)
                    ins.then_inc(s_acc, 1)
            weights_stationary("S0", XTh, XTl, CH)
            weights_moving("Y0", XTh, XTl, T, NT, True)

            def counts_product(dst_, ys, a, exact_first):
                n_s = len(ys)
                for s_i in range(n_s):
                    yh, yl, ad = ys[s_i]
                    for part, y_ in enumerate((yh, yl)):
                        y_, ad_ = (y_, ad) if exact_first else (y_.bitcast(f32), ad.bitcast(f32))
                        l_, r_ = (y_, ad_) if a else (ad_, y_)
                        ins = mm(dst_, l_, r_, start=s_i == 0 and part == 0, stop=s_i == n_s - 1 and part == 1)
                return ins

            pe.wait_ge(s_adjr, 16)

            def aggregate_cols(fast):
                for blk in range(KB):
                    for c, (c0, cn) in enumerate(CH):
                        m = 3 * blk + c
                        if c == 0:
                            pe.wait_ge(s_y0[blk % 2], 32 * (blk // 2 + 1))
                        pe.wait_ge(s_done, N["HT"] + m + 1)
                        ins = counts_product(bank((N["HT"] + m) % 4, 128, cn),
                                             [(y0sh[blk % 2][:, s, :], y0sl[blk % 2][:, s, :], adjr[:, s, c0:c0 + cn])
                                              for s in range(NT)], True, fast)
                        ins.then_inc(s_acc, 1)

            with pe.If(slow_ == 0):
                aggregate_cols(True)
            with pe.Else():
                aggregate_cols(False)
            pe.wait_ge(s_done, 4 + N["Y1"])
            weights_moving("Y1", XTh, XTl, T, NT, True)
            weights_moving("S1", XTh, XTl, T, NT, True)
            pe.wait_ge(s_y1h, 16)
            pe.wait_ge(s_y1l, 16)

            def aggregate_rows(fast):
                for t in range(NT + 1):
                    if t < NT:
                        pe.wait_ge(s_at[t % 2], 16 * (t // 2 + 1))
                        for c in range(2):
                            n_ = N["X2"] + 2 * t + c
                            cols = slice(512 * c, 512 * c + 512)
                            pe.wait_ge(s_done, n_ + 1)
                            ins = counts_product(bank(n_ % 4, T, 512),
                                                 [(y1h[:, s, cols], y1l[:, s, cols], adt[t % 2][:, s, :])
                                                  for s in range(NT)], False, fast)
                            ins.then_inc(s_acc, 1)
                    if t:
                        pe.wait_ge(s_x2n, t)
                        if t > 1:
                            pe.wait_ge(s_Tlo, 2 * (NT + t - 1))
                        transposes(x2n[:, (t - 1) % 2, :], s_T)

            with pe.If(slow_ == 0):
                aggregate_rows(True)
            with pe.Else():
                aggregate_rows(False)
            pe.wait_ge(s_pool, 1)
            pe.wait_ge(s_gw, 64)
            for k in range(KB):
                ins = mm(bank(6, 128, 1), wg1[:, k, :], pool8[:, k:k + 1], start=k == 0, stop=k == KB - 1)
            ins.then_inc(s_gmm, 1)
            pe.wait_ge(s_ghid, 1)
            mm(bank(7, 1, NE), hid[:, :], wg2[:, :], start=True, stop=True).then_inc(s_gmm, 1)
            pe.wait_ge(s_pool, 3)
            mm(bank(6, NE, 128), gate[:, 52:56], ones[0:1, :], start=True, stop=True)
            mm(bank(7, 128, 2), ones[0:1, :], gate[:, 40:42], start=True, stop=True).then_inc(s_gmm, 1)
            pe.wait_ge(s_gate, 1)
            pe.wait_ge(s_eb, 16 * 3)
            pe.wait_ge(s_Tlo, 4 * NT)
            for c in range(2):
                mm(bank(4 + c, T, 512), w4[:, 0:T], b3[:, 2, 512 * c:512 * c + 512], start=True, stop=True)
            for a in range(2):
                for k in range(KB):
                    ins = mm(bank(6, 128, 1, a * KB + k), b3[:, a, k * 128:(k + 1) * 128], w4[:, 0:1], start=True, stop=True)
            ins.then_inc(s_gmm, 1)
            pe.wait_ge(s_gate, 2)
            weights_stationary("Q", XTh, XTl, CH)
            weights_stationary("K", XTh, XTl, CH)
            weights_moving("V", XTh, XTl, T, NT, True)

            def scores(m, u):
                s, t = m % 2, m % NT
                for c0, cn in SCH:
                    dst_ = ps[0:T, 1536 * s + c0:1536 * s + c0 + cn]
                    q_ = QS[u][:, t * T:(t + 1) * T]
                    mm(dst_, q_, KH[u][:, c0:c0 + cn], start=True, stop=False)
                    ins = mm(dst_, q_, KL[u][:, c0:c0 + cn], start=False, stop=True)
                ins.then_inc(s_s, 1)

            def step(m, i):
                s = m % 2

                def val(k, c):
                    return m * k + c + 7 * 2 * NT * k if i is None else i * (2 * NT * k) + (m * k + c)
                for c, b0_, nb in ((0, 0, 4), (1, 4, 4), (2, 8, 2)):
                    if c == 0:
                        pe.wait_ge(s_exp, val(1, 1))
                        pe.wait_ge(s_tb, val(1, 1))
                    else:
                        pe.wait_ge(s_ta, val(2, c))
                    for b in range(nb):
                        ins = tr(bank(6 + (3 * m + c) % 2, T, T, b * T), Pt[s][:, (b0_ + b) * T:(b0_ + b + 1) * T],
                                 ident[0:T, 0:T])
                    ins.then_inc(s_pt, 1)
                if i is not None or m + 2 < 2 * NT:
                    if m + 2 == NT:
                        pe.wait_ge(s_qk[1], i * 96 + 96 if i is not None else 96 * (H // 2))
                    if m + 2 == 2 * NT:
                        pe.wait_ge(s_qk[0], i * 96 + 192)
                    scores(m + 2, (m + 2) // NT % 2)
                pe.wait_ge(s_ta, val(2, 3))
                pe.wait_ge(s_tb, val(1, 2))
                hc = (14 + m // NT) * HD
                for b in range(NT):
                    v_in = v[:, b, hc:hc + HD] if i is None else v[:, b, ds(i * 128 + (m // NT) * HD, HD)]
                    ins = mm(ps[0:T, 1536 * s + 1280:1536 * s + 1280 + HD], PT[s][:, b, :], v_in,
                             start=b == 0, stop=b == NT - 1)
                ins.then_inc(s_pv, 1)

            pe.wait_ge(s_done, 4 + N["O"])
            pe.wait_ge(s_qk[0], 96)
            scores(0, 0)
            scores(1, 0)
            with pe.Fori(0, H // 2 - 1) as i:
                for m in range(2 * NT):
                    step(m, i)
            for m in range(2 * NT):
                step(m, None)
            for t in range(NT):
                if t == 0:
                    pe.wait_ge(s_ev, H * NT)
                else:
                    pe.wait_ge(s_Tlo, 2 * (2 * NT + t))
                transposes(ao[:, t, :], s_T)
            pe.wait_ge(s_Tlo, 6 * NT)
            weights_moving("O", XTh, XTl, T, NT, True)


_INS = ['x', 'src', 'dst', 'L0_gnn_W_self0', 'L0_gnn_W_neigh0', 'L0_gnn_b0', 'L0_gnn_W_self1', 'L0_gnn_W_neigh1',
        'L0_gnn_b1', 'L0_mix_Wq', 'L0_mix_Wk', 'L0_mix_Wv', 'L0_mix_proj', 'L0_ffn_Wq', 'L0_ffn_bq', 'L0_ffn_Wk',
        'L0_ffn_bk', 'L0_ffn_Wv', 'L0_ffn_bv', 'L0_ffn_Wg1', 'L0_ffn_bg1', 'L0_ffn_Wg2', 'L0_ffn_bg2', 'L0_ffn_Wo',
        'L0_ffn_bo']
_OUTS = [((1250, 1024), 'float32')]
_SCRATCH = [("adj", (1250, 1280)), ("base", (1250, 1024)), ("y0hi", (1250, 1024)), ("y0lo", (1250, 1024)),
            ("s0T", (1024, 1250)), ("y1hi", (1250, 1024)), ("y1lo", (1250, 1024)), ("x2d", (1250, 1024)),
            ("qhi", (1024, 1250)), ("qlo", (1024, 1250)), ("khi", (1024, 1250)), ("klo", (1024, 1250)),
            ("degrow", (1250,))]


def kernel(**inputs):
    import numpy as _np
    import concourse.bacc as _bacc
    from concourse import mybir as _mybir
    from concourse.bass_utils import run_bass_kernel_spmd as _run

    nc = _bacc.Bacc("TRN2", target_bir_lowering=False, num_devices=1)
    arrays, args = {}, []
    for name in _INS:
        a = _np.ascontiguousarray(inputs[name])
        arrays[f"in_{name}_dram"] = a
        args.append(nc.dram_tensor(f"in_{name}_dram", a.shape, _mybir.dt.from_np(a.dtype), kind="ExternalInput").ap())
    for i, (shape, dtype) in enumerate(_OUTS):
        dt = _mybir.dt.from_np(_np.dtype(dtype))
        args.append(nc.dram_tensor(f"out_{i}_dram", shape, dt, kind="ExternalOutput").ap())
    for name, shape in _SCRATCH:
        args.append(nc.dram_tensor(f"scratch_{name}", shape, _mybir.dt.float32, kind="Internal").ap())
    gps_layer_kernel(nc, *args)
    r = _run(nc, [arrays], core_ids=[0])
    got = tuple(r.results[0][f"out_{i}_dram"] for i in range(len(_OUTS)))
    return got[0]
```

```python
import concourse.bass as bass
from concourse import mybir
from contextlib import ExitStack


class Count:

    def __init__(self):
        self.n, self.turn, self.per = 0, None, 0

    def add(self):
        self.n += 1
        return self.n if self.turn is None else self.turn * self.per + self.n

    def enter(self, turn, per):
        self.turn, self.per, self.start = turn, per, self.n

    def leave(self, turns):
        assert self.n - self.start == self.per, (self.n - self.start, self.per)
        self.turn, self.n = None, self.start + self.per * turns


def gps_layer_kernel(nc, x, src, dst, W_self0, W_neigh0, b0, W_self1, W_neigh1, b1,
                     mWq, mWk, mWv, proj, fWq, fbq, fWk, fbk, fWv, fbv, Wg1, bg1, Wg2, bg2,
                     Wo, bo, out, adj, base, y0hi, y0lo, s0T, x2d, qhi, qlo, khi, klo, vhi, vlo,
                     degrow):
    f32, f32r = mybir.dt.float32, mybir.dt.float32r
    bf16, f16, i32 = mybir.dt.bfloat16, mybir.dt.float16, mybir.dt.int32
    u32 = mybir.dt.uint32
    ALU, ACT, AX = mybir.AluOpType, mybir.ActivationFunctionType, mybir.AxisListType
    ds = bass.ds

    R, D = x.shape
    T = 125
    NT = R // T
    KB = D // 128
    E = src.shape[0]
    ET = E // T
    GE = 4
    NG = ET // GE
    RING = 4 * GE
    PF_ = proj.shape[1]
    PB = PF_ // 128
    DW = 32
    NW = -(-R // DW)
    AW = NW * DW
    KW = NT * DW
    NE = fWq.shape[0]
    H, HD = 16, 64
    WQ = 256
    NQ = D // WQ
    CH = [(0, 418), (418, 416), (834, 416)]
    CM = CH[0][1]
    HB = 4
    UN = 3 * NT
    LAG = 3
    SCORES_AT = [3 * t for t in range(NT)]
    ROWS_AT = [min(q + 3, UN - 1) for q in SCORES_AT]
    OUT_AT = [(4, 5, 7, 8, 10, 11), (4, 6, 7, 9, 10, 12), (5, 6, 8, 9, 10, 12)]
    OUT_STEPS = [(NT * (k + 1) - 1 + d, k, part) for k in range(3 * HB) for part, d in enumerate(OUT_AT[k % 3])]

    def output_steps(n, first, last):
        steps = [(k, part) for at_, k, part in OUT_STEPS if at_ == n or (last and n == HB * UN and at_ > n)]
        return steps + [(k - 3 * HB, part) for at_, k, part in OUT_STEPS if at_ - HB * UN == n and not first
                        and n < HB * UN]

    MG = [(0, 4), (4, 8), (8, NT)]
    SCH = [(0, 512), (512, 512), (1024, R - 1024)]
    SCALE = 0.125
    FAST_MAX = 4096.0
    assert R == NT * T and E == ET * T and ET == NG * GE and NW % 2 == 0

    ctx = ExitStack()
    with ctx:
        def sb(name, shape, dt=f32):
            return ctx.enter_context(nc.sbuf_tensor(name, shape, dt))

        def sem(name):
            return ctx.enter_context(nc.semaphore(name))

        ident = sb("ident", [128, 128])
        ones = sb("ones", [128, 128])
        onesr = sb("onesr", [128, 2], f32r)
        b0c = sb("b0c", [128, KB])
        deginv = sb("deginv", [T, NT])
        degmax = sb("degmax", [1, 2])
        slow = sb("slow", [1, 1], i32)
        st6 = sb("st6", [T, 2, 6])
        mv = sb("mv", [T, 8])
        stat = sb("stat", [T, NT, 2])
        zcol = sb("zcol", [T, 2])
        qkvb = sb("qkvb", [128, 3 * KB])
        pooled = sb("pooled", [128, NT, KB])
        pool8 = sb("pool8", [128, KB])
        gate = sb("gate", [1, 64])
        gidx = sb("gidx", [1, 8], u32)
        gidxf = sb("gidxf", [1, 8])
        hid = sb("hid", [128, 1])
        wsel = sb("wsel", [128, 2])
        w4 = sb("w4", [NE, 128])
        iot4 = sb("iot4", [1, NE])
        att_m = sb("att_m", [T, 2])

        ARENA = 208160
        base_at = nc.sbuf_base
        base_at += -base_at % 32
        arena = sb("arena", [128, ARENA // 4])

        def at(name, shape, dt, offset):
            return nc.alloc_sbuf_tensor_at(name, shape, dt, offset=base_at + offset)

        XTh = at("XTh", [128, KB, R], f32r, 0)
        XTl = at("XTl", [128, KB, R], f32r, 40000)
        o = 80000
        Wst = at("Wst", [128, 2, KB // 2, WQ], f32, o)
        o += 8192
        Wh = [at(f"Wh{i}", [128, KB, WQ], f32r, o + 8192 * i) for i in range(2)]
        Wl = [at(f"Wl{i}", [128, KB, WQ], f32r, o + 16384 + 8192 * i) for i in range(2)]
        o += 32768
        G0 = o
        raw = at("raw", [NG, 2, GE * T], i32, 0)
        ef = at("ef", [NG, 6, GE * T], f32, 4000)
        dhi_i = at("dhi_i", [NG, GE * T], i32, 16000)
        iotw = at("iotw", [128, NW], f32, 18016)
        pcol = at("pcol", [128, 2], f32, 18176)
        gmm = at("gmm", [NG, 2], f32, 18208)
        cond = at("cond", [NG, 3, NW], f32, 18240)
        bnd = at("bnd", [NW, 2], f32, 18720)
        brow = at("brow", [1, 4, NW], f32, 18752)
        K0 = G0 + 77088
        slo = at("slo", [T, ET], f32, K0)
        key = at("key", [T, ET], f32, K0 + 1280)
        iot = at("iot", [128, KW], f16, K0 + 2560)
        tk = at("tk", [128, NW], f32, K0 + 3200)
        zw = at("zw", [T, 128], bf16, K0 + 3360)
        bint = at("bint", [1, 2, NW], i32, K0 + 3616)
        adjr = at("adjr", [T, NT, AW], f32r, G0)
        ohs = at("ohs", [T, RING, 128], bf16, G0 + 61984)
        ohk = at("ohk", [T, RING, KW], bf16, G0 + 61984 + 256 * RING)
        degp = at("degp", [T, R], f32, 203136)
        Mqh = at("Mqh", [128, KB, PF_], f32r, G0)
        Mql = at("Mql", [128, KB, PF_], f32r, G0 + 8192)
        Mkh = at("Mkh", [128, KB, PF_], f32r, G0 + 16384)
        Mkl = at("Mkl", [128, KB, PF_], f32r, G0 + 24576)
        L = G0 + 32768
        prh = at("prh", [128, KB, PF_], f32r, L)
        prl = at("prl", [128, KB, PF_], f32r, L + 8192)
        prf = at("prf", [128, KB, PF_], f32, L + 16384)
        xs = at("xs", [T, 2, D], f32, L + 24576)
        xn = at("xn", [T, 2, D], f32, L + 32768)
        xnh = [at(f"xnh{i}", [T, D], f32r, L + 4096 * i) for i in range(2)]
        xnl = [at(f"xnl{i}", [T, D], f32r, L + 8192 + 4096 * i) for i in range(2)]
        kph = at("kph", [T, 2, PF_], f32r, L + 16384)
        kpl = at("kpl", [T, 2, PF_], f32r, L + 18432)
        qph = at("qph", [128, PB, R], f32r, L)
        qpl = at("qpl", [128, PB, R], f32r, L + 10016)
        elm = at("elm", [128, 2, CM], f32, L + 20480)
        elf = at("elf", [128, 2, CM], f32, L + 40960)
        GTh = at("GTh", [128, KB, PF_], f32r, L + 24576)
        GTl = at("GTl", [128, KB, PF_], f32r, L + 32768)
        kvh = at("kvh", [128, PB, D], f32r, G0 + 16384)
        kvl = at("kvl", [128, PB, D], f32r, G0 + 24576)
        xr = at("xr", [T, 2, D], f32, G0)
        bt2 = at("bt2", [T, 2, 512], f32, G0 + 8192)
        b1B = at("b1B", [T, D], f32, G0 + 12288)
        y0t = [at(f"y0t{c}", [T, 4, WQ], f32, G0 + 51200 + 4096 * c) for c in range(2)]
        s0t = at("s0t", [128, 4, CM], f32, G0 + 51200)
        ot2 = [at(f"ot2{c}", [128, 4, CM], f32, G0 + 16384 + 6720 * c) for c in range(2)]
        y0sh = [at(f"y0sh{i}", [T, NT, 128], f32r, G0 + 51200 + 10240 * i) for i in range(2)]
        y0sl = [at(f"y0sl{i}", [T, NT, 128], f32r, G0 + 56320 + 10240 * i) for i in range(2)]
        s0c = at("s0c", [128, 2, CM], f32, G0 + 71744)
        zt = at("zt", [128, 2, CM], f32, G0 + 75104)
        deginvB = at("deginvB", [128, R], f32, 203136)
        y1l = at("y1l", [T, NT, D], f32r, G0)
        bs = at("bs", [T, 4, WQ], f32, 203136)
        adt = [at(f"adt{i}", [T, NT, 128], f32r, 80000 + 5120 * i) for i in range(2)]
        b2 = at("b2", [T, 2, D], f32, 80000 + 10240)
        x2s = at("x2s", [T, 2, D], f32, 80000 + 18432)
        x2n = at("x2n", [T, 2, D], f32, 80000 + 26624)
        V0 = G0 + 40960
        y1h = at("y1h", [T, NT, D], f32r, V0)
        wg1 = at("wg1", [128, KB, 128], f32, 80000 + 34816)
        wg2 = at("wg2", [128, NE], f32, 80000 + 38912)
        bgr = at("bgr", [1, 8], f32, 80000 + 38944)
        bg1c = at("bg1c", [128, 1], f32, 80000 + 38976)
        wst2 = at("wst2", [128, 2, 2, KB // 2, WQ], f32, G0)
        b3 = at("b3", [NE, 3, D], f32, V0)
        place = [[G0 + 5024 * b for b in (6, 7, 0, 1)]] + [[80000 + 5024 * (4 * k + b) for b in range(4)] for k in range(2)]
        place += [[G0 + 5024 * b for b in (2, 3, 4, 5)]]
        KH = [at(f"KH{i}", [128, R], f32r, place[i][0]) for i in range(HB)]
        QS = [at(f"QS{i}", [128, R], f32r, place[i][1]) for i in range(HB)]
        KM = [at(f"KM{i}", [HD + 2, R], f32r, place[i][2]) for i in range(HB)]
        QM = [at(f"QM{i}", [HD + 2, R], f32r, place[i][3]) for i in range(HB)]
        VS = [at(f"VS{i}", [T, NT, 2 * HD], f32r, V0 + 5120 * i) for i in range(2)]
        VL = [at(f"VL{i}", [T, NT, HD], f32r, V0 + 10240 + 2560 * i) for i in range(2)]
        EX = [at(f"EX{i}", [T, CM], f32, V0 + 15360 + 1696 * i) for i in range(3)]
        EH = [at(f"EH{i}", [T, CM], f32r, V0 + 20448 + 1696 * i) for i in range(4)]
        EL = [at(f"EL{i}", [T, CM], f32r, V0 + 27232 + 1696 * i) for i in range(4)]
        RB = at("RB", [HD, CM], f32, V0 + 34016)
        OB = [at(f"OB{i}", [128, CM], f32, V0 + 35712 + 1696 * i) for i in range(2)]
        MB = at("MB", [T, 2, HD + 2], f32r, V0 + 39104)
        x2r = at("x2r", [T, 4, WQ], f32, V0)
        ot = at("ot", [T, 4, WQ], f32, V0 + 4096)
        boB = at("boB", [T, D], f32, V0 + 8192)

        ps = ctx.enter_context(nc.psum_tensor("ps", [128, 8 * 512], f32))

        def bank(i, p=128, n=512, c=0):
            return ps[0:p, 512 * i + c:512 * i + c + n]

        names = ["Mq", "Mk", "GT", "QP", "KV", "NUM", "Y0", "S0", "HT", "Y1", "S1", "X2", "Q", "K", "V", "O"]
        tiles = [KB, KB, 4, PB * 3, 4 * PB, 2 * NT, 4 * NT, 3 * KB, 3 * KB, 4 * NT, 4 * NT, 2 * NT, 3 * KB, 3 * KB,
                 4 * NT, 4 * NT]
        split = {"Mq", "Mk", "GT", "KV", "Y0", "Y1", "Q", "K", "V"}
        N, HI, STORED = {}, {}, {}
        n = h = 0
        st = 16
        for name, m in zip(names, tiles):
            N[name], HI[name], STORED[name] = n, h, st
            n += m
            h += m if name in split else 0
            if name in ("S0", "S1", "O"):
                st += 16 * (m // 4)
            if name in ("Y0", "Q", "K", "V"):
                st += 32 * (m // 4)
        END, ST_END = n, st
        ORDER = ["Mq", "Mk", "KV", "Y0", "S0", "Y1", "S1", "Q", "K", "V", "O"]
        SIZE = dict(zip(names, tiles))

        def slot_free(ph, u, i):
            k = ORDER.index(ph)
            before = 0 if k == 0 else N[ORDER[k - 1]] + SIZE[ORDER[k - 1]] * (3 + u) // 4
            same = N[ph] + SIZE[ph] * (1 + u) // 4
            if isinstance(i, int):
                return (before, same)[i]
            return i * (same - before) + before
        WIN_Y0 = list(range(2, 2 * NT, 3))
        NS0 = NW // 2 - len(WIN_Y0)
        WIN_S0 = [list(range(j * NS0 // 12, (j + 1) * NS0 // 12)) for j in range(12)]
        assert len(WIN_Y0) % 2 == 0 and NS0 % 2 == 0
        WRDY = {k: 4 * i for i, k in enumerate(["Mq", "Mk", "Y0", "S0", "Y1", "S1", "Q", "K", "V", "O"])}

        s_const = sem("s_const")
        s_edges = sem("s_edges")
        s_small = sem("s_small")
        s_passed = sem("s_passed")
        s_gw = sem("s_gw")
        s_eb = sem("s_eb")
        s_w = [sem(f"s_w{k}") for k in range(2)]
        s_we = [sem(f"s_we{k}") for k in range(2)]
        s_wv = sem("s_wv")
        s_gp = sem("s_gp")
        s_whi = sem("s_whi")
        s_comb = sem("s_comb")
        s_wready = sem("s_wready")
        s_acc = sem("s_acc")
        s_hi = sem("s_hi")
        s_done = sem("s_done")
        s_st = [sem(f"s_st{k}") for k in range(4)]
        s_dve = sem("s_dve")
        s_act = sem("s_act")
        s_proj = sem("s_proj")
        s_idx = sem("s_idx")
        s_idxT = sem("s_idxT")
        s_bnd = sem("s_bnd")
        s_oh = sem("s_oh")
        s_ohfree = sem("s_ohfree")
        s_win = sem("s_win")
        s_winev = sem("s_winev")
        s_degp = sem("s_degp")
        s_deg = sem("s_deg")
        s_slow = sem("s_slow")
        s_dinv = sem("s_dinv")
        s_adj = sem("s_adj")
        s_row = sem("s_row")
        s_x = [sem(f"s_x{k}") for k in range(2)]
        s_xn = sem("s_xn")
        s_xg = sem("s_xg")
        s_xh = sem("s_xh")
        s_xl = sem("s_xl")
        s_T = sem("s_T")
        s_Thi = sem("s_Thi")
        s_Tlo = sem("s_Tlo")
        s_kp = sem("s_kp")
        s_G = sem("s_G")
        s_elm = sem("s_elm")
        s_ele = sem("s_ele")
        s_elf = sem("s_elf")
        s_elh = sem("s_elh")
        s_ell = sem("s_ell")
        s_wt = sem("s_wt")
        s_wthi = sem("s_wthi")
        s_wtlo = sem("s_wtlo")
        s_z = sem("s_z")
        s_xr = [sem(f"s_xr{k}") for k in range(2)]
        s_bt = [sem(f"s_bt{k}") for k in range(2)]
        s_b1 = sem("s_b1")
        s_y0 = [sem(f"s_y0{k}") for k in range(2)]
        s_s0 = [sem(f"s_s0{k}") for k in range(2)]
        s_zt = sem("s_zt")
        s_hh = sem("s_hh")
        s_bs = [sem(f"s_bs{k}") for k in range(4)]
        s_at = [sem(f"s_at{k}") for k in range(2)]
        s_b2 = [sem(f"s_b2{k}") for k in range(2)]
        s_x2 = [sem(f"s_x2{k}") for k in range(2)]
        s_x2n = sem("s_x2n")
        s_pool = sem("s_pool")
        s_gmm = sem("s_gmm")
        s_ghid = sem("s_ghid")
        s_gate = sem("s_gate")
        s_qk = [sem(f"s_qk{k}") for k in range(HB)]
        s_qk_first = sem("s_qk_first")
        s_v = [sem(f"s_v{k}") for k in range(2)]
        s_fill = sem("s_fill")
        s_s = sem("s_s")
        s_mx = sem("s_mx")
        s_mb = sem("s_mb")
        s_mt = sem("s_mt")
        s_mr = sem("s_mr")
        s_sc = sem("s_sc")
        s_eh = sem("s_eh")
        s_ex = sem("s_ex")
        s_el = [sem("s_el0"), sem("s_el1"), sem("s_el2")]
        s_pv = sem("s_pv")
        s_ob = sem("s_ob")
        s_ao = sem("s_ao")
        s_aol = sem("s_aol")
        s_x2r = [sem(f"s_x2r{k}") for k in range(4)]
        s_bo = sem("s_bo")

        block = ctx.enter_context(nc.Block())

        xt = x.rearrange("(t p) c -> t p c", p=T)

        def wait_apart(eng, sem_, value):
            eng.wait_ge(sem_, value)
            if not isinstance(value, int):
                eng.sem_inc(s_passed, 1)

        def load_qk(eng, h):
            k, rows = h % HB, slice(h * HD, (h + 1) * HD)
            for d_, a_ in ((KH[k][0:HD], khi), (KH[k][HD:128], khi), (QS[k][0:HD], qhi), (QS[k][HD:128], qlo),
                           (KM[k][0:HD], klo), (QM[k][0:HD], qhi)):
                eng.dma_start(d_.bitcast(f32), a_[rows, :]).then_inc(s_qk[k] if h else s_qk_first, 16)

        @block.sync
        def _(sp):
            for k in range(4):
                sp.sem_inc(s_st[k], 16)
            sp.dma_start(raw[:, 0, :], src.rearrange("(p e) -> p e", p=NG)).then_inc(s_edges, 16)
            sp.dma_start(raw[:, 1, :], dst.rearrange("(p e) -> p e", p=NG)).then_inc(s_edges, 16)
            sp.dma_start(prf[:, :, :], proj.rearrange("(k p) n -> p k n", p=128)).then_inc(s_proj, 16)
            with nc.allow_non_contiguous_dma(reason="one small column layout"):
                sp.dma_start(b0c[:, :], b0.rearrange("(k p) -> p k", p=128)).then_inc(s_small, 16)
            for t in range(2 * NT):
                if t >= 2:
                    sp.wait_ge(s_xn if t < NT + 2 else s_xg, t - 1 if t < NT + 2 else t - 1 - NT)
                sp.dma_start(xs[:, t % 2, :], xt[t % NT, :, :]).then_inc(s_x[t % 2], 16)
            sp.wait_ge(s_acc, N["KV"])
            sp.dma_start(b1B[:, :], b1.partition_broadcast(T)).then_inc(s_b1, 16)
            for t in range(NT + 1):
                if t < NT:
                    if t >= 2:
                        sp.wait_ge(s_done, 4 + N["NUM"] + 2 * (t - 1))
                    sp.dma_start(xr[:, t % 2, :], xt[t, :, :]).then_inc(s_xr[t % 2], 16)
                if t >= 1:
                    for c in range(2):
                        sp.wait_ge(s_done, 4 + N["NUM"] + 2 * (t - 1) + c + 1)
                        sp.dma_start(base[(t - 1) * T:t * T, 512 * c:512 * c + 512], bt2[:, c, :])\
                          .then_inc(s_bt[c], 16)
            def store_cols(ph, outs, tb, per_quarter_blocks=2):
                with sp.Fori(0, 2) as i:
                    for j in range(12):
                        u, b, c = j // 6, j // 3 % 2, j % 3
                        c0, cn = CH[c]
                        slot = (N[ph] + j) % 4
                        sp.wait_ge(s_done, i * 12 + (4 + N[ph] + j + 1))
                        for o_, t_ in zip(outs, tb):
                            dst_ = o_[ds(i * 512 + (2 * u + b) * 128, 128), c0:c0 + cn]
                            sp.dma_start(dst_, t_[:, slot, 0:cn]).then_inc(s_st[slot], 16)

            def store_rows(ph, outs, tb):
                with sp.Fori(0, 2) as i:
                    for j in range(2 * NT):
                        u, t = j // NT, j % NT
                        slot = (N[ph] + j) % 4
                        sp.wait_ge(s_done, i * (2 * NT) + (4 + N[ph] + j + 1))
                        for o_, t_ in zip(outs, tb):
                            sp.dma_start(o_[t * T:(t + 1) * T, ds(i * 512 + u * WQ, WQ)], t_[0:T, slot, 0:WQ])\
                              .then_inc(s_st[slot], 16)

            def stored(ph_next):
                for k in range(4):
                    sp.wait_ge(s_st[k], STORED[ph_next])

            store_rows("Y0", [y0hi, y0lo], y0t)
            store_cols("S0", [s0T], [s0t])
            stored("HT")
            y0v = [a.rearrange("(s p) c -> p s c", p=T) for a in (y0hi, y0lo)]
            for blk in range(KB):
                if blk >= 2:
                    sp.wait_ge(s_acc, N["HT"] + 3 * (blk - 1))
                for a_, d_ in zip(y0v, (y0sh, y0sl)):
                    sp.dma_start(d_[blk % 2][:, :, :].bitcast(f32), a_[:, :, blk * 128:(blk + 1) * 128])\
                      .then_inc(s_y0[blk % 2], 16)
                for c, (c0, cn) in enumerate(CH):
                    m = 3 * blk + c
                    if m >= 2:
                        sp.wait_ge(s_zt, m - 1)
                    elif m == 0:
                        sp.wait_ge(s_deg, len(CH))
                    sp.dma_start(s0c[:, m % 2, 0:cn], s0T[blk * 128:(blk + 1) * 128, c0:c0 + cn])\
                      .then_inc(s_s0[m % 2], 16)
                    if c != 1 and 2 <= blk < 2 + NT // 2:
                        b = 2 * (blk - 2) + c // 2
                        sp.dma_start(adj.rearrange("(b p) d -> p b d", p=T)[:, b:b + 1, :],
                                     adjr[:, b:b + 1, :].bitcast(f32)).then_inc(s_adj, 16)
                    if m == 5:
                        sp.wait_ge(s_dinv, 3)
                        sp.dma_start(degrow.rearrange("(a n) -> a n", a=1), deginvB[0:1, :]).then_inc(s_row, 16)
                        sp.wait_ge(s_row, 16)
                        with nc.allow_non_contiguous_dma(reason="one small column layout"):
                            sp.dma_start(deginv[:, :], degrow.rearrange("(t p) -> p t", p=T)).then_inc(s_row, 16)
            store_rows("S1", [base], [bs])
            stored("X2")
            sp.wait_ge(s_acc, N["X2"])
            sp.wait_ge(s_adj, 16 * NT)
            adv = adj.rearrange("(b p) d -> p b d", p=T)
            for t in range(NT + 1):
                if t < NT:
                    if t >= 2:
                        sp.wait_ge(s_acc, N["X2"] + 2 * (t - 1))
                    sp.dma_start(adt[t % 2][:, :, :].bitcast(f32), adv[:, :, t * T:t * T + 128])\
                      .then_inc(s_at[t % 2], 16)
                    if t >= 2:
                        sp.wait_ge(s_done, 4 + N["X2"] + 2 * (t - 1))
                    sp.dma_start(b2[:, t % 2, :], base[t * T:(t + 1) * T, :]).then_inc(s_b2[t % 2], 16)
                if t >= 1:
                    sp.wait_ge(s_done, 4 + N["X2"] + 2 * t)
                    sp.dma_start(x2d[(t - 1) * T:t * T, :], x2s[:, (t - 1) % 2, :]).then_inc(s_x2[(t - 1) % 2], 16)
                if t == 0:
                    sp.dma_start(wg1[:, :, :], Wg1.rearrange("(k p) n -> p k n", p=128)).then_inc(s_gw, 16)
                    sp.dma_start(wg2[:, :], Wg2).then_inc(s_gw, 16)
                    sp.dma_start(bgr[:, 0:NE], bg2.rearrange("(a n) -> a n", a=1)).then_inc(s_gw, 16)
                    with nc.allow_non_contiguous_dma(reason="one small column layout"):
                        sp.dma_start(bg1c[:, :], bg1.rearrange("(p a) -> p a", a=1)).then_inc(s_gw, 16)
            sp.wait_ge(s_acc, N["Q"])
            for k_, b_ in enumerate((fbq, fbk, fbv)):
                sp.dma_start(b3[:, k_, :], b_).then_inc(s_eb, 16)
            store_cols("Q", [qhi, qlo], ot2)
            store_cols("K", [khi, klo], ot2)
            store_rows("V", [vhi, vlo], ot2)
            stored("V")

            def load_v(h):
                k, cols = h % 2, slice(h * HD, (h + 1) * HD)
                for d_, a_ in ((VS[k][:, :, 0:HD], vhi), (VL[k][:, :, :], vlo)):
                    sp.dma_start(d_.bitcast(f32), a_.rearrange("(s p) c -> p s c", p=T)[:, :, cols])\
                      .then_inc(s_v[k], 16)

            sp.wait_ge(s_acc, N["O"])
            load_qk(sp, 1)
            load_qk(sp, 2)
            stored("O")
            load_v(0)
            load_v(1)
            load_qk(sp, 3)
            for h in range(1, H - 1):
                sp.wait_ge(s_pv, 4 + UN * h)
                load_v(h + 1)
                if h + 3 < H:
                    load_qk(sp, h + 3)
            sp.wait_ge(s_pv, 4 + H * UN)
            sp.dma_start(boB[:, :], bo.partition_broadcast(T)).then_inc(s_bo, 16)
            store_rows("O", [out], [ot])
            for k in range(4):
                sp.wait_ge(s_st[k], ST_END)
            sp.wait_ge(s_x2[0], 16 * (NT // 2))
            sp.wait_ge(s_x2[1], 16 * (NT // 2))

        @block.gpsimd
        def _(g):
            g.sem_inc(s_wready, 2)
            g.sem_inc(s_el[1], 2)
            g.memset(ident[:, :], 0.0).then_inc(s_gp, 1)
            g.memset(ones[:, :], 1.0).then_inc(s_const, 1)
            g.wait_ge(s_gp, 1)
            g.affine_select(out=ident[:, :], in_=ident[:, :], compare_op=ALU.not_equal, fill=1.0,
                            base=0, pattern=[[-1, 128]], channel_multiplier=1).then_inc(s_const, 1)
            imp = dict(allow_small_or_imprecise_dtypes=True)
            g.iota(iot[:, :], pattern=[[1, KW]], base=0, channel_multiplier=0, **imp).then_inc(s_const, 1)
            g.iota(tk[:, :], pattern=[[KW, NW]], base=0, channel_multiplier=0, **imp).then_inc(s_const, 1)
            g.iota(iotw[:, :], pattern=[[1, NW]], base=0, channel_multiplier=0, **imp).then_inc(s_const, 1)
            g.iota(iot4[:, :], pattern=[[1, NE]], base=0, channel_multiplier=0, **imp).then_inc(s_const, 1)
            g.iota(pcol[:, 0:1], pattern=[[0, 1]], base=NG, channel_multiplier=-1, **imp).then_inc(s_const, 1)
            g.iota(pcol[:, 1:2], pattern=[[0, 1]], base=1, channel_multiplier=1, **imp).then_inc(s_const, 1)

            gp = [1]

            def split_half(w, u, kh, hi_value):
                g.tensor_copy(Wh[u][:, 4 * kh:4 * kh + 4, :], w).then_inc(s_gp, 1)
                g.wait_ge(s_gp, hi_value)
                g.tensor_sub(Wl[u][:, 4 * kh:4 * kh + 4, :], w, Wh[u][:, 4 * kh:4 * kh + 4, :].bitcast(f32))\
                 .then_inc(s_wready, 1)

            def cols_(i, u):
                c0 = i * 512 + u * WQ
                return slice(c0, c0 + WQ) if isinstance(i, int) else ds(c0, WQ)

            def quarters(ph, w, loads):
                wv = w.rearrange("(k p) n -> p k n", p=128)
                with g.Fori(0, 2) as i:
                    for u in range(2):
                        g.wait_ge(s_wready, i * 4 + (2 * (WRDY[ph] + u) + 2))
                        for kh in range(2):
                            g.dma_start(Wst[:, kh, :, :], wv[:, 4 * kh:4 * kh + 4, cols_(i, u)])\
                             .then_inc(s_w[kh], 16)
                        for kh in range(2):
                            wait_apart(g, s_w[kh], i * 32 + 16 * (loads + u + 1))
                            if kh == 0:
                                wait_apart(g, s_acc, slot_free(ph, u, i))
                            split_half(Wst[:, kh, :, :], u, kh, i * 4 + (gp[0] + 2 * u + kh + 1))
                gp[0] += 8

            def mix_load(q, kh):
                wv = (mWq, mWk)[q // 4].rearrange("(k p) n -> p k n", p=128)
                g.dma_start(Wst[:, kh, :, :], wv[:, 4 * kh:4 * kh + 4, cols_(q % 4 // 2, q % 2)]).then_inc(s_w[kh], 16)

            for kh in range(2):
                mix_load(0, kh)
            for q in range(8):
                for kh in range(2):
                    g.wait_ge(s_whi, 2 * q + kh + 1)
                    g.tensor_sub(Wl[q % 2][:, 4 * kh:4 * kh + 4, :], Wst[:, kh, :, :],
                                 Wh[q % 2][:, 4 * kh:4 * kh + 4, :].bitcast(f32)).then_inc(s_wready, 1)
                    if q < 7:
                        g.wait_ge(s_wready, 2 + 2 * q + kh + 1)
                        mix_load(q + 1, kh)
            for t in range(NT):
                g.wait_ge(s_xh, t + 1)
                if t >= 2:
                    g.wait_ge(s_G, t - 1)
                g.tensor_sub(xnl[t % 2][:, :], xn[:, t % 2, :], xnh[t % 2][:, :].bitcast(f32)).then_inc(s_xl, 1)
            wst_rows = Wst[:, :, :, :].rearrange("p a b c -> p (a b c)").rearrange("p (e n) -> p e n", e=2)
            g.wait_ge(s_wready, 2 * WRDY["Y0"] + 2)
            for j in range(4):
                if j:
                    g.wait_ge(s_wt, 4 * j)
                g.dma_start(wst_rows, mWv[j * WQ:(j + 1) * WQ, :].rearrange("(e p) n -> p e n", p=128))\
                 .then_inc(s_wv, 16)
            g.wait_ge(s_wt, 16)
            quarters("Y0", W_neigh0, 8)
            quarters("S0", W_self0, 12)
            quarters("Y1", W_neigh1, 16)
            quarters("S1", W_self1, 20)
            g.wait_ge(s_gate, 1)
            e1 = g.value_load(gidx[0:1, 0:1], min_val=0, max_val=NE - 1)
            e2 = g.value_load(gidx[0:1, 1:2], min_val=0, max_val=NE - 1)

            def expert_load(q, kh):
                wv = (fWq, fWk, fWv)[q // 4].rearrange("e (k p) n -> p e k n", p=128)
                for a, e in enumerate((e1, e2)):
                    g.dma_start(wst2[:, kh, a, :, :], wv[:, ds(e, 1), 4 * kh:4 * kh + 4, q % 4 * WQ:(q % 4 + 1) * WQ]
                                .rearrange("p e k n -> p (e k) n")).then_inc(s_we[kh], 16)

            for kh in range(2):
                expert_load(0, kh)
            for kh in range(2):
                g.wait_ge(s_wready, 2 * WRDY["Q"] + 2 + kh + 1)
                expert_load(1, kh)
            for q in range(1, 12):
                for kh in range(2):
                    g.wait_ge(s_comb, 2 * q + kh + 1)
                    if kh == 0:
                        g.wait_ge(s_acc, slot_free("QKV"[q // 4], q % 2, q % 4 // 2))
                    gp[0] += 1
                    split_half(wst2[:, kh, 0, :, :], q % 2, kh, gp[0])
                    if q < 11:
                        g.wait_ge(s_wready, 2 * WRDY["Q"] + 2 + 2 * q + kh + 1)
                        expert_load(q + 1, kh)
            g.wait_ge(s_wready, 2 * WRDY["V"] + 2 + 8)
            for k in range(4):
                g.wait_ge(s_st[k], STORED["V"])
            load_qk(g, 0)
            fills = [(MB[:, :, 0:HD], 0.0), (VS[0][:, :, HD:2 * HD], 1.0), (VS[1][:, :, HD:2 * HD], 1.0)]
            fills += [(KM[k][HD:HD + 2, :], 1.0) for k in range(HB)]
            for n, (a, value) in enumerate(fills):
                if n == 4:
                    g.wait_ge(s_acc, N["O"])
                if n == 6:
                    for k in range(4):
                        g.wait_ge(s_st[k], STORED["O"])
                g.memset(a.bitcast(f32), value).then_inc(s_fill, 1)
                g.wait_ge(s_fill, n + 1)

            def odd_lows(i, hh):
                for q in range(UN):
                    n = hh * UN + q
                    if q % 2:
                        cn = CH[q // NT][1]
                        wait_apart(g, s_ex, i * (HB * UN) + (n + 1 + 2))
                        g.tensor_sub(EL[n % 4][:, 0:cn], EX[n % 3][:, 0:cn], EH[n % 4][:, 0:cn].bitcast(f32))\
                         .then_inc(s_el[1], 1)

            with g.Fori(0, H // HB - 1) as i:
                for hh in range(HB):
                    odd_lows(i, hh)
            for hh in range(HB - 1):
                odd_lows(H // HB - 1, hh)
            g.wait_ge(s_pv, 4 + UN * (H - 1))
            quarters("O", Wo, 24)

        @block.scalar
        def _(act):
            act.sem_inc(s_winev, 2)
            act.sem_inc(s_ex, 2)
            own = Count()

            def order(ins):
                ins.then_inc(s_act, 1)
                act.wait_ge(s_act, own.add())

            def highs(ph, loops, per, dst_of, bias_of=None, p=128, cols=None, slots=0, uses=0, after=None):
                with act.Fori(0, loops) as i:
                    for j in range(per):
                        slot = (N[ph] + j) % 4
                        n_ = cols(j)
                        wait_apart(act, s_acc, i * per + (N[ph] + j + 1))
                        if uses:
                            wait_apart(act, s_st[slot], i * (uses * per // 4) + (STORED[ph] + uses * (j // 4)))
                        b_ = bias_of(i, j) if bias_of else 0.0
                        act.activation(dst_of(i, j).bitcast(f32r) if uses else dst_of(i, j), bank(slot, p, n_),
                                       ACT.Identity if bias_of else ACT.Copy, bias=b_).then_inc(s_hi, 1)
                        if after:
                            after(i, j)

            def window_out(w, u):
                wait_apart(act, s_win, w + 1)
                act.copy(adjr[:, :, ds(w * DW, DW)].bitcast(f32),
                         bank(4 + u, T, KW).rearrange("p (b d) -> p b d", d=DW)).then_inc(s_winev, 1)

            def transposed_hi(t, m):
                for b in range(2):
                    act.wait_ge(s_T, m(b))
                    act.copy(XTh[:, 4 * b:4 * b + 4, t], bank(4 + b, 128, 4 * T).rearrange("p (k n) -> p k n", n=T))\
                       .then_inc(s_Thi, 1)

            def feature_exp(m, p, n_):
                act.wait_ge(s_elm, m + 1)
                act.activation(elm[0:p, m % 2, 0:n_], elm[0:p, m % 2, 0:n_], ACT.Exp).then_inc(s_ele, 1)

            def weights_hi(q):
                for kh in range(2):
                    act.wait_ge(s_w[kh], 16 * (q + 1))
                    if kh == 0 and q >= 2:
                        act.wait_ge(s_acc, 2 * (q - 1))
                    act.copy(Wh[q % 2][:, 4 * kh:4 * kh + 4, :], Wst[:, kh, :, :]).then_inc(s_whi, 1)

            weights_hi(0)
            weights_hi(1)
            for t in range(NT):
                if t < 8:
                    for j in range(2 * t, 2 * t + 2):
                        act.wait_ge(s_acc, j + 1)
                        act.copy((Mqh, Mkh)[j // 8][:, j % 8, :], bank(j % 4, 128, PF_)).then_inc(s_hi, 1)
                if t == 0:
                    act.wait_ge(s_bnd, 1)
                transposed_hi(slice(t * T, (t + 1) * T), lambda b: 2 * t + b + 1)
                if t + 2 < 8:
                    weights_hi(t + 2)
            for t in range(NT + 1):
                if t < NT:
                    act.wait_ge(s_xg, t + 1)
                    if t >= 2:
                        act.wait_ge(s_G, t - 1)
                    act.copy(xnh[t % 2][:, :], xn[:, t % 2, :]).then_inc(s_xh, 1)
                if t >= 1:
                    m = t - 1
                    feature_exp(m, T, PF_)
                    act.wait_ge(s_elf, m + 1)
                    if m >= 2:
                        act.wait_ge(s_G, m - 1)
                    act.copy(kph[:, m % 2, :], elf[0:T, m % 2, 0:PF_]).then_inc(s_elh, 1)
            act.wait_ge(s_acc, N["GT"] + 4)
            for j in range(4):
                act.copy(GTh[:, 2 * j:2 * j + 2, :].rearrange("p a n -> p (a n)"), bank(j)).then_inc(s_hi, 1)
            for j in range(PB * 3):
                c0, cn = CH[j % 3]
                feature_exp(NT + j, 128, cn)
                act.wait_ge(s_elf, NT + j + 1)
                act.copy(qph[:, j // 3, c0:c0 + cn], elf[:, (NT + j) % 2, 0:cn]).then_inc(s_elh, 1)
            for j in range(4):
                for b in range(4):
                    act.wait_ge(s_wt, 4 * j + b + 1)
                    if b == 0:
                        act.wait_ge(s_acc, slot_free("KV", j % 2, j // 2))
                    act.copy(Wh[j % 2][:, 2 * b:2 * b + 2, :].rearrange("p a n -> p (a n)"), bank(4 + b))\
                       .then_inc(s_wthi, 1)
                for b in range(PB):
                    m = PB * j + b
                    act.wait_ge(s_acc, N["KV"] + m + 1)
                    act.copy(kvh[:, b, j * WQ:(j + 1) * WQ], bank((N["KV"] + m) % 4, 128, WQ)).then_inc(s_hi, 1)
            for k in range(2):
                act.wait_ge(s_bt[k], 16 * NT)

            def y0_windows(i, j):
                if j in WIN_Y0:
                    k = WIN_Y0.index(j)
                    window_out(act.snap(i * len(WIN_Y0) + k), k % 2)

            highs("Y0", 2, 2 * NT, lambda i, j: y0t[0][0:T, (N["Y0"] + j) % 4, 0:WQ], p=T, cols=lambda j: WQ, uses=32,
                  after=y0_windows)
            act.wait_ge(s_done, 4 + N["S0"])
            for k in range(4):
                act.wait_ge(s_st[k], STORED["S0"])
            with act.Fori(0, 2) as i:
                for j in range(12):
                    slot, cn = (N["S0"] + j) % 4, CH[j % 3][1]
                    wait_apart(act, s_acc, i * 12 + (N["S0"] + j + 1))
                    wait_apart(act, s_st[slot], i * 48 + (STORED["S0"] + 16 * (j // 4)))
                    act.copy(s0t[:, slot, 0:cn], bank(slot, 128, cn)).then_inc(s_done, 1)
                    for k in WIN_S0[j]:
                        window_out(act.snap(i * NS0 + (2 * len(WIN_Y0) + k)), k % 2)
            for m in range(3 * KB):
                c0, cn = CH[m % 3]
                act.wait_ge(s_zt, m + 1)
                act.copy(XTh[:, m // 3, c0:c0 + cn], zt[:, m % 2, 0:cn]).then_inc(s_hh, 1)
            act.wait_ge(s_adj, 16 * NT)
            highs("Y1", 2, 2 * NT, lambda i, j: y1h[:, j % NT, ds(i * 512 + j // NT * WQ, WQ)], p=T, cols=lambda j: WQ)
            act.wait_ge(s_row, 32)
            with act.Fori(0, 2) as i:
                for j in range(2 * NT):
                    slot, u, t = (N["S1"] + j) % 4, j // NT, j % NT
                    act.wait_ge(s_st[slot], i * 80 + (STORED["S1"] + 16 * (j // 4)))
                    act.dma_start(bs[:, slot, :], base[t * T:(t + 1) * T, ds(i * 512 + u * WQ, WQ)])\
                       .then_inc(s_bs[slot], 16)

            for t in range(NT):
                transposed_hi(slice(t * T, (t + 1) * T), lambda b: 2 * (NT + t) + b + 1)
            act.wait_ge(s_gmm, 1)
            act.wait_ge(s_gw, 16 * 4)
            act.activation(hid[:, :], bank(6, 128, 1), ACT.Relu, bias=bg1c[:, 0:1]).then_inc(s_ghid, 1)
            act.wait_ge(s_pool, 2)
            act.activation(gate[:, 33:34], gate[:, 32:33], ACT.Exp).then_inc(s_ghid, 1)
            for k in range(2):
                act.wait_ge(s_x2[k], 16 * (NT // 2))
            for kh in range(2):
                act.wait_ge(s_comb, kh + 1)
                act.copy(Wh[0][:, 4 * kh:4 * kh + 4, :], wst2[:, kh, 0, :, :]).then_inc(s_whi, 1)
            for a, ph in enumerate(("Q", "K")):
                highs(ph, 2, 12, lambda i, j: ot2[0][:, (N[ph] + j) % 4, 0:CH[j % 3][1]],
                      bias_of=lambda i, j: qkvb[:, ds(i * 4 + (KB * a + j // 3), 1)], cols=lambda j: CH[j % 3][1], uses=32)

            highs("V", 2, 2 * NT, lambda i, j: ot2[0][0:T, (N["V"] + j) % 4, 0:WQ], p=T, cols=lambda j: WQ, uses=32)

            def maxima_rows(i, h1, grp):
                t0, t1 = MG[grp]
                act.wait_ge(s_mt, i * (HB * NT) + (h1 * NT + t1))
                act.copy(QM[h1 % HB][HD:HD + 2, t0 * T:t1 * T], ps[HD:HD + 2, 3584:3584 + (t1 - t0) * T])\
                   .then_inc(s_mr, 1)

            def output_hi(i, k):
                h, (c0, cn) = k // 3, CH[k % 3]
                rows = slice(HD * (h % 2), HD * (h % 2) + HD)
                blk = i * (HB // 2) + h // 2
                act.wait_ge(s_ob, i * (3 * HB) + (k + 1 + 2))
                act.activation(XTh[rows, ds(blk, 1), c0:c0 + cn].rearrange("p a n -> p (a n)"), OB[k % 2][rows, 0:cn],
                               ACT.Identity, bias=qkvb[rows, ds(blk + 2 * KB, 1)]).then_inc(s_ao, 1)

            def heads(i, first, last):
                for n in range(HB * UN):
                    h, q = n // UN, n % UN
                    c, j = q // NT, q % NT
                    cn = CH[c][1]
                    for grp in range(3):
                        if q == min(ROWS_AT[MG[grp][1] - 1] + 1, UN - 1) and not (last and h == HB - 1):
                            maxima_rows(i, h + 1, grp)
                    src_ = bank(3 + n % 2, T, cn)
                    wait_apart(act, s_sc, i * (HB * UN) + (n + 1))
                    act.wait_ge(s_pv, i * (HB * UN) + (n + 1))
                    act.activation(EH[n % 4][:, 0:cn], src_, ACT.Exp, scale=SCALE).then_inc(s_eh, 1)
                    if last and h == HB - 1 and q >= 3 and (n - 3) % 2:
                        act.wait_ge(s_el[2], (q - 3) // 2 + 1)
                    else:
                        act.wait_ge(s_el[(n - 3) % 2], i * (HB * UN // 2) + ((n - 3) // 2 + 1 + 2))
                    act.activation(EX[n % 3][:, 0:cn], src_, ACT.Exp, scale=SCALE).then_inc(s_ex, 1)
                    for k, part in output_steps(n, first, last):
                        if part == 4:
                            output_hi(i, k)
                if last:
                    for k, part in output_steps(HB * UN, first, last):
                        if part == 4:
                            output_hi(i, k)

            for grp in range(3):
                maxima_rows(0, 0, grp)
            heads(0, True, False)
            with act.Fori(0, H // HB - 2) as i:
                heads(act.snap(i + 1), False, False)
            heads(H // HB - 1, False, True)
            with act.Fori(0, 2) as i:
                for j in range(2 * NT):
                    slot, u, t = (N["O"] + j) % 4, j // NT, j % NT
                    act.wait_ge(s_done, i * (2 * NT) + (N["O"] + j + 1))
                    act.dma_start(x2r[:, slot, :], x2d[t * T:(t + 1) * T, ds(i * 512 + u * WQ, WQ)])\
                       .then_inc(s_x2r[slot], 16)

        @block.vector
        def _(dve):
            v_ = nc.vector
            dve.sem_inc(s_done, 4)
            dve.sem_inc(s_el[0], 2)
            dve.sem_inc(s_ob, 2)
            own = Count()

            def order(ins):
                ins.then_inc(s_dve, 1)
                dve.wait_ge(s_dve, own.add())

            def flat(a):
                return a.rearrange("p a n -> p (a n)")

            v_.memset(zw[:, :], 0.0).then_inc(s_const, 1)
            dve.wait_ge(s_const, 9)
            v_.tensor_copy(onesr[:, :], ones[:, 0:2]).then_inc(s_const, 1)
            dve.wait_ge(s_edges, 32)
            sf, df, hf, bf_, slf, kf = (ef[:, k, :] for k in range(6))
            v_.tensor_copy(sf, raw[:, 0, :]).then_inc(s_dve, 1); own.add()
            v_.tensor_copy(df, raw[:, 1, :]).then_inc(s_dve, 1); own.add()
            order(v_.tensor_scalar(dhi_i[:, :], raw[:, 1, :], 5, None, ALU.logical_shift_right))
            order(v_.tensor_copy(hf, dhi_i[:, :]))
            order(v_.tensor_scalar(bf_, sf, float(T), None, ALU.is_ge))
            for b in range(2, NT):
                order(v_.scalar_tensor_tensor(bf_, sf, float(T * b), bf_, ALU.is_ge, ALU.add))
            v_.scalar_tensor_tensor(slf, bf_, -float(T), sf, ALU.mult, ALU.add).then_inc(s_idx, 1)
            order(v_.scalar_tensor_tensor(kf, bf_, float(DW), df, ALU.mult, ALU.add))
            v_.scalar_tensor_tensor(kf, hf, float(KW - DW), kf, ALU.mult, ALU.add).then_inc(s_idx, 1)
            order(v_.tensor_reduce(gmm[:, 0:1], hf, AX.X, ALU.min))
            order(v_.tensor_reduce(gmm[:, 1:2], hf, AX.X, ALU.max))
            order(v_.tensor_scalar(cond[:, 0, :], iotw[0:NG, :], gmm[:, 0:1], None, ALU.is_ge))
            order(v_.scalar_tensor_tensor(cond[:, 0, :], iotw[0:NG, :], gmm[:, 1:2], cond[:, 0, :], ALU.is_le, ALU.mult))
            v_.tensor_scalar(cond[:, 1, :], cond[:, 0, :], pcol[0:NG, 0:1], None, ALU.mult).then_inc(s_idx, 1)
            v_.tensor_scalar(cond[:, 2, :], cond[:, 0, :], pcol[0:NG, 1:2], None, ALU.mult).then_inc(s_idx, 1)
            dve.wait_ge(s_idxT, 1)
            v_.tensor_copy(slo[:, :].rearrange("e (p g) -> e g p", g=GE),
                           bank(4, T, ET).rearrange("e (g p) -> e g p", g=GE)).then_inc(s_dve, 1); own.add()
            dve.wait_ge(s_idxT, 2)
            v_.tensor_copy(key[:, :].rearrange("e (p g) -> e g p", g=GE),
                           bank(5, T, ET).rearrange("e (g p) -> e g p", g=GE)).then_inc(s_dve, 1); own.add()
            dve.wait_ge(s_idxT, 3)
            v_.tensor_reduce(bnd[:, 0:1], bank(6, NW, NG), AX.X, ALU.max).then_inc(s_idx, 1)
            v_.tensor_reduce(bnd[:, 1:2], bank(6, NW, NG, NG), AX.X, ALU.max).then_inc(s_idx, 1)
            dve.wait_ge(s_idxT, 4)
            order(v_.tensor_scalar(brow[:, 0, :], bank(7, 1, NW), -1.0, float(NG), ALU.mult, ALU.add))
            order(v_.tensor_sub(brow[:, 1, :], bank(7, 1, NW, NW), brow[:, 0, :]))
            order(v_.tensor_scalar(brow[:, 2, :], brow[:, 0, :], float(NG - 1), None, ALU.min))
            order(v_.tensor_scalar(brow[:, 3, :], brow[:, 1, :], 1.0, None, ALU.max))
            order(v_.tensor_copy(bint[:, :, :], brow[:, 2:4, :]))
            v_.memset(degmax[:, :], 0.0).then_inc(s_bnd, 1)

            tot = dve.alloc_register("groups_dve")
            dve.reg_mov(tot, 0)
            at_tile = dve.alloc_register("first_tile_dve")

            def window_onehots(w):
                lo = dve.value_load(bint[0:1, 0, ds(w, 1)], min_val=0, max_val=NG - 1)
                cnt = dve.value_load(bint[0:1, 1, ds(w, 1)], min_val=1, max_val=NG)
                before = dve.snap(tot, min_val=0, max_val=NW * NG)
                dve.reg_mov(at_tile, lo * GE)
                tk_ = tk[0:T, ds(w, 1)]
                with dve.Fori(0, cnt) as k:
                    col = dve.snap(at_tile, min_val=0, max_val=ET - GE)
                    r = dve.snap(((before + k) & (RING // GE - 1)) * GE, min_val=0, max_val=RING - GE)
                    dve.wait_ge(s_ohfree, (before + k) + 1)
                    ohs_, ohk_ = ohs[:, ds(r, GE), :], ohk[:, ds(r, GE), :]
                    slo_, key_ = slo[:, ds(col, GE)], key[:, ds(col, GE)]
                    v_.tensor_tensor(ohs_, iot[0:T, 0:128].unsqueeze(1).to_broadcast([T, GE, 128]),
                                     slo_.unsqueeze(2).to_broadcast([T, GE, 128]), ALU.is_equal)
                    for m in range(GE):
                        ins = v_.tensor_scalar(ohk_[:, m, :], iot[0:T, :], tk_, key_[:, m:m + 1], ALU.add, ALU.is_equal)
                    ins.then_inc(s_oh, 1)
                    dve.reg_add(at_tile, at_tile, GE)
                dve.reg_add(tot, tot, cnt)

            def lows(ph, loops, per, hi_of, lo_of, bias_of=None, p=128, cols=None, before=None, own=None,
                     own_per=0):
                with dve.Fori(0, loops) as i:
                    if own:
                        own.enter(i, own_per)
                    for j in range(per):
                        if before:
                            before(i, j)
                        slot = (N[ph] + j) % 4
                        dve.wait_ge(s_hi, i * per + (HI[ph] + j + 1))
                        a = bank(slot, p, cols(j))
                        if bias_of:
                            ins = v_.scalar_tensor_tensor(lo_of(i, j), a, bias_of(i, j), hi_of(i, j), ALU.add, ALU.subtract)
                        else:
                            ins = v_.tensor_sub(lo_of(i, j), a, hi_of(i, j))
                        ins.then_inc(s_done, 1)
                if own:
                    own.leave(loops)

            def normalise(src_, dst_, done, keep=None):
                for c in range(2):
                    v_.bn_stats(st6[:, c, :], src_[:, 512 * c:512 * c + 512]).then_inc(s_dve, 1)
                    last = own.add()
                dve.wait_ge(s_dve, last)
                order(v_.bn_aggr(mv[:, 0:2], st6[:, :, :].rearrange("p a b -> p (a b)")))
                order(v_.tensor_scalar(mv[:, 2:3], mv[:, 1:2], 1e-5, None, ALU.add))
                order(v_.tensor_scalar(mv[:, 3:4].bitcast(i32), mv[:, 2:3].bitcast(i32), 1, None,
                                       ALU.logical_shift_right))
                order(v_.tensor_copy(mv[:, 4:5], mv[:, 3:4].bitcast(i32)))
                order(v_.tensor_scalar(mv[:, 4:5], mv[:, 4:5], float(0x1FC00000), None, ALU.add))
                order(v_.tensor_copy(mv[:, 3:4].bitcast(i32), mv[:, 4:5]))
                for _ in range(3):
                    order(v_.reciprocal(mv[:, 4:5], mv[:, 3:4]))
                    order(v_.scalar_tensor_tensor(mv[:, 4:5], mv[:, 4:5], mv[:, 2:3], mv[:, 3:4], ALU.mult, ALU.add))
                    order(v_.tensor_scalar(mv[:, 3:4], mv[:, 4:5], 0.5, None, ALU.mult))
                order(v_.reciprocal(mv[:, 5:6], mv[:, 3:4]))
                if keep is not None:
                    v_.tensor_copy(stat[:, keep, 0:1], mv[:, 0:1]).then_inc(s_dve, 1); own.add()
                    v_.tensor_copy(stat[:, keep, 1:2], mv[:, 5:6]).then_inc(s_dve, 1); own.add()
                v_.tensor_scalar(dst_, src_, mv[:, 0:1], mv[:, 5:6], ALU.subtract, ALU.mult).then_inc(done, 1)

            def transposed_lo(t, m, sums=None):
                for b in range(2):
                    dve.wait_ge(s_Thi, m(b))
                    a = bank(4 + b, 128, 4 * T).rearrange("p (k n) -> p k n", n=T)
                    if sums is not None:
                        v_.tensor_reduce(pooled[:, sums, 4 * b:4 * b + 4], a, AX.X, ALU.add).then_inc(s_dve, 1)
                        own.add()
                    v_.tensor_sub(XTl[:, 4 * b:4 * b + 4, t], a, XTh[:, 4 * b:4 * b + 4, t].bitcast(f32))\
                      .then_inc(s_Tlo, 1)

            def feature(m, a, p, n_, full, hi_, lo_):
                s = m % 2
                dve.wait_ge(*full)
                v_.tensor_scalar(elm[0:p, s, 0:n_], a, 0.0, None, ALU.min).then_inc(s_elm, 1)
                dve.wait_ge(s_ele, m + 1)
                ins = v_.scalar_tensor_tensor(elf[0:p, s, 0:n_], a, 0.0, elm[0:p, s, 0:n_], ALU.max, ALU.add)
                ins.then_inc(s_elf, 1)
                dve.wait_ge(s_elh, m + 1)
                v_.tensor_sub(lo_, elf[0:p, s, 0:n_], hi_.bitcast(f32)).then_inc(s_ell, 1)

            dve.wait_ge(s_proj, 16)
            order(v_.tensor_copy(prh[:, :, :], prf[:, :, :]))
            v_.tensor_sub(prl[:, :, :], prf[:, :, :], prh[:, :, :].bitcast(f32)).then_inc(s_proj, 1)

            def x_tile(t):
                dve.wait_ge(s_x[t % 2], 16 * (t // 2 + 1))
                if t >= 2:
                    dve.wait_ge(s_T, 2 * (t - 1))
                normalise(xs[:, t % 2, :], xn[:, t % 2, :], s_xn, keep=t)

            x_tile(0)
            for t in range(NT):
                if t + 1 < NT:
                    x_tile(t + 1)
                if t < 8:
                    for j in range(2 * t, 2 * t + 2):
                        mh, ml = ((Mqh, Mql), (Mkh, Mkl))[j // 8]
                        dve.wait_ge(s_hi, j + 1)
                        v_.tensor_sub(ml[:, j % 8, :], bank(j % 4, 128, PF_), mh[:, j % 8, :].bitcast(f32))\
                          .then_inc(s_done, 1)
                transposed_lo(slice(t * T, (t + 1) * T), lambda b: 2 * t + b + 1)
            for t in range(NT + 1):
                if t < NT:
                    dve.wait_ge(s_x[t % 2], 16 * ((NT + t) // 2 + 1))
                    if t < 2:
                        dve.wait_ge(s_T, 2 * NT)
                    else:
                        dve.wait_ge(s_xl, t - 1)
                    v_.tensor_scalar(xn[:, t % 2, :], xs[:, t % 2, :], stat[:, t, 0:1], stat[:, t, 1:2],
                                     ALU.subtract, ALU.mult).then_inc(s_xg, 1)
                if t >= 1:
                    m = t - 1
                    feature(m, bank(6 + m % 2, T, PF_), T, PF_, (s_kp, m + 1), kph[:, m % 2, :], kpl[:, m % 2, :])
            for j in range(4):
                dve.wait_ge(s_hi, HI["GT"] + j + 1)
                v_.tensor_sub(flat(GTl[:, 2 * j:2 * j + 2, :]), bank(j), flat(GTh[:, 2 * j:2 * j + 2, :]).bitcast(f32))\
                  .then_inc(s_done, 1)
            for j in range(PB * 3):
                c0, cn = CH[j % 3]
                feature(NT + j, bank((N["QP"] + j) % 4, 128, cn), 128, cn, (s_acc, N["QP"] + j + 1),
                        qph[:, j // 3, c0:c0 + cn], qpl[:, j // 3, c0:c0 + cn])
                dve.wait_ge(s_elf, NT + j + 1)
                dve.sem_inc(s_done, 1)
            for j in range(4):
                for b in range(4):
                    dve.wait_ge(s_wthi, 4 * j + b + 1)
                    v_.tensor_sub(flat(Wl[j % 2][:, 2 * b:2 * b + 2, :]), bank(4 + b),
                                  flat(Wh[j % 2][:, 2 * b:2 * b + 2, :]).bitcast(f32)).then_inc(s_wtlo, 1)
                for b in range(PB):
                    m = PB * j + b
                    dve.wait_ge(s_hi, HI["KV"] + m + 1)
                    v_.tensor_sub(kvl[:, b, j * WQ:(j + 1) * WQ], bank((N["KV"] + m) % 4, 128, WQ),
                                  kvh[:, b, j * WQ:(j + 1) * WQ].bitcast(f32)).then_inc(s_done, 1)
            dve.wait_ge(s_b1, 16)
            for t in range(NT):
                dve.wait_ge(s_xr[t % 2], 16 * (t // 2 + 1))
                order(v_.tensor_add(xr[:, t % 2, :], xr[:, t % 2, :], b1B[:, :]))
                dve.wait_ge(s_z, t + 1)
                order(v_.tensor_scalar(zcol[:, 0:1], bank(4 + t % 2, T, 1), 1e-8, None, ALU.add))
                order(v_.reciprocal(zcol[:, 1:2], zcol[:, 0:1]))
                for c in range(2):
                    m = N["NUM"] + 2 * t + c
                    dve.wait_ge(s_acc, m + 1)
                    if t:
                        dve.wait_ge(s_bt[c], 16 * t)
                    v_.scalar_tensor_tensor(bt2[:, c, :], bank(m % 4, T, 512), zcol[:, 1:2],
                                            xr[:, t % 2, 512 * c:512 * c + 512], ALU.mult, ALU.add).then_inc(s_done, 1)
            def y0_windows(i, j):
                if j + 2 in WIN_Y0:
                    window_onehots(dve.snap(i * len(WIN_Y0) + WIN_Y0.index(j + 2)))

            lows("Y0", 2, 2 * NT, lambda i, j: y0t[0][0:T, (N["Y0"] + j) % 4, 0:WQ],
                 lambda i, j: y0t[1][0:T, (N["Y0"] + j) % 4, 0:WQ].bitcast(f32r), p=T, cols=lambda j: WQ,
                 before=y0_windows)
            def column_sums(c0, n_):
                v_.tensor_reduce(degp[:, ds(c0, n_)], adjr[:, :, ds(c0, n_)].bitcast(f32).rearrange("p b d -> p d b"),
                                 AX.X, ALU.add).then_inc(s_degp, 1)

            dve.wait_ge(s_winev, 2 + 2 * len(WIN_Y0) - 1)
            column_sums(0, DW * (2 * len(WIN_Y0) - 1))
            with dve.Fori(0, 2) as i:
                for k in range(NS0):
                    w = dve.snap(i * NS0 + (2 * len(WIN_Y0) + k))
                    window_onehots(w)
                    dve.wait_ge(s_winev, i * NS0 + (2 + 2 * len(WIN_Y0) + k))
                    column_sums(dve.snap(i * (NS0 * DW) + (2 * len(WIN_Y0) + k - 1) * DW), DW)
            dve.wait_ge(s_winev, 2 + NW)
            column_sums((NW - 1) * DW, R - (NW - 1) * DW)
            for c, (c0, cn) in enumerate(CH):
                dve.wait_ge(s_deg, c + 1)
                v_.tensor_scalar(deginvB[:, c0:c0 + cn], bank((6, 7, 4)[c], 128, cn), 1.0, None, ALU.max)\
                  .then_inc(s_dve, 1)
                last = own.add()
            dve.wait_ge(s_dve, last)
            order(v_.tensor_reduce(degmax[:, 0:1], deginvB[0:1, :], AX.X, ALU.max))
            order(v_.tensor_scalar(degmax[:, 1:2], degmax[:, 0:1], FAST_MAX, None, ALU.is_gt))
            v_.tensor_copy(slow[:, :], degmax[:, 1:2]).then_inc(s_slow, 1)
            for c0, cn in CH:
                v_.reciprocal(deginvB[:, c0:c0 + cn], deginvB[:, c0:c0 + cn]).then_inc(s_dinv, 1)
            for m in range(3 * KB):
                c0, cn = CH[m % 3]
                z = zt[:, m % 2, 0:cn]
                if m < 3:
                    dve.wait_ge(s_dinv, m + 1)
                dve.wait_ge(s_acc, N["HT"] + m + 1)
                order(v_.tensor_mul(z, bank((N["HT"] + m) % 4, 128, cn), deginvB[:, c0:c0 + cn]))
                dve.wait_ge(s_s0[m % 2], 16 * (m // 2 + 1))
                order(v_.tensor_add(z, z, s0c[:, m % 2, 0:cn]))
                v_.tensor_scalar(z, z, b0c[:, m // 3:m // 3 + 1], 0.0, ALU.add, ALU.max).then_inc(s_zt, 1)
                dve.wait_ge(s_hh, m + 1)
                v_.tensor_sub(XTl[:, m // 3, c0:c0 + cn], z, XTh[:, m // 3, c0:c0 + cn].bitcast(f32)).then_inc(s_done, 1)
            lows("Y1", 2, 2 * NT, lambda i, j: y1h[:, j % NT, ds(i * 512 + j // NT * WQ, WQ)].bitcast(f32),
                 lambda i, j: y1l[:, j % NT, ds(i * 512 + j // NT * WQ, WQ)], p=T, cols=lambda j: WQ)
            with dve.Fori(0, 2) as i:
                for j in range(2 * NT):
                    slot = (N["S1"] + j) % 4
                    dve.wait_ge(s_acc, i * (2 * NT) + (N["S1"] + j + 1))
                    dve.wait_ge(s_bs[slot], i * 80 + 16 * (j // 4 + 1))
                    v_.tensor_add(bs[:, slot, :], bank(slot, T, WQ), bs[:, slot, :]).then_inc(s_done, 1)
            dve.wait_ge(s_row, 32)
            for t in range(NT + 1):
                if t < NT:
                    s = t % 2
                    dve.wait_ge(s_b2[s], 16 * (t // 2 + 1))
                    if t >= 2:
                        dve.wait_ge(s_x2[s], 16 * (t // 2))
                        dve.wait_ge(s_T, 2 * (NT + t - 1))
                    for c in range(2):
                        m = N["X2"] + 2 * t + c
                        dve.wait_ge(s_acc, m + 1)
                        v_.scalar_tensor_tensor(x2s[:, s, 512 * c:512 * c + 512], bank(m % 4, T, 512), deginv[:, t:t + 1],
                                                b2[:, s, 512 * c:512 * c + 512], ALU.mult, ALU.add).then_inc(s_done, 1)
                    dve.wait_ge(s_done, 4 + N["X2"] + 2 * t + 2)
                    normalise(x2s[:, s, :], x2n[:, s, :], s_x2n)
                if t >= 1:
                    transposed_lo(slice((t - 1) * T, t * T), lambda b: 2 * (NT + t - 1) + b + 1, sums=t - 1)
            def combine(q4, kh, q):
                sa, sb_ = wst2[:, kh, 0, :, :], wst2[:, kh, 1, :, :]
                dve.wait_ge(s_we[kh], q4 * 32 + 32 * (q + 1))
                order(v_.tensor_scalar(sa, sa, wsel[:, 0:1], None, ALU.mult))
                v_.scalar_tensor_tensor(sa, sb_, wsel[:, 1:2], sa, ALU.mult, ALU.add).then_inc(s_comb, 1)

            dve.wait_ge(s_dve, own.n)
            order(v_.tensor_reduce(pool8[:, :], pooled[:, :, :].rearrange("p t k -> p k t"), AX.X, ALU.add))
            v_.tensor_scalar(pool8[:, :], pool8[:, :], 1.0 / R, None, ALU.mult).then_inc(s_pool, 1)
            order(v_.memset(gate[:, :], -3.0e38))
            dve.wait_ge(s_gw, 16 * 4)
            dve.wait_ge(s_gmm, 2)
            order(v_.tensor_add(gate[:, 0:NE], bank(7, 1, NE), bgr[:, 0:NE]))
            order(v_.max(gate[:, 8:16], gate[:, 0:8]))
            order(v_.max_index(gidx[:, :], gate[:, 8:16], gate[:, 0:8]))
            order(v_.tensor_copy(gidxf[:, :], gidx[:, :]))
            v_.tensor_sub(gate[:, 32:33], gate[:, 9:10], gate[:, 8:9]).then_inc(s_pool, 1)
            dve.wait_ge(s_ghid, 2)
            order(v_.tensor_scalar(gate[:, 34:35], gate[:, 33:34], 1.0, None, ALU.add))
            order(v_.reciprocal(gate[:, 40:41], gate[:, 34:35]))
            order(v_.tensor_mul(gate[:, 41:42], gate[:, 33:34], gate[:, 40:41]))
            for e in range(2):
                order(v_.tensor_scalar(gate[:, 44 + 4 * e:48 + 4 * e], iot4[:, :], gidxf[:, e:e + 1],
                                       gate[:, 40 + e:41 + e], ALU.is_equal, ALU.mult))
            v_.tensor_add(gate[:, 52:56], gate[:, 44:48], gate[:, 48:52]).then_inc(s_pool, 1)
            dve.wait_ge(s_gmm, 3)
            order(v_.tensor_copy(w4[:, :], bank(6, NE, 128)))
            v_.tensor_copy(wsel[:, :], bank(7, 128, 2)).then_inc(s_gate, 1)
            dve.wait_ge(s_gate, 1)
            for kh in range(2):
                combine(0, kh, 0)
            for kh in range(2):
                dve.wait_ge(s_whi, 16 + kh + 1)
                v_.tensor_sub(Wl[0][:, 4 * kh:4 * kh + 4, :], wst2[:, kh, 0, :, :],
                              Wh[0][:, 4 * kh:4 * kh + 4, :].bitcast(f32)).then_inc(s_wready, 1)
            dve.wait_ge(s_gmm, 4)
            v_.tensor_copy(qkvb[:, :], bank(6, 128, 3 * KB)).then_inc(s_gate, 1)
            for a, ph in enumerate(("Q", "K")):
                def next_quarter(i, j):
                    if j % 6 in (1, 2):
                        combine(i * 2, j % 6 - 1, 4 * a + j // 6 + 1)
                lows(ph, 2, 12, lambda i, j: ot2[0][:, (N[ph] + j) % 4, 0:CH[j % 3][1]],
                     lambda i, j: ot2[1][:, (N[ph] + j) % 4, 0:CH[j % 3][1]].bitcast(f32r),
                     bias_of=lambda i, j: qkvb[:, ds(i * 4 + (KB * a + j // 3), 1)], cols=lambda j: CH[j % 3][1],
                     before=next_quarter, own=own, own_per=4)
            for q in range(4):
                for t in range(NT):
                    if t in (1, 2) and q < 3:
                        combine(0, t - 1, 8 + q + 1)
                    j = q * NT + t
                    slot = (N["V"] + j) % 4
                    dve.wait_ge(s_hi, HI["V"] + j + 1)
                    v_.tensor_sub(ot2[1][0:T, slot, 0:WQ].bitcast(f32r), bank(slot, T, WQ), ot2[0][0:T, slot, 0:WQ])\
                      .then_inc(s_done, 1)

            def maxima(i, m, first_bank=0):
                n = i * (HB * NT) + m
                dve.wait_ge(s_s, n + 1)
                v_.tensor_reduce(att_m[:, m % 2:m % 2 + 1], ps[0:T, 512 * first_bank:512 * first_bank + R], AX.X, ALU.max)\
                  .then_inc(s_mx, 1)
                dve.wait_ge(s_mx, n + 1)
                if m >= 2:
                    dve.wait_ge(s_mt, n - 1)
                order(v_.tensor_scalar(MB[:, m % 2, HD:HD + 1], att_m[:, m % 2:m % 2 + 1], -1.0, None, ALU.mult))
                v_.scalar_tensor_tensor(MB[:, m % 2, HD + 1:HD + 2], att_m[:, m % 2:m % 2 + 1], -1.0,
                                        MB[:, m % 2, HD:HD + 1].bitcast(f32), ALU.mult, ALU.subtract).then_inc(s_mb, 1)

            def output(i, k, part):
                h, cn = k // 3, CH[k % 3][1]
                rows = slice(HD * (h % 2), HD * (h % 2) + HD)
                if part == 0:
                    dve.wait_ge(s_pv, i * (HB * UN) + (NT * (k + 1) + 4))
                if part < 3:
                    a, b = cn * part // 3, cn * (part + 1) // 3
                    order(v_.reciprocal(RB[:, a:b], ps[HD:128, 2560 + 512 * (k % 2) + a:2560 + 512 * (k % 2) + b]))
                    return
                v_.tensor_mul(OB[k % 2][rows, 0:cn], bank(5 + k % 2, HD, cn), RB[:, 0:cn]).then_inc(s_ob, 1)

            def output_lo(i, k):
                h, (c0, cn) = k // 3, CH[k % 3]
                rows = slice(HD * (h % 2), HD * (h % 2) + HD)
                blk = i * (HB // 2) + h // 2
                dve.wait_ge(s_ao, i * (3 * HB) + (k + 1))
                v_.scalar_tensor_tensor(XTl[rows, ds(blk, 1), c0:c0 + cn].rearrange("p a n -> p (a n)"),
                                        OB[k % 2][rows, 0:cn], qkvb[rows, ds(blk + 2 * KB, 1)],
                                        XTh[rows, ds(blk, 1), c0:c0 + cn].rearrange("p a n -> p (a n)").bitcast(f32),
                                        ALU.add, ALU.subtract).then_inc(s_aol, 1)

            def outputs(i, n, first, last):
                for k, part in output_steps(n, first, last):
                    if part < 4:
                        output(i, k, part)
                    elif part == 5:
                        output_lo(i, k)

            def heads(i, first, last):
                for n in range(HB * UN):
                    h, q = n // UN, n % UN
                    cn = CH[q // NT][1]
                    last_head = last and h == HB - 1
                    if q in SCORES_AT and not last_head:
                        maxima(i, (h + 1) * NT + SCORES_AT.index(q))
                    if n % 2 == 0 or last_head:
                        dve.wait_ge(s_ex, i * (HB * UN) + (n + 1 + 2))
                        v_.tensor_sub(EL[n % 4][:, 0:cn], EX[n % 3][:, 0:cn], EH[n % 4][:, 0:cn].bitcast(f32))\
                          .then_inc(s_el[2 * (n % 2)], 1)
                    outputs(i, n, first, last)
                if last:
                    outputs(i, HB * UN, first, last)

            dve.wait_ge(s_fill, 1)
            for t in range(NT):
                maxima(0, t, 3 * (t % 2))
            heads(0, True, False)
            with dve.Fori(0, H // HB - 2) as i:
                own.enter(i, HB * (NT + 3 * 3))
                heads(dve.snap(i + 1), False, False)
            own.leave(H // HB - 2)
            heads(H // HB - 1, False, True)
            dve.wait_ge(s_bo, 16)
            with dve.Fori(0, 2) as i:
                own.enter(i, 2 * NT)
                for j in range(2 * NT):
                    slot, u, t = (N["O"] + j) % 4, j // NT, j % NT
                    dve.wait_ge(s_acc, i * (2 * NT) + (N["O"] + j + 1))
                    dve.wait_ge(s_x2r[slot], i * 80 + 16 * (j // 4 + 1))
                    dve.wait_ge(s_st[slot], i * 80 + (STORED["O"] + 16 * (j // 4)))
                    order(v_.tensor_add(ot[:, slot, :], bank(slot, T, WQ), x2r[:, slot, :]))
                    v_.tensor_add(ot[:, slot, :], ot[:, slot, :], boB[:, ds(i * 512 + u * WQ, WQ)]).then_inc(s_done, 1)
            own.leave(2)

        @block.tensor
        def _(pe):
            mm, tr = nc.tensor.matmul, nc.tensor.transpose
            pe.sem_inc(s_pv, 4)
            pe.sem_inc(s_ohfree, RING // GE)
            pe.wait_ge(s_const, 10)

            def three(dst_, ah, al, bh, bl, start, stop):
                mm(dst_, ah, bh, start=start, stop=False)
                mm(dst_, ah, bl, start=False, stop=False)
                return mm(dst_, al, bh, start=False, stop=stop)

            def wait_weights(i, ph, u):
                pe.wait_ge(s_wready, i * 4 + (2 * (WRDY[ph] + u + 1) + 2))

            def weights_stationary(ph, bh, bl, chunks, after=None):
                per = 4 * len(chunks)
                with pe.Fori(0, 2) as i:
                    for u in range(2):
                        wait_weights(i, ph, u)
                        for b in range(2):
                            for c, (c0, cn) in enumerate(chunks):
                                j = (2 * u + b) * len(chunks) + c
                                slot = (N[ph] + j) % 4
                                pe.wait_ge(s_done, i * per + (N[ph] + j + 1))
                                for k in range(KB):
                                    ins = three(bank(slot, 128, cn), Wh[u][:, k, b * 128:(b + 1) * 128],
                                                Wl[u][:, k, b * 128:(b + 1) * 128], bh[:, k, c0:c0 + cn],
                                                bl[:, k, c0:c0 + cn], k == 0, k == KB - 1)
                                ins.then_inc(s_acc, 1)
                                if after:
                                    after(i, j)

            def weights_moving(ph, ah, al, rows, count, after=None):
                per = 2 * count
                with pe.Fori(0, 2) as i:
                    for u in range(2):
                        wait_weights(i, ph, u)
                        for t in range(count):
                            j = u * count + t
                            slot = (N[ph] + j) % 4
                            pe.wait_ge(s_done, i * per + (N[ph] + j + 1))
                            for k in range(KB):
                                ins = three(bank(slot, rows, WQ), ah[:, k, t * rows:(t + 1) * rows],
                                            al[:, k, t * rows:(t + 1) * rows], Wh[u][:, k, :], Wl[u][:, k, :],
                                            k == 0, k == KB - 1)
                            ins.then_inc(s_acc, 1)
                            if after:
                                after(i, j)

            for a in range(2):
                pe.wait_ge(s_idx, a + 1)
                for e in range(GE):
                    ins = tr(bank(4 + a, T, NG, e * NG), ef[:, 4 + a, e * T:(e + 1) * T], ident[0:NG, 0:NG])
                ins.then_inc(s_idxT, 1)
            pe.wait_ge(s_idx, 4)
            for a in range(2):
                ins = tr(bank(6, NW, NG, a * NG), cond[:, 1 + a, :], ident[0:NG, 0:NG])
            ins.then_inc(s_idxT, 1)
            pe.wait_ge(s_idx, 6)
            for a in range(2):
                ins = tr(bank(7, 1, NW, a * NW), bnd[:, a:a + 1], ident[0:NW, 0:NW])
            ins.then_inc(s_idxT, 1)
            tot = pe.alloc_register("groups_pe")
            pe.reg_mov(tot, 0)

            def window(w, u):
                cnt = pe.value_load(bint[0:1, 1, ds(w, 1)], min_val=1, max_val=NG)
                before = pe.snap(tot, min_val=0, max_val=NW * NG)
                pe.wait_ge(s_winev, w + 1)
                acc = bank(4 + u, 128, KW)
                mm(acc, zw[:, :], iot[0:T, :], start=True, stop=False)
                with pe.Fori(0, cnt) as k:
                    r = pe.snap(((before + k) & (RING // GE - 1)) * GE, min_val=0, max_val=RING - GE)
                    pe.wait_ge(s_oh, (before + k) + 1)
                    ohs_, ohk_ = ohs[:, ds(r, GE), :], ohk[:, ds(r, GE), :]
                    for m in range(GE):
                        ins = mm(acc, ohs_[:, m, :], ohk_[:, m, :], start=False, stop=False)
                    ins.then_inc(s_ohfree, 1)
                mm(acc, zw[:, :], iot[0:T, :], start=False, stop=True).then_inc(s_win, 1)
                pe.reg_add(tot, tot, cnt)

            def transposes(src_, sem_):
                for b in range(2):
                    for k in range(4):
                        c0 = (4 * b + k) * 128
                        ins = tr(bank(4 + b, 128, T, k * T), src_[:, c0:c0 + 128], ident[0:T, 0:T])
                    ins.then_inc(sem_, 1)

            pe.wait_ge(s_bnd, 1)
            pe.wait_ge(s_proj, 17)
            for t in range(NT):
                if t < 8:
                    pe.wait_ge(s_wready, 2 * (t + 1) + 2)
                    for b in range(2):
                        j = 2 * t + b
                        pe.wait_ge(s_done, j + 1)
                        for k in range(KB):
                            ins = three(bank(j % 4, 128, PF_), Wh[t % 2][:, k, b * 128:(b + 1) * 128],
                                        Wl[t % 2][:, k, b * 128:(b + 1) * 128], prh[:, k, :], prl[:, k, :],
                                        k == 0, k == KB - 1)
                        ins.then_inc(s_acc, 1)
                pe.wait_ge(s_xn, t + 1)
                if t:
                    pe.wait_ge(s_Tlo, 2 * t)
                transposes(xn[:, t % 2, :], s_T)
            pe.wait_ge(s_done, 4 + N["GT"])
            pe.wait_ge(s_Tlo, 2 * NT)
            for t in range(1, NT + 2):
                if t <= NT:
                    m = t - 1
                    if m >= 2:
                        pe.wait_ge(s_elf, m - 1)
                    for k in range(KB):
                        ins = three(bank(6 + m % 2, T, PF_), XTh[:, k, m * T:t * T], XTl[:, k, m * T:t * T],
                                    Mkh[:, k, :], Mkl[:, k, :], k == 0, k == KB - 1)
                    ins.then_inc(s_kp, 1)
                if t >= 2:
                    m = t - 2
                    pe.wait_ge(s_ell, m + 1)
                    pe.wait_ge(s_xl, m + 1)
                    for k in range(KB):
                        dst_ = bank(k // 2, 128, PF_, PF_ * (k % 2))
                        ah, al = (a[m % 2][:, k * 128:(k + 1) * 128] for a in (xnh, xnl))
                        bh, bl = kph[:, m % 2, :], kpl[:, m % 2, :]
                        mm(dst_, ah, bh, start=m == 0 and k % 2 == 0, stop=False, skip_group_check=True)
                        mm(dst_, ah, bl, start=False, stop=False, skip_group_check=True)
                        ins = mm(dst_, al, bh, start=False, stop=m == NT - 1, skip_group_check=True)
                        if m == NT - 1 and k % 2:
                            ins.then_inc(s_acc, 1)
                            if k == KB - 1:
                                pe.wait_ge(s_acc, N["GT"] + 4)
                                pe.sem_inc(s_G, 1)
                    if m < NT - 1:
                        ins.then_inc(s_G, 1)
            for j in range(PB * 3):
                n_ = N["QP"] + j
                c0, cn = CH[j % 3]
                pb = j // 3
                pe.wait_ge(s_done, n_ + 1)
                for k in range(KB):
                    ins = three(bank(n_ % 4, 128, cn), Mqh[:, k, pb * 128:(pb + 1) * 128],
                                Mql[:, k, pb * 128:(pb + 1) * 128], XTh[:, k, c0:c0 + cn], XTl[:, k, c0:c0 + cn],
                                k == 0, k == KB - 1)
                ins.then_inc(s_acc, 1)
            wst_rows = Wst[:, :, :, :].rearrange("p a b c -> p (a b c)").rearrange("p (e n) -> p e n", e=2)
            pe.wait_ge(s_elf, NT)
            pe.wait_ge(s_Tlo, 2 * NT)
            for j in range(4):
                pe.wait_ge(s_wv, 16 * (j + 1))
                for b in range(4):
                    if j:
                        pe.wait_ge(s_wtlo, 4 * (j - 1) + b + 1)
                    for k in range(2):
                        for e in range(2):
                            c0 = (2 * b + k) * 128
                            ins = tr(bank(4 + b, 128, 128, k * WQ + e * 128), wst_rows[:, e, c0:c0 + 128], ident[:, :])
                    ins.then_inc(s_wt, 1)
                pe.wait_ge(s_wtlo, 4 * j + 4)
                for b in range(PB):
                    n_ = N["KV"] + PB * j + b
                    pe.wait_ge(s_done, n_ + 1)
                    for k in range(KB):
                        ins = three(bank(n_ % 4, 128, WQ), GTh[:, k, b * 128:(b + 1) * 128],
                                    GTl[:, k, b * 128:(b + 1) * 128], Wh[j % 2][:, k, :], Wl[j % 2][:, k, :],
                                    k == 0, k == KB - 1)
                    ins.then_inc(s_acc, 1)
            pe.wait_ge(s_ell, NT + PB * 3)
            pe.wait_ge(s_done, 4 + N["NUM"])
            for t in range(NT):
                rows = slice(t * T, (t + 1) * T)
                if t >= 2:
                    pe.wait_ge(s_done, 4 + N["NUM"] + 2 * (t - 2) + 1)
                for b in range(PB):
                    mm(bank(4 + t % 2, T, 2), qph[:, b, rows], onesr[:, :], start=b == 0, stop=False)
                    ins = mm(bank(4 + t % 2, T, 2), qpl[:, b, rows], onesr[:, :], start=False, stop=b == PB - 1)
                ins.then_inc(s_z, 1)
                for c in range(2):
                    n_ = N["NUM"] + 2 * t + c
                    pe.wait_ge(s_done, n_ + 1)
                    for b in range(PB):
                        ins = three(bank(n_ % 4, T, 512), qph[:, b, rows], qpl[:, b, rows],
                                    kvh[:, b, 512 * c:512 * c + 512], kvl[:, b, 512 * c:512 * c + 512],
                                    b == 0, b == PB - 1)
                    ins.then_inc(s_acc, 1)
            def y0_windows(i, j):
                if j in WIN_Y0:
                    k = WIN_Y0.index(j)
                    window(pe.snap(i * len(WIN_Y0) + k), k % 2)

            weights_moving("Y0", XTh, XTl, T, NT, after=y0_windows)
            def s0_windows(i, j):
                for k in WIN_S0[j]:
                    window(pe.snap(i * NS0 + (2 * len(WIN_Y0) + k)), k % 2)

            weights_stationary("S0", XTh, XTl, CH, after=s0_windows)
            pe.wait_ge(s_degp, 2 + 2 * NS0)
            for c, (c0, cn) in enumerate(CH):
                mm(bank((6, 7, 4)[c], 128, cn), ones[0:T, :], degp[:, c0:c0 + cn], start=True, stop=True)\
                    .then_inc(s_deg, 1)
            pe.wait_ge(s_slow, 1)
            slow_ = pe.value_load(slow[0:1, 0:1], min_val=0, max_val=1)

            def counts_product(dst_, ys, a, exact_first):
                n_s = len(ys)
                for s_i in range(n_s):
                    yh, yl, ad = ys[s_i]
                    for part, y_ in enumerate((yh, yl)):
                        y_, ad_ = (y_, ad) if exact_first else (y_.bitcast(f32), ad.bitcast(f32))
                        l_, r_ = (y_, ad_) if a else (ad_, y_)
                        ins = mm(dst_, l_, r_, start=s_i == 0 and part == 0, stop=s_i == n_s - 1 and part == 1)
                return ins


            def aggregate_cols(fast):
                for blk in range(KB):
                    for c, (c0, cn) in enumerate(CH):
                        m = 3 * blk + c
                        if c == 0:
                            pe.wait_ge(s_y0[blk % 2], 32 * (blk // 2 + 1))
                        pe.wait_ge(s_done, N["HT"] + m + 1)
                        ins = counts_product(bank((N["HT"] + m) % 4, 128, cn),
                                             [(y0sh[blk % 2][:, s, :], y0sl[blk % 2][:, s, :], adjr[:, s, c0:c0 + cn])
                                              for s in range(NT)], True, fast)
                        ins.then_inc(s_acc, 1)

            with pe.If(slow_ == 0):
                aggregate_cols(True)
            with pe.Else():
                aggregate_cols(False)
            pe.wait_ge(s_done, 4 + N["Y1"])
            weights_moving("Y1", XTh, XTl, T, NT)
            weights_moving("S1", XTh, XTl, T, NT)
            pe.wait_ge(s_done, 4 + N["S1"])

            def aggregate_rows(fast):
                for t in range(NT + 1):
                    if t < NT:
                        pe.wait_ge(s_at[t % 2], 16 * (t // 2 + 1))
                        for c in range(2):
                            n_ = N["X2"] + 2 * t + c
                            cols = slice(512 * c, 512 * c + 512)
                            pe.wait_ge(s_done, n_ + 1)
                            ins = counts_product(bank(n_ % 4, T, 512),
                                                 [(y1h[:, s, cols], y1l[:, s, cols], adt[t % 2][:, s, 0:T])
                                                  for s in range(NT)], False, fast)
                            ins.then_inc(s_acc, 1)
                    if t:
                        pe.wait_ge(s_x2n, t)
                        if t > 1:
                            pe.wait_ge(s_Tlo, 2 * (NT + t - 1))
                        transposes(x2n[:, (t - 1) % 2, :], s_T)

            with pe.If(slow_ == 0):
                aggregate_rows(True)
            with pe.Else():
                aggregate_rows(False)
            pe.wait_ge(s_pool, 1)
            pe.wait_ge(s_gw, 64)
            for k in range(KB):
                ins = mm(bank(6, 128, 1), wg1[:, k, :], pool8[:, k:k + 1], start=k == 0, stop=k == KB - 1)
            ins.then_inc(s_gmm, 1)
            pe.wait_ge(s_ghid, 1)
            mm(bank(7, 1, NE), hid[:, :], wg2[:, :], start=True, stop=True).then_inc(s_gmm, 1)
            pe.wait_ge(s_pool, 3)
            mm(bank(6, NE, 128), gate[:, 52:56], ones[0:1, :], start=True, stop=True)
            mm(bank(7, 128, 2), ones[0:1, :], gate[:, 40:42], start=True, stop=True).then_inc(s_gmm, 1)
            pe.wait_ge(s_gate, 1)
            pe.wait_ge(s_eb, 16 * 3)
            pe.wait_ge(s_Tlo, 4 * NT)
            for a in range(3):
                for k in range(KB):
                    ins = mm(bank(6, 128, 1, a * KB + k), b3[:, a, k * 128:(k + 1) * 128], w4[:, 0:1], start=True, stop=True)
            ins.then_inc(s_gmm, 1)
            pe.wait_ge(s_gate, 2)
            weights_stationary("Q", XTh, XTl, CH)
            weights_stationary("K", XTh, XTl, CH)
            weights_moving("V", XTh, XTl, T, NT)

            def query_scores(i, m, first_bank=0):
                n, t, k = i * (HB * NT) + m, m % NT, m // NT % HB
                if m:
                    if first_bank == 0 or m >= 2:
                        pe.wait_ge(s_mx, n if m >= NT else m - 1)
                if m == 0:
                    pe.wait_ge(s_qk_first, 96)
                elif t == 0:
                    pe.wait_ge(s_qk[k], i * 96 + 96 * (m // NT // HB + (1 if k else 0)))
                for c0, cn in SCH:
                    dst_ = ps[0:T, 512 * first_bank + c0:512 * first_bank + c0 + cn]
                    mm(dst_, QS[k][:, t * T:(t + 1) * T], KH[k][:, c0:c0 + cn], start=True, stop=False)
                    ins = mm(dst_, QS[k][0:HD, t * T:(t + 1) * T], KM[k][0:HD, c0:c0 + cn], start=False, stop=True)
                ins.then_inc(s_s, 1)

            def maxima_row(i, m):
                t = m % NT
                grp = [t in range(a, b) for a, b in MG].index(True)
                pe.wait_ge(s_mb, i * (HB * NT) + (m + 1))
                if t == MG[grp][0] and m:
                    pe.wait_ge(s_mr, i * (3 * HB) + (m // NT * 3 + grp))
                tr(bank(7, HD + 2, T, (t - MG[grp][0]) * T), MB[:, m % 2, :].bitcast(f32), ident[0:T, 0:T])\
                    .then_inc(s_mt, 1)

            def key_scores(i, n):
                k, q = n // UN, n % UN
                (c0, cn), j = CH[q // NT], q % NT
                keys = slice(j * T, (j + 1) * T)
                if q == 0:
                    pe.wait_ge(s_mr, i * (3 * HB) + 3 * (k + 1))
                pe.wait_ge(s_ex, i * (HB * UN) + (n + 1))
                mm(bank(3 + n % 2, T, cn), KH[k][:, keys], QS[k][:, c0:c0 + cn], start=True, stop=False)
                mm(bank(3 + n % 2, T, cn), KM[k][:, keys], QM[k][:, c0:c0 + cn], start=False, stop=True)\
                    .then_inc(s_sc, 1)

            def values(i, n, last):
                h, q = n // UN, n % UN
                cn, j = CH[q // NT][1], q % NT
                chunk = 3 * h + q // NT
                out_ = 5 + chunk % 2
                if q == 0:
                    pe.wait_ge(s_v[h % 2], i * (16 * HB) + 32 * (h // 2 + 1))
                if j == 0:
                    pe.wait_ge(s_ob, i * (3 * HB) + (chunk + 1))
                pe.wait_ge(s_eh, i * (HB * UN) + (n + 1))
                mm(bank(out_, 128, cn), VS[h % 2][:, j, :], EH[n % 4][:, 0:cn], start=j == 0, stop=False)
                mm(bank(out_, HD, cn), VL[h % 2][:, j, :], EH[n % 4][:, 0:cn], start=False, stop=False)
                if last and h == HB - 1 and n % 2:
                    pe.wait_ge(s_el[2], q // 2 + 1)
                else:
                    pe.wait_ge(s_el[n % 2], i * (HB * UN // 2) + (n // 2 + 1 + 2))
                mm(bank(out_, 128, cn), VS[h % 2][:, j, :], EL[n % 4][:, 0:cn], start=False, stop=j == NT - 1)\
                    .then_inc(s_pv, 1)

            def heads(i, first, last):
                for n in range(HB * UN + (LAG if last else 0)):
                    h, q = n // UN, n % UN
                    ahead = not (last and h == HB - 1) and n < HB * UN
                    if q in SCORES_AT and ahead:
                        query_scores(i, (h + 1) * NT + SCORES_AT.index(q))
                    if n < HB * UN:
                        key_scores(i, n)
                    if n >= LAG or not first:
                        values(i, n - LAG, last)
                    if q in ROWS_AT and ahead:
                        maxima_row(i, (h + 1) * NT + ROWS_AT.index(q))

            pe.wait_ge(s_done, 4 + N["O"])
            for t in range(NT):
                query_scores(0, t, 3 * (t % 2))
                if t:
                    maxima_row(0, t - 1)
            maxima_row(0, NT - 1)
            pe.wait_ge(s_fill, HB + 3)
            heads(0, True, False)
            with pe.Fori(0, H // HB - 2) as i:
                heads(pe.snap(i + 1), False, False)
            heads(H // HB - 1, False, True)
            pe.wait_ge(s_aol, 3 * H)
            weights_moving("O", XTh, XTl, T, NT)


_INS = ['x', 'src', 'dst', 'L0_gnn_W_self0', 'L0_gnn_W_neigh0', 'L0_gnn_b0', 'L0_gnn_W_self1', 'L0_gnn_W_neigh1',
        'L0_gnn_b1', 'L0_mix_Wq', 'L0_mix_Wk', 'L0_mix_Wv', 'L0_mix_proj', 'L0_ffn_Wq', 'L0_ffn_bq', 'L0_ffn_Wk',
        'L0_ffn_bk', 'L0_ffn_Wv', 'L0_ffn_bv', 'L0_ffn_Wg1', 'L0_ffn_bg1', 'L0_ffn_Wg2', 'L0_ffn_bg2', 'L0_ffn_Wo',
        'L0_ffn_bo']
_OUTS = [((1250, 1024), 'float32')]
_SCRATCH = [("adj", (1250, 1280)), ("base", (1250, 1024)), ("y0hi", (1250, 1024)), ("y0lo", (1250, 1024)),
            ("s0T", (1024, 1250)), ("x2d", (1250, 1024)),
            ("qhi", (1024, 1250)), ("qlo", (1024, 1250)), ("khi", (1024, 1250)), ("klo", (1024, 1250)), ("vhi", (1250, 1024)), ("vlo", (1250, 1024)),
            ("degrow", (1250,))]


def kernel(**inputs):
    import numpy as _np
    import concourse.bacc as _bacc
    from concourse import mybir as _mybir
    from concourse.bass_utils import run_bass_kernel_spmd as _run

    nc = _bacc.Bacc("TRN2", target_bir_lowering=False, num_devices=1)
    arrays, args = {}, []
    for name in _INS:
        a = _np.ascontiguousarray(inputs[name])
        arrays[f"in_{name}_dram"] = a
        args.append(nc.dram_tensor(f"in_{name}_dram", a.shape, _mybir.dt.from_np(a.dtype), kind="ExternalInput").ap())
    for i, (shape, dtype) in enumerate(_OUTS):
        dt = _mybir.dt.from_np(_np.dtype(dtype))
        args.append(nc.dram_tensor(f"out_{i}_dram", shape, dt, kind="ExternalOutput").ap())
    for name, shape in _SCRATCH:
        args.append(nc.dram_tensor(f"scratch_{name}", shape, _mybir.dt.float32, kind="Internal").ap())
    gps_layer_kernel(nc, *args)
    r = _run(nc, [arrays], core_ids=[0])
    got = tuple(r.results[0][f"out_{i}_dram"] for i in range(len(_OUTS)))
    return got[0]
```

```python
import concourse.bass as bass
from concourse import mybir
from contextlib import ExitStack


class Count:

    def __init__(self):
        self.n, self.turn, self.per = 0, None, 0

    def add(self):
        self.n += 1
        return self.n if self.turn is None else self.turn * self.per + self.n

    def enter(self, turn, per):
        self.turn, self.per, self.start = turn, per, self.n

    def leave(self, turns):
        assert self.n - self.start == self.per, (self.n - self.start, self.per)
        self.turn, self.n = None, self.start + self.per * turns


def gps_layer_kernel(nc, x, src, dst, W_self0, W_neigh0, b0, W_self1, W_neigh1, b1,
                     mWq, mWk, mWv, proj, fWq, fbq, fWk, fbk, fWv, fbv, Wg1, bg1, Wg2, bg2,
                     Wo, bo, out, adj, base, y0hi, y0lo, s0T, x2d, qhi, qlo, khi, klo, vhi, vlo,
                     degrow):
    f32, f32r = mybir.dt.float32, mybir.dt.float32r
    bf16, f16, i32 = mybir.dt.bfloat16, mybir.dt.float16, mybir.dt.int32
    u32 = mybir.dt.uint32
    ALU, ACT, AX = mybir.AluOpType, mybir.ActivationFunctionType, mybir.AxisListType
    ds = bass.ds

    R, D = x.shape
    T = 125
    NT = R // T
    KB = D // 128
    E = src.shape[0]
    ET = E // T
    GE = 4
    NG = ET // GE
    RING = 4 * GE
    PF_ = proj.shape[1]
    PB = PF_ // 128
    DW = 32
    NW = -(-R // DW)
    AW = NW * DW
    KW = NT * DW
    NE = fWq.shape[0]
    H, HD = 16, 64
    WQ = 256
    CH = [(0, 418), (418, 416), (834, 416)]
    CM = CH[0][1]
    HB = 4
    UN = 3 * NT
    LAG = 3
    SCORES_AT = [3 * t for t in range(NT)]
    ROWS_AT = [min(q + 3, UN - 1) for q in SCORES_AT]
    OUT_AT = [(4, 5, 7, 8, 10, 11), (4, 6, 7, 9, 10, 12), (5, 6, 8, 9, 10, 12)]
    OUT_STEPS = [(NT * (k + 1) - 1 + d, k, part) for k in range(3 * HB) for part, d in enumerate(OUT_AT[k % 3])]

    def output_steps(n, first, last):
        steps = [(k, part) for at_, k, part in OUT_STEPS if at_ == n or (last and n == HB * UN and at_ > n)]
        return steps + [(k - 3 * HB, part) for at_, k, part in OUT_STEPS if at_ - HB * UN == n and not first
                        and n < HB * UN]

    MG = [(0, 4), (4, 8), (8, NT)]
    SCH = [(0, 512), (512, 512), (1024, R - 1024)]
    SCALE = 0.125
    FAST_MAX = 4096.0
    assert NT % 2 == 0 and R == NT * T and E == ET * T and ET == NG * GE and NW % 2 == 0

    ctx = ExitStack()
    with ctx:
        def sb(name, shape, dt=f32):
            return ctx.enter_context(nc.sbuf_tensor(name, shape, dt))

        def sem(name):
            return ctx.enter_context(nc.semaphore(name))

        ident = sb("ident", [128, 128])
        ones = sb("ones", [128, 128])
        onesr = sb("onesr", [128, 2], f32r)
        b0c = sb("b0c", [128, KB])
        deginv = sb("deginv", [T, NT])
        degmax = sb("degmax", [1, 2])
        slow = sb("slow", [1, 1], i32)
        bnparts = sb("bnparts", [T, 2, 2, 6])
        roots = sb("roots", [T, 8, 2])
        stat = sb("stat", [T, NT, 3])
        zcol = sb("zcol", [T, 2])
        qkvb = sb("qkvb", [128, 3 * KB])
        pooled = sb("pooled", [128, NT, KB])
        pool8 = sb("pool8", [128, KB])
        gate = sb("gate", [1, 64])
        gidx = sb("gidx", [1, 8], u32)
        gidxf = sb("gidxf", [1, 8])
        hid = sb("hid", [128, 1])
        wsel = sb("wsel", [128, 2])
        w4 = sb("w4", [NE, 128])
        iot4 = sb("iot4", [1, NE])
        att_m = sb("att_m", [T, 2])

        ARENA = 208160
        D0 = 203136
        base_at = nc.sbuf_base
        base_at += -base_at % 32
        arena = sb("arena", [128, ARENA // 4])

        def at(name, shape, dt, offset):
            return nc.alloc_sbuf_tensor_at(name, shape, dt, offset=base_at + offset)

        XTh = at("XTh", [128, KB, R], f32r, 0)
        XTl = at("XTl", [128, KB, R], f32r, 40000)
        W0 = 80000
        o = W0
        Wst = at("Wst", [128, 2, KB // 2, WQ], f32, o)
        o += 8192
        Wh = [at(f"Wh{i}", [128, KB, WQ], f32r, o + 8192 * i) for i in range(2)]
        Wl = [at(f"Wl{i}", [128, KB, WQ], f32r, o + 16384 + 8192 * i) for i in range(2)]
        o += 32768
        G0 = o
        raw = at("raw", [NG, 2, GE * T], i32, D0)
        iotw = at("iotw", [128, NW], f32, D0 + 4000)
        pcol = at("pcol", [128, 2], f32, D0 + 4160)
        gmm = at("gmm", [NG, 2], f32, D0 + 4192)
        bnd = at("bnd", [NW, 2], f32, D0 + 4224)
        ef = at("ef", [NG, 6, GE * T], f32, W0 + 8192)
        dhi_i = at("dhi_i", [NG, GE * T], i32, W0 + 20192)
        cond = at("cond", [NG, 3, NW], f32, W0 + 22208)
        brow = at("brow", [1, 4, NW], f32, W0 + 22688)
        K0 = G0 + 77088
        slo = at("slo", [T, ET], f32, K0)
        key = at("key", [T, ET], f32, K0 + 1280)
        iot = at("iot", [128, KW], f16, K0 + 2560)
        tk = at("tk", [128, NW], f32, K0 + 3200)
        zw = at("zw", [T, 128], bf16, K0 + 3360)
        bint = at("bint", [1, 2, NW], i32, K0 + 3616)
        adjr = at("adjr", [T, NT, AW], f32r, G0)
        ohs = at("ohs", [T, RING, 128], bf16, G0 + 61984)
        ohk = at("ohk", [T, RING, KW], bf16, G0 + 61984 + 256 * RING)
        degp = at("degp", [T, R], f32, D0)
        Mqh = at("Mqh", [128, KB, PF_], f32r, G0)
        Mql = at("Mql", [128, KB, PF_], f32r, G0 + 8192)
        Mkh = at("Mkh", [128, KB, PF_], f32r, G0 + 16384)
        Mkl = at("Mkl", [128, KB, PF_], f32r, G0 + 24576)
        L = G0 + 32768
        prh = at("prh", [128, KB, PF_], f32r, L)
        prl = at("prl", [128, KB, PF_], f32r, L + 8192)
        prf = at("prf", [128, KB, PF_], f32, L + 16384)
        Wst1 = at("Wst1", [128, 2, KB // 2, WQ], f32, L + 16384)
        xs = at("xs", [T, 2, D], f32, L + 24576)
        xn = at("xn", [T, 2, D], f32, L + 32768)
        xnh = [at(f"xnh{i}", [T, D], f32r, L + 4096 * i) for i in range(2)]
        xnl = [at(f"xnl{i}", [T, D], f32r, L + 8192 + 4096 * i) for i in range(2)]
        kph = at("kph", [T, 2, PF_], f32r, L + 16384)
        kpl = at("kpl", [T, 2, PF_], f32r, L + 18432)
        qph = at("qph", [128, PB, R], f32r, L)
        qpl = at("qpl", [128, PB, R], f32r, L + 10016)
        elm = at("elm", [128, 2, CM], f32, L + 20480)
        elf = at("elf", [128, 2, CM], f32, L + 40960)
        GTh = at("GTh", [128, KB, PF_], f32r, L + 24576)
        GTl = at("GTl", [128, KB, PF_], f32r, L + 32768)
        kvh = at("kvh", [128, PB, D], f32r, G0 + 16384)
        kvl = at("kvl", [128, PB, D], f32r, G0 + 24576)
        xr = at("xr", [T, 3, D], f32, G0)
        bt2 = at("bt2", [T, 4, 512], f32, G0 + 53248)
        b1B = at("b1B", [T, D], f32, G0 + 12288)
        y0t = [at(f"y0t{c}", [T, 4, WQ], f32, G0 + 51200 + 4096 * c) for c in range(2)]
        s0t = at("s0t", [128, 4, CM], f32, G0 + 51200)
        ot2 = [at(f"ot2{c}", [128, 4, CM], f32, G0 + 16384 + 6720 * c) for c in range(2)]
        y0sh = [at(f"y0sh{i}", [T, NT, 128], f32r, G0 + 51200 + 10240 * i) for i in range(2)]
        y0sl = [at(f"y0sl{i}", [T, NT, 128], f32r, G0 + 56320 + 10240 * i) for i in range(2)]
        s0c = at("s0c", [128, 2, CM], f32, G0 + 71744)
        zt = at("zt", [128, 2, CM], f32, G0 + 75104)
        deginvB = at("deginvB", [128, R], f32, D0)
        y1l = at("y1l", [T, NT, D], f32r, G0)
        bs = at("bs", [T, 4, WQ], f32, D0)
        adt = [at(f"adt{i}", [T, NT, 128], f32r, W0 + 5120 * i) for i in range(2)]
        b2 = at("b2", [T, 2, D], f32, W0 + 10240)
        x2s = at("x2s", [T, 2, D], f32, W0 + 18432)
        x2n = at("x2n", [T, 2, D], f32, W0 + 26624)
        V0 = G0 + 40960
        y1h = at("y1h", [T, NT, D], f32r, V0)
        wg1 = at("wg1", [128, KB, 128], f32, W0 + 34816)
        wg2 = at("wg2", [128, NE], f32, W0 + 38912)
        bgr = at("bgr", [1, 8], f32, W0 + 38944)
        bg1c = at("bg1c", [128, 1], f32, W0 + 38976)
        wst2 = at("wst2", [128, 2, 2, KB // 2, WQ], f32, G0)
        b3 = at("b3", [NE, 3, D], f32, V0)
        place = [[G0 + 5024 * b for b in (6, 7, 0, 1)]] + [[W0 + 5024 * (4 * k + b) for b in range(4)] for k in range(2)]
        place += [[G0 + 5024 * b for b in (2, 3, 4, 5)]]
        KH = [at(f"KH{i}", [128, R], f32r, place[i][0]) for i in range(HB)]
        QS = [at(f"QS{i}", [128, R], f32r, place[i][1]) for i in range(HB)]
        KM = [at(f"KM{i}", [HD + 2, R], f32r, place[i][2]) for i in range(HB)]
        QM = [at(f"QM{i}", [HD + 2, R], f32r, place[i][3]) for i in range(HB)]
        VS = [at(f"VS{i}", [T, NT, 2 * HD], f32r, V0 + 5120 * i) for i in range(2)]
        VL = [at(f"VL{i}", [T, NT, HD], f32r, V0 + 10240 + 2560 * i) for i in range(2)]
        EX = [at(f"EX{i}", [T, CM], f32, V0 + 15360 + 1696 * i) for i in range(3)]
        EH = [at(f"EH{i}", [T, CM], f32r, V0 + 20448 + 1696 * i) for i in range(4)]
        EL = [at(f"EL{i}", [T, CM], f32r, V0 + 27232 + 1696 * i) for i in range(4)]
        RB = at("RB", [HD, CM], f32, V0 + 34016)
        OB = [at(f"OB{i}", [128, CM], f32, V0 + 35712 + 1696 * i) for i in range(2)]
        MB = at("MB", [T, 2, HD + 2], f32r, V0 + 39104)
        x2r = at("x2r", [T, 4, WQ], f32, V0)
        ot = at("ot", [T, 4, WQ], f32, V0 + 4096)
        boB = at("boB", [T, D], f32, V0 + 8192)

        ps = ctx.enter_context(nc.psum_tensor("ps", [128, 8 * 512], f32))

        def bank(i, p=128, n=512, c=0):
            return ps[0:p, 512 * i + c:512 * i + c + n]

        names = ["Mq", "Mk", "GT", "QP", "KV", "NUM", "Y0", "S0", "HT", "Y1", "S1", "X2", "Q", "K", "V", "O"]
        tiles = [KB, KB, 4, PB * 3, 4 * PB, 2 * NT, 4 * NT, 3 * KB, 3 * KB, 4 * NT, 4 * NT, 2 * NT, 3 * KB, 3 * KB,
                 4 * NT, 4 * NT]
        split = {"Mq", "Mk", "GT", "KV", "Y0", "Y1", "Q", "K", "V"}
        N, HI, STORED = {}, {}, {}
        n = h = 0
        st = 16
        for name, m in zip(names, tiles):
            N[name], HI[name], STORED[name] = n, h, st
            n += m
            h += m if name in split else 0
            if name in ("S0", "S1", "O"):
                st += 16 * (m // 4)
            if name in ("Y0", "Q", "K", "V"):
                st += 32 * (m // 4)
        ST_END = st
        ORDER = ["Mq", "Mk", "KV", "Y0", "S0", "Y1", "S1", "Q", "K", "V", "O"]
        SIZE = dict(zip(names, tiles))

        def slot_free(ph, u, i):
            k = ORDER.index(ph)
            before = 0 if k == 0 else N[ORDER[k - 1]] + SIZE[ORDER[k - 1]] * (3 + u) // 4
            same = N[ph] + SIZE[ph] * (1 + u) // 4
            if isinstance(i, int):
                return (before, same)[i]
            return i * (same - before) + before
        WIN_Y0 = list(range(2, 2 * NT, 3))
        NS0 = NW // 2 - len(WIN_Y0)
        WIN_S0 = [list(range(j * NS0 // 12, (j + 1) * NS0 // 12)) for j in range(12)]
        assert len(WIN_Y0) % 2 == 0 and NS0 % 2 == 0
        WRDY = {k: 4 * i for i, k in enumerate(["Mq", "Mk", "Y0", "S0", "Y1", "S1", "Q", "K", "V", "O"])}

        s_const = sem("s_const")
        s_edges = sem("s_edges")
        s_small = sem("s_small")
        s_passed = sem("s_passed")
        s_gw = sem("s_gw")
        s_eb = sem("s_eb")
        s_w = [sem(f"s_w{k}") for k in range(2)]
        s_wm = [sem(f"s_wm{k}") for k in range(4)]
        s_we = [sem(f"s_we{k}") for k in range(2)]
        s_wv = sem("s_wv")
        s_gp = sem("s_gp")
        s_whi = sem("s_whi")
        s_comb = sem("s_comb")
        s_wready = sem("s_wready")
        s_acc = sem("s_acc")
        s_hi = sem("s_hi")
        s_done = sem("s_done")
        s_st = [sem(f"s_st{k}") for k in range(4)]
        s_dve = sem("s_dve")
        s_proj = sem("s_proj")
        s_idx = sem("s_idx")
        s_idxT = sem("s_idxT")
        s_bnd = sem("s_bnd")
        s_oh = sem("s_oh")
        s_ohfree = sem("s_ohfree")
        s_win = sem("s_win")
        s_winev = sem("s_winev")
        s_degp = sem("s_degp")
        s_deg = sem("s_deg")
        s_slow = sem("s_slow")
        s_dinv = sem("s_dinv")
        s_adj = sem("s_adj")
        s_row = sem("s_row")
        s_x = [sem(f"s_x{k}") for k in range(2)]
        s_xn = sem("s_xn")
        s_xg = sem("s_xg")
        s_xh = sem("s_xh")
        s_xl = sem("s_xl")
        s_T = sem("s_T")
        s_Thi = sem("s_Thi")
        s_Tlo = sem("s_Tlo")
        s_kp = sem("s_kp")
        s_G = sem("s_G")
        s_elm = sem("s_elm")
        s_ele = sem("s_ele")
        s_elf = sem("s_elf")
        s_elh = sem("s_elh")
        s_ell = sem("s_ell")
        s_wt = sem("s_wt")
        s_wthi = sem("s_wthi")
        s_wtlo = sem("s_wtlo")
        s_z = sem("s_z")
        s_xr = [sem(f"s_xr{k}") for k in range(3)]
        s_bt = [sem(f"s_bt{k}") for k in range(4)]
        s_b1 = sem("s_b1")
        s_y0 = [sem(f"s_y0{k}") for k in range(2)]
        s_s0 = [sem(f"s_s0{k}") for k in range(2)]
        s_zt = sem("s_zt")
        s_hh = sem("s_hh")
        s_bs = [sem(f"s_bs{k}") for k in range(4)]
        s_at = [sem(f"s_at{k}") for k in range(2)]
        s_b2 = [sem(f"s_b2{k}") for k in range(2)]
        s_x2 = [sem(f"s_x2{k}") for k in range(2)]
        s_x2n = sem("s_x2n")
        s_pool = sem("s_pool")
        s_gmm = sem("s_gmm")
        s_ghid = sem("s_ghid")
        s_top = sem("s_top")
        s_gate = sem("s_gate")
        s_we_first = [sem(f"s_we_first{k}") for k in range(2)]
        s_qk = [sem(f"s_qk{k}") for k in range(HB)]
        s_qk_first = sem("s_qk_first")
        s_v = [sem(f"s_v{k}") for k in range(2)]
        s_fill = sem("s_fill")
        s_s = sem("s_s")
        s_mx = sem("s_mx")
        s_mb = sem("s_mb")
        s_mt = sem("s_mt")
        s_mr = sem("s_mr")
        s_sc = sem("s_sc")
        s_eh = sem("s_eh")
        s_ex = sem("s_ex")
        s_el = [sem("s_el0"), sem("s_el1"), sem("s_el2")]
        s_pv = sem("s_pv")
        s_ob = sem("s_ob")
        s_ao = sem("s_ao")
        s_aol = sem("s_aol")
        s_x2r = [sem(f"s_x2r{k}") for k in range(4)]
        s_bo = sem("s_bo")

        block = ctx.enter_context(nc.Block())

        xt = x.rearrange("(t p) c -> t p c", p=T)

        def wait_apart(eng, sem_, value):
            eng.wait_ge(sem_, value)
            if not isinstance(value, int):
                eng.sem_inc(s_passed, 1)

        def load_qk(eng, h):
            k, rows = h % HB, slice(h * HD, (h + 1) * HD)
            for d_, a_ in ((KH[k][0:HD], khi), (KH[k][HD:128], khi), (QS[k][0:HD], qhi), (QS[k][HD:128], qlo),
                           (KM[k][0:HD], klo), (QM[k][0:HD], qhi)):
                eng.dma_start(d_.bitcast(f32), a_[rows, :]).then_inc(s_qk[k] if h else s_qk_first, 16)

        def low_written(i, n, last):
            if n % 3 == 2:
                return s_el[0], i * (HB * UN // 3) + (n // 3 + 1 + 1)
            if last and n // UN == HB - 1:
                q = n % UN
                return s_el[2], 2 * (q // 3) + q % 3 + 1
            return s_el[1], i * (2 * HB * UN // 3) + (2 * (n // 3) + n % 3 + 1 + 2)

        @block.sync
        def _(sp):
            for k in range(4):
                sp.sem_inc(s_st[k], 16)
            sp.dma_start(prf[:, :, :], proj.rearrange("(k p) n -> p k n", p=128)).then_inc(s_proj, 16)
            with nc.allow_non_contiguous_dma(reason="one small column layout"):
                sp.dma_start(b0c[:, :], b0.rearrange("(k p) -> p k", p=128)).then_inc(s_small, 16)
            for t in range(2 * NT):
                if t >= 2:
                    sp.wait_ge(s_xn if t < NT + 2 else s_xg, t - 1 if t < NT + 2 else t - 1 - NT)
                sp.dma_start(xs[:, t % 2, :], xt[t % NT, :, :]).then_inc(s_x[t % 2], 16)
                if t == 1:
                    sp.dma_start(raw[:, 0, :], src.rearrange("(p e) -> p e", p=NG)).then_inc(s_edges, 16)
                    sp.dma_start(raw[:, 1, :], dst.rearrange("(p e) -> p e", p=NG)).then_inc(s_edges, 16)
            sp.wait_ge(s_acc, N["KV"])
            sp.dma_start(b1B[:, :], b1.partition_broadcast(T)).then_inc(s_b1, 16)
            for t in range(NT + 1):
                if t < NT:
                    if t >= 3:
                        sp.wait_ge(s_done, 4 + N["NUM"] + 2 * (t - 2))
                    sp.dma_start(xr[:, t % 3, :], xt[t, :, :]).then_inc(s_xr[t % 3], 16)
                if t >= 1:
                    for c in range(2):
                        sp.wait_ge(s_done, 4 + N["NUM"] + 2 * (t - 1) + c + 1)
                        sp.dma_start(base[(t - 1) * T:t * T, 512 * c:512 * c + 512], bt2[:, (t - 1) % 2 * 2 + c, :])\
                          .then_inc(s_bt[(t - 1) % 2 * 2 + c], 16)
            def store_cols(ph, outs, tb):
                with sp.Fori(0, 2) as i:
                    for j in range(12):
                        u, b, c = j // 6, j // 3 % 2, j % 3
                        c0, cn = CH[c]
                        slot = (N[ph] + j) % 4
                        sp.wait_ge(s_done, i * 12 + (4 + N[ph] + j + 1))
                        for o_, t_ in zip(outs, tb):
                            dst_ = o_[ds(i * 512 + (2 * u + b) * 128, 128), c0:c0 + cn]
                            sp.dma_start(dst_, t_[:, slot, 0:cn]).then_inc(s_st[slot], 16)

            def store_rows(ph, outs, tb):
                with sp.Fori(0, 2) as i:
                    for j in range(2 * NT):
                        u, t = j // NT, j % NT
                        slot = (N[ph] + j) % 4
                        sp.wait_ge(s_done, i * (2 * NT) + (4 + N[ph] + j + 1))
                        for o_, t_ in zip(outs, tb):
                            sp.dma_start(o_[t * T:(t + 1) * T, ds(i * 512 + u * WQ, WQ)], t_[0:T, slot, 0:WQ])\
                              .then_inc(s_st[slot], 16)

            def stored(ph_next):
                for k in range(4):
                    sp.wait_ge(s_st[k], STORED[ph_next])

            store_rows("Y0", [y0hi, y0lo], y0t)
            store_cols("S0", [s0T], [s0t])
            stored("HT")
            y0v = [a.rearrange("(s p) c -> p s c", p=T) for a in (y0hi, y0lo)]

            def load_y0(blk):
                for a_, d_ in zip(y0v, (y0sh, y0sl)):
                    sp.dma_start(d_[blk % 2][:, :, :].bitcast(f32), a_[:, :, blk * 128:(blk + 1) * 128])\
                      .then_inc(s_y0[blk % 2], 16)

            load_y0(0)
            sp.wait_ge(s_deg, len(CH))
            load_y0(1)
            for blk in range(KB):
                for c, (c0, cn) in enumerate(CH):
                    m = 3 * blk + c
                    if m >= 2:
                        sp.wait_ge(s_zt, m - 1)
                    sp.dma_start(s0c[:, m % 2, 0:cn], s0T[blk * 128:(blk + 1) * 128, c0:c0 + cn])\
                      .then_inc(s_s0[m % 2], 16)
                    if c == 0 and 1 <= blk < KB - 1:
                        sp.wait_ge(s_acc, N["HT"] + 3 * blk)
                        load_y0(blk + 1)
                    if c != 1 and 2 <= blk < 2 + NT // 2:
                        b = 2 * (blk - 2) + c // 2
                        sp.dma_start(adj.rearrange("(b p) d -> p b d", p=T)[:, b:b + 1, :],
                                     adjr[:, b:b + 1, :].bitcast(f32)).then_inc(s_adj, 16)
                    if m == 5:
                        sp.wait_ge(s_dinv, 3)
                        sp.dma_start(degrow.rearrange("(a n) -> a n", a=1), deginvB[0:1, :]).then_inc(s_row, 16)
                        sp.wait_ge(s_row, 16)
                        with nc.allow_non_contiguous_dma(reason="one small column layout"):
                            sp.dma_start(deginv[:, :], degrow.rearrange("(t p) -> p t", p=T)).then_inc(s_row, 16)
            store_rows("S1", [base], [bs])
            stored("X2")
            sp.wait_ge(s_acc, N["X2"])
            sp.wait_ge(s_adj, 16 * NT)
            adv = adj.rearrange("(b p) d -> p b d", p=T)
            for t in range(NT + 1):
                if t < NT:
                    if t >= 2:
                        sp.wait_ge(s_acc, N["X2"] + 2 * (t - 1))
                        sp.dma_start(adt[t % 2][:, :, :].bitcast(f32), adv[:, :, t * T:t * T + 128])\
                          .then_inc(s_at[t % 2], 16)
                    if t >= 2:
                        sp.wait_ge(s_done, 4 + N["X2"] + 2 * (t - 1))
                    sp.dma_start(b2[:, t % 2, :], base[t * T:(t + 1) * T, :]).then_inc(s_b2[t % 2], 16)
                if t >= 1:
                    sp.wait_ge(s_done, 4 + N["X2"] + 2 * t)
                    sp.dma_start(x2d[(t - 1) * T:t * T, :], x2s[:, (t - 1) % 2, :]).then_inc(s_x2[(t - 1) % 2], 16)
                if t == 0:
                    sp.dma_start(wg1[:, :, :], Wg1.rearrange("(k p) n -> p k n", p=128)).then_inc(s_gw, 16)
                    sp.dma_start(wg2[:, :], Wg2).then_inc(s_gw, 16)
                    sp.dma_start(bgr[:, 0:NE], bg2.rearrange("(a n) -> a n", a=1)).then_inc(s_gw, 16)
                    with nc.allow_non_contiguous_dma(reason="one small column layout"):
                        sp.dma_start(bg1c[:, :], bg1.rearrange("(p a) -> p a", a=1)).then_inc(s_gw, 16)
            sp.wait_ge(s_acc, N["Q"])
            for k_, b_ in enumerate((fbq, fbk, fbv)):
                sp.dma_start(b3[:, k_, :], b_).then_inc(s_eb, 16)
            store_cols("Q", [qhi, qlo], ot2)
            store_cols("K", [khi, klo], ot2)
            store_rows("V", [vhi, vlo], ot2)
            stored("V")

            def load_v(h):
                k, cols = h % 2, slice(h * HD, (h + 1) * HD)
                for d_, a_ in ((VS[k][:, :, 0:HD], vhi), (VL[k][:, :, :], vlo)):
                    sp.dma_start(d_.bitcast(f32), a_.rearrange("(s p) c -> p s c", p=T)[:, :, cols])\
                      .then_inc(s_v[k], 16)

            sp.wait_ge(s_acc, N["O"])
            load_qk(sp, 1)
            load_qk(sp, 2)
            stored("O")
            load_v(0)
            load_v(1)
            load_qk(sp, 3)
            for h in range(1, H - 1):
                sp.wait_ge(s_pv, 4 + UN * h)
                load_v(h + 1)
                if h + 3 < H:
                    load_qk(sp, h + 3)
            sp.wait_ge(s_pv, 4 + H * UN)
            sp.dma_start(boB[:, :], bo.partition_broadcast(T)).then_inc(s_bo, 16)
            store_rows("O", [out], [ot])
            for k in range(4):
                sp.wait_ge(s_st[k], ST_END)
            sp.wait_ge(s_x2[0], 16 * (NT // 2))
            sp.wait_ge(s_x2[1], 16 * (NT // 2))

        @block.gpsimd
        def _(g):
            g.sem_inc(s_wready, 2)
            g.sem_inc(s_el[1], 2)
            g.memset(ident[:, :], 0.0).then_inc(s_gp, 1)
            g.memset(ones[:, :], 1.0).then_inc(s_const, 1)
            g.wait_ge(s_gp, 1)
            g.affine_select(out=ident[:, :], in_=ident[:, :], compare_op=ALU.not_equal, fill=1.0,
                            base=0, pattern=[[-1, 128]], channel_multiplier=1).then_inc(s_const, 1)
            imp = dict(allow_small_or_imprecise_dtypes=True)
            g.iota(iot[:, :], pattern=[[1, KW]], base=0, channel_multiplier=0, **imp).then_inc(s_const, 1)
            g.iota(tk[:, :], pattern=[[KW, NW]], base=0, channel_multiplier=0, **imp).then_inc(s_const, 1)
            g.iota(iotw[:, :], pattern=[[1, NW]], base=0, channel_multiplier=0, **imp).then_inc(s_const, 1)
            g.iota(iot4[:, :], pattern=[[1, NE]], base=0, channel_multiplier=0, **imp).then_inc(s_const, 1)
            g.iota(pcol[:, 0:1], pattern=[[0, 1]], base=NG, channel_multiplier=-1, **imp).then_inc(s_const, 1)
            g.iota(pcol[:, 1:2], pattern=[[0, 1]], base=1, channel_multiplier=1, **imp).then_inc(s_const, 1)

            gp = [1]

            def split_half(w, u, kh, hi_value):
                g.tensor_copy(Wh[u][:, 4 * kh:4 * kh + 4, :], w).then_inc(s_gp, 1)
                g.wait_ge(s_gp, hi_value)
                g.tensor_sub(Wl[u][:, 4 * kh:4 * kh + 4, :], w, Wh[u][:, 4 * kh:4 * kh + 4, :].bitcast(f32))\
                 .then_inc(s_wready, 1)

            def cols_(i, u):
                c0 = i * 512 + u * WQ
                return slice(c0, c0 + WQ) if isinstance(i, int) else ds(c0, WQ)

            def quarters(ph, w, loads):
                wv = w.rearrange("(k p) n -> p k n", p=128)
                with g.Fori(0, 2) as i:
                    for u in range(2):
                        g.wait_ge(s_wready, i * 4 + (2 * (WRDY[ph] + u) + 2))
                        for kh in range(2):
                            g.dma_start(Wst[:, kh, :, :], wv[:, 4 * kh:4 * kh + 4, cols_(i, u)])\
                             .then_inc(s_w[kh], 16)
                        for kh in range(2):
                            wait_apart(g, s_w[kh], i * 32 + 16 * (loads + u + 1))
                            if kh == 0:
                                wait_apart(g, s_acc, slot_free(ph, u, i))
                            split_half(Wst[:, kh, :, :], u, kh, i * 4 + (gp[0] + 2 * u + kh + 1))
                gp[0] += 8

            for q in range(8):
                for kh in range(2):
                    g.wait_ge(s_whi, 2 * q + kh + 1)
                    g.tensor_sub(Wl[q % 2][:, 4 * kh:4 * kh + 4, :], (Wst, Wst1)[q % 2][:, kh, :, :],
                                 Wh[q % 2][:, 4 * kh:4 * kh + 4, :].bitcast(f32)).then_inc(s_wready, 1)
            for t in range(NT):
                g.wait_ge(s_xh, t + 1)
                if t >= 2:
                    g.wait_ge(s_G, t - 1)
                g.tensor_sub(xnl[t % 2][:, :], xn[:, t % 2, :], xnh[t % 2][:, :].bitcast(f32)).then_inc(s_xl, 1)
            wst_rows = Wst[:, :, :, :].rearrange("p a b c -> p (a b c)").rearrange("p (e n) -> p e n", e=2)
            g.wait_ge(s_wready, 2 * WRDY["Y0"] + 2)
            for j in range(4):
                if j:
                    g.wait_ge(s_wt, 4 * j)
                g.dma_start(wst_rows, mWv[j * WQ:(j + 1) * WQ, :].rearrange("(e p) n -> p e n", p=128))\
                 .then_inc(s_wv, 16)
            g.wait_ge(s_wt, 16)
            quarters("Y0", W_neigh0, 0)
            quarters("S0", W_self0, 4)
            quarters("Y1", W_neigh1, 8)
            quarters("S1", W_self1, 12)
            g.wait_ge(s_top, 1)
            e1 = g.value_load(gidx[0:1, 0:1], min_val=0, max_val=NE - 1)
            e2 = g.value_load(gidx[0:1, 1:2], min_val=0, max_val=NE - 1)

            def expert_load(q, kh):
                wv = (fWq, fWk, fWv)[q // 4].rearrange("e (k p) n -> p e k n", p=128)
                for a, e in enumerate((e1, e2)):
                    g.dma_start(wst2[:, kh, a, :, :], wv[:, ds(e, 1), 4 * kh:4 * kh + 4, q % 4 * WQ:(q % 4 + 1) * WQ]
                                .rearrange("p e k n -> p (e k) n")).then_inc(s_we[kh], 16)

            for kh in range(2):
                g.wait_ge(s_wready, 2 * WRDY["Q"] + 2 + kh + 1)
                expert_load(1, kh)
            for q in range(1, 12):
                for kh in range(2):
                    g.wait_ge(s_comb, 2 * q + kh + 1)
                    if kh == 0:
                        g.wait_ge(s_acc, slot_free("QKV"[q // 4], q % 2, q % 4 // 2))
                    gp[0] += 1
                    split_half(wst2[:, kh, 0, :, :], q % 2, kh, gp[0])
                    if q < 11:
                        g.wait_ge(s_wready, 2 * WRDY["Q"] + 2 + 2 * q + kh + 1)
                        expert_load(q + 1, kh)
            g.wait_ge(s_wready, 2 * WRDY["V"] + 2 + 8)
            for k in range(4):
                g.wait_ge(s_st[k], STORED["V"])
            load_qk(g, 0)
            fills = [(MB[:, :, 0:HD], 0.0), (VS[0][:, :, HD:2 * HD], 1.0), (VS[1][:, :, HD:2 * HD], 1.0)]
            fills += [(KM[k][HD:HD + 2, :], 1.0) for k in range(HB)]
            for n, (a, value) in enumerate(fills):
                if n == 4:
                    g.wait_ge(s_acc, N["O"])
                if n == 6:
                    for k in range(4):
                        g.wait_ge(s_st[k], STORED["O"])
                g.memset(a.bitcast(f32), value).then_inc(s_fill, 1)
                g.wait_ge(s_fill, n + 1)

            def exp_lows(i, hh):
                for q in range(UN):
                    n = hh * UN + q
                    if q % 3 < 2:
                        cn = CH[q // NT][1]
                        wait_apart(g, s_ex, i * (HB * UN) + (n + 1 + 2))
                        g.tensor_sub(EL[n % 4][:, 0:cn], EX[n % 3][:, 0:cn], EH[n % 4][:, 0:cn].bitcast(f32))\
                         .then_inc(s_el[1], 1)

            with g.Fori(0, H // HB - 1) as i:
                for hh in range(HB):
                    exp_lows(i, hh)
            for hh in range(HB - 1):
                exp_lows(H // HB - 1, hh)
            g.wait_ge(s_pv, 4 + UN * (H - 1))
            quarters("O", Wo, 16)

        @block.scalar
        def _(act):
            act.sem_inc(s_winev, 2)
            act.sem_inc(s_ex, 2)
            def highs(ph, loops, per, dst_of, bias_of=None, p=128, cols=None, uses=0, after=None):
                with act.Fori(0, loops) as i:
                    for j in range(per):
                        slot = (N[ph] + j) % 4
                        n_ = cols(j)
                        wait_apart(act, s_acc, i * per + (N[ph] + j + 1))
                        if uses:
                            wait_apart(act, s_st[slot], i * (uses * per // 4) + (STORED[ph] + uses * (j // 4)))
                        b_ = bias_of(i, j) if bias_of else 0.0
                        act.activation(dst_of(i, j).bitcast(f32r) if uses else dst_of(i, j), bank(slot, p, n_),
                                       ACT.Identity if bias_of else ACT.Copy, bias=b_).then_inc(s_hi, 1)
                        if after:
                            after(i, j)

            def window_out(w, u):
                wait_apart(act, s_win, w + 1)
                act.copy(adjr[:, :, ds(w * DW, DW)].bitcast(f32),
                         bank(4 + u, T, KW).rearrange("p (b d) -> p b d", d=DW)).then_inc(s_winev, 1)

            def transposed_hi(t, m):
                for b in range(2):
                    act.wait_ge(s_T, m(b))
                    act.copy(XTh[:, 4 * b:4 * b + 4, t], bank(4 + b, 128, 4 * T).rearrange("p (k n) -> p k n", n=T))\
                       .then_inc(s_Thi, 1)

            def feature_exp(m, p, n_):
                act.wait_ge(s_elm, m + 1)
                act.activation(elm[0:p, m % 2, 0:n_], elm[0:p, m % 2, 0:n_], ACT.Exp).then_inc(s_ele, 1)

            def mix_load(q, kh):
                wv = (mWq, mWk)[q // 4].rearrange("(k p) n -> p k n", p=128)
                act.dma_start((Wst, Wst1)[q % 2][:, kh, :, :],
                              wv[:, 4 * kh:4 * kh + 4, q % 4 * WQ:(q % 4 + 1) * WQ]).then_inc(s_wm[q % 2 * 2 + kh], 16)

            def weights_hi(q):
                for kh in range(2):
                    if 1 <= q < 7:
                        act.wait_ge(s_wready, 2 + 2 * (q - 1) + kh + 1)
                        mix_load(q + 1, kh)
                    act.wait_ge(s_wm[q % 2 * 2 + kh], 16 * (q // 2 + 1))
                    if kh == 0 and q >= 2:
                        act.wait_ge(s_acc, 2 * (q - 1))
                    act.copy(Wh[q % 2][:, 4 * kh:4 * kh + 4, :], (Wst, Wst1)[q % 2][:, kh, :, :]).then_inc(s_whi, 1)
                if q == 0:
                    act.wait_ge(s_proj, 17)
                    for half in range(2):
                        mix_load(1, half)

            for half in range(2):
                mix_load(0, half)
            weights_hi(0)
            weights_hi(1)
            for t in range(NT):
                if t < 8:
                    for j in range(2 * t, 2 * t + 2):
                        act.wait_ge(s_acc, j + 1)
                        act.copy((Mqh, Mkh)[j // 8][:, j % 8, :], bank(j % 4, 128, PF_)).then_inc(s_hi, 1)
                transposed_hi(slice(t * T, (t + 1) * T), lambda b: 2 * t + b + 1)
                if t + 2 < 8:
                    weights_hi(t + 2)
            act.wait_ge(s_wready, 2 + 16)
            for t in range(NT + 1):
                if t < NT:
                    act.wait_ge(s_xg, t + 1)
                    if t >= 2:
                        act.wait_ge(s_G, t - 1)
                    act.copy(xnh[t % 2][:, :], xn[:, t % 2, :]).then_inc(s_xh, 1)
                if t >= 1:
                    m = t - 1
                    feature_exp(m, T, PF_)
                    act.wait_ge(s_elf, m + 1)
                    if m >= 2:
                        act.wait_ge(s_G, m - 1)
                    act.copy(kph[:, m % 2, :], elf[0:T, m % 2, 0:PF_]).then_inc(s_elh, 1)
            act.wait_ge(s_acc, N["GT"] + 4)
            for j in range(4):
                act.copy(GTh[:, 2 * j:2 * j + 2, :].rearrange("p a n -> p (a n)"), bank(j)).then_inc(s_hi, 1)
            for j in range(PB * 3):
                c0, cn = CH[j % 3]
                feature_exp(NT + j, 128, cn)
                act.wait_ge(s_elf, NT + j + 1)
                act.copy(qph[:, j // 3, c0:c0 + cn], elf[:, (NT + j) % 2, 0:cn]).then_inc(s_elh, 1)
            for j in range(4):
                for b in range(4):
                    act.wait_ge(s_wt, 4 * j + b + 1)
                    if b == 0:
                        act.wait_ge(s_acc, slot_free("KV", j % 2, j // 2))
                    act.copy(Wh[j % 2][:, 2 * b:2 * b + 2, :].rearrange("p a n -> p (a n)"), bank(4 + b))\
                       .then_inc(s_wthi, 1)
                for b in range(PB):
                    m = PB * j + b
                    act.wait_ge(s_acc, N["KV"] + m + 1)
                    act.copy(kvh[:, b, j * WQ:(j + 1) * WQ], bank((N["KV"] + m) % 4, 128, WQ)).then_inc(s_hi, 1)
            for k in range(4):
                act.wait_ge(s_bt[k], 16 * (NT // 2))

            def y0_windows(i, j):
                if j in WIN_Y0:
                    k = WIN_Y0.index(j)
                    window_out(act.snap(i * len(WIN_Y0) + k), k % 2)

            highs("Y0", 2, 2 * NT, lambda i, j: y0t[0][0:T, (N["Y0"] + j) % 4, 0:WQ], p=T, cols=lambda j: WQ, uses=32,
                  after=y0_windows)
            act.wait_ge(s_done, 4 + N["S0"])
            for k in range(4):
                act.wait_ge(s_st[k], STORED["S0"])
            with act.Fori(0, 2) as i:
                for j in range(12):
                    slot, cn = (N["S0"] + j) % 4, CH[j % 3][1]
                    wait_apart(act, s_acc, i * 12 + (N["S0"] + j + 1))
                    wait_apart(act, s_st[slot], i * 48 + (STORED["S0"] + 16 * (j // 4)))
                    act.copy(s0t[:, slot, 0:cn], bank(slot, 128, cn)).then_inc(s_done, 1)
                    for k in WIN_S0[j]:
                        window_out(act.snap(i * NS0 + (2 * len(WIN_Y0) + k)), k % 2)
            for m in range(3 * KB):
                c0, cn = CH[m % 3]
                act.wait_ge(s_zt, m + 1)
                act.copy(XTh[:, m // 3, c0:c0 + cn], zt[:, m % 2, 0:cn]).then_inc(s_hh, 1)
            act.wait_ge(s_adj, 16 * NT)
            highs("Y1", 2, 2 * NT, lambda i, j: y1h[:, j % NT, ds(i * 512 + j // NT * WQ, WQ)], p=T, cols=lambda j: WQ)
            act.wait_ge(s_row, 32)
            with act.Fori(0, 2) as i:
                for j in range(2 * NT):
                    slot, u, t = (N["S1"] + j) % 4, j // NT, j % NT
                    act.wait_ge(s_st[slot], i * 80 + (STORED["S1"] + 16 * (j // 4)))
                    act.dma_start(bs[:, slot, :], base[t * T:(t + 1) * T, ds(i * 512 + u * WQ, WQ)])\
                       .then_inc(s_bs[slot], 16)

            act.wait_ge(s_wready, 2 * (WRDY["S1"] + 4) + 2)
            act.wait_ge(s_acc, N["S1"] + 3 * NT)
            adv = adj.rearrange("(b p) d -> p b d", p=T)
            for t in range(2):
                act.dma_start(adt[t][:, :, :].bitcast(f32), adv[:, :, t * T:t * T + 128]).then_inc(s_at[t], 16)
            for t in range(NT):
                transposed_hi(slice(t * T, (t + 1) * T), lambda b: 2 * (NT + t) + b + 1)
            act.wait_ge(s_gmm, 1)
            act.wait_ge(s_gw, 16 * 4)
            act.activation(hid[:, :], bank(6, 128, 1), ACT.Relu, bias=bg1c[:, 0:1]).then_inc(s_ghid, 1)
            act.wait_ge(s_pool, 2)
            act.activation(gate[:, 33:34], gate[:, 32:33], ACT.Exp).then_inc(s_ghid, 1)
            act.wait_ge(s_top, 1)
            wv = fWq.rearrange("e (k p) n -> p e k n", p=128)
            chosen = [act.value_load(gidx[0:1, a:a + 1], min_val=0, max_val=NE - 1) for a in range(2)]
            for kh in range(2):
                for a, e in enumerate(chosen):
                    act.dma_start(wst2[:, kh, a, :, :], wv[:, ds(e, 1), 4 * kh:4 * kh + 4, 0:WQ]
                                  .rearrange("p e k n -> p (e k) n")).then_inc(s_we_first[kh], 16)
            for k in range(2):
                act.wait_ge(s_x2[k], 16 * (NT // 2))
            for kh in range(2):
                act.wait_ge(s_comb, kh + 1)
                act.copy(Wh[0][:, 4 * kh:4 * kh + 4, :], wst2[:, kh, 0, :, :]).then_inc(s_whi, 1)
            for a, ph in enumerate(("Q", "K")):
                highs(ph, 2, 12, lambda i, j: ot2[0][:, (N[ph] + j) % 4, 0:CH[j % 3][1]],
                      bias_of=lambda i, j: qkvb[:, ds(i * 4 + (KB * a + j // 3), 1)], cols=lambda j: CH[j % 3][1], uses=32)

            highs("V", 2, 2 * NT, lambda i, j: ot2[0][0:T, (N["V"] + j) % 4, 0:WQ], p=T, cols=lambda j: WQ, uses=32)

            def maxima_rows(i, h1, grp):
                t0, t1 = MG[grp]
                act.wait_ge(s_mt, i * (HB * NT) + (h1 * NT + t1))
                act.copy(QM[h1 % HB][HD:HD + 2, t0 * T:t1 * T], ps[HD:HD + 2, 3584:3584 + (t1 - t0) * T])\
                   .then_inc(s_mr, 1)

            def output_hi(i, k):
                h, (c0, cn) = k // 3, CH[k % 3]
                rows = slice(HD * (h % 2), HD * (h % 2) + HD)
                blk = i * (HB // 2) + h // 2
                act.wait_ge(s_ob, i * (3 * HB) + (k + 1 + 2))
                act.activation(XTh[rows, ds(blk, 1), c0:c0 + cn].rearrange("p a n -> p (a n)"), OB[k % 2][rows, 0:cn],
                               ACT.Identity, bias=qkvb[rows, ds(blk + 2 * KB, 1)]).then_inc(s_ao, 1)

            def heads(i, first, last):
                for n in range(HB * UN):
                    h, q = n // UN, n % UN
                    c, j = q // NT, q % NT
                    cn = CH[c][1]
                    for grp in range(3):
                        if q == min(ROWS_AT[MG[grp][1] - 1] + 1, UN - 1) and not (last and h == HB - 1):
                            maxima_rows(i, h + 1, grp)
                    src_ = bank(3 + n % 2, T, cn)
                    wait_apart(act, s_sc, i * (HB * UN) + (n + 1))
                    act.wait_ge(s_pv, i * (HB * UN) + (n + 1))
                    act.activation(EH[n % 4][:, 0:cn], src_, ACT.Exp, scale=SCALE).then_inc(s_eh, 1)
                    act.wait_ge(*low_written(i, n - 3, last))
                    act.activation(EX[n % 3][:, 0:cn], src_, ACT.Exp, scale=SCALE).then_inc(s_ex, 1)
                    for k, part in output_steps(n, first, last):
                        if part == 4:
                            output_hi(i, k)
                if last:
                    for k, part in output_steps(HB * UN, first, last):
                        if part == 4:
                            output_hi(i, k)

            for grp in range(3):
                maxima_rows(0, 0, grp)
            heads(0, True, False)
            with act.Fori(0, H // HB - 2) as i:
                heads(act.snap(i + 1), False, False)
            heads(H // HB - 1, False, True)
            with act.Fori(0, 2) as i:
                for j in range(2 * NT):
                    slot, u, t = (N["O"] + j) % 4, j // NT, j % NT
                    act.wait_ge(s_done, i * (2 * NT) + (N["O"] + j + 1))
                    act.dma_start(x2r[:, slot, :], x2d[t * T:(t + 1) * T, ds(i * 512 + u * WQ, WQ)])\
                       .then_inc(s_x2r[slot], 16)

        @block.vector
        def _(dve):
            v_ = nc.vector
            dve.sem_inc(s_done, 4)
            dve.sem_inc(s_el[0], 1)
            dve.sem_inc(s_ob, 2)
            own = Count()

            def tick(ins):
                ins.then_inc(s_dve, 1)
                return own.add()

            def order(ins):
                dve.wait_ge(s_dve, tick(ins))

            def flat(a):
                return a.rearrange("p a n -> p (a n)")

            v_.memset(zw[:, :], 0.0).then_inc(s_const, 1)
            dve.wait_ge(s_const, 9)
            v_.tensor_copy(onesr[:, :], ones[:, 0:2]).then_inc(s_const, 1)
            dve.wait_ge(s_proj, 16)
            order(v_.tensor_copy(prh[:, :, :], prf[:, :, :]))
            v_.tensor_sub(prl[:, :, :], prf[:, :, :], prh[:, :, :].bitcast(f32)).then_inc(s_proj, 1)

            tot = dve.alloc_register("groups_dve")
            dve.reg_mov(tot, 0)
            at_tile = dve.alloc_register("first_tile_dve")

            def window_onehots(w):
                lo = dve.value_load(bint[0:1, 0, ds(w, 1)], min_val=0, max_val=NG - 1)
                cnt = dve.value_load(bint[0:1, 1, ds(w, 1)], min_val=1, max_val=NG)
                before = dve.snap(tot, min_val=0, max_val=NW * NG)
                dve.reg_mov(at_tile, lo * GE)
                tk_ = tk[0:T, ds(w, 1)]
                with dve.Fori(0, cnt) as k:
                    col = dve.snap(at_tile, min_val=0, max_val=ET - GE)
                    r = dve.snap(((before + k) & (RING // GE - 1)) * GE, min_val=0, max_val=RING - GE)
                    dve.wait_ge(s_ohfree, (before + k) + 1)
                    ohs_, ohk_ = ohs[:, ds(r, GE), :], ohk[:, ds(r, GE), :]
                    slo_, key_ = slo[:, ds(col, GE)], key[:, ds(col, GE)]
                    v_.tensor_tensor(ohs_, iot[0:T, 0:128].unsqueeze(1).to_broadcast([T, GE, 128]),
                                     slo_.unsqueeze(2).to_broadcast([T, GE, 128]), ALU.is_equal)
                    for m in range(GE):
                        ins = v_.tensor_scalar(ohk_[:, m, :], iot[0:T, :], tk_, key_[:, m:m + 1], ALU.add, ALU.is_equal)
                    ins.then_inc(s_oh, 1)
                    dve.reg_add(at_tile, at_tile, GE)
                dve.reg_add(tot, tot, cnt)

            def lows(ph, loops, per, hi_of, lo_of, bias_of=None, p=128, cols=None, before=None, own=None,
                     own_per=0):
                with dve.Fori(0, loops) as i:
                    if own:
                        own.enter(i, own_per)
                    for j in range(per):
                        if before:
                            before(i, j)
                        slot = (N[ph] + j) % 4
                        dve.wait_ge(s_hi, i * per + (HI[ph] + j + 1))
                        a = bank(slot, p, cols(j))
                        if bias_of:
                            ins = v_.scalar_tensor_tensor(lo_of(i, j), a, bias_of(i, j), hi_of(i, j), ALU.add, ALU.subtract)
                        else:
                            ins = v_.tensor_sub(lo_of(i, j), a, hi_of(i, j))
                        ins.then_inc(s_done, 1)
                if own:
                    own.leave(loops)

            def tile_stats(t, src_, k=0):
                for c in range(2):
                    last = tick(v_.bn_stats(bnparts[:, k, c, :], src_[:, 512 * c:512 * c + 512]))
                dve.wait_ge(s_dve, last)
                order(v_.bn_aggr(stat[:, t, 0:2], flat(bnparts[:, k, :, :])))

            def inverse_roots(t, n):
                var, rstd = (flat(stat[:, t:t + n, k:k + 1]) for k in (1, 2))
                bits, asf, est, half, sq, prod, new0, new1 = (roots[:, k, 0:n] for k in range(8))
                order(v_.tensor_scalar(var, var, 1e-5, None, ALU.add))
                tick(v_.tensor_scalar(half, var, -0.5, None, ALU.mult))
                order(v_.tensor_scalar(bits.bitcast(i32), var.bitcast(i32), 1, None, ALU.logical_shift_right))
                order(v_.tensor_copy(asf, bits.bitcast(i32)))
                order(v_.tensor_scalar(est.bitcast(i32), asf, -1.0, float(0x5F3759DF), ALU.mult, ALU.add))
                for new in (new0, new1, rstd):
                    order(v_.tensor_mul(sq, est, est))
                    order(v_.tensor_mul(prod, sq, half))
                    order(v_.scalar_tensor_tensor(new, prod, 1.5, est, ALU.add, ALU.mult))
                    est = new

            def normalise(t, src_, dst_, done):
                v_.tensor_scalar(dst_, src_, stat[:, t, 0:1], stat[:, t, 2:3], ALU.subtract, ALU.mult).then_inc(done, 1)

            def transposed_lo(t, m, sums=None, parts=(True, True)):
                for b in range(2):
                    a = bank(4 + b, 128, 4 * T).rearrange("p (k n) -> p k n", n=T)
                    if parts[0]:
                        dve.wait_ge(s_Thi, m(b))
                    if sums is not None and parts[0]:
                        tick(v_.tensor_reduce(pooled[:, sums, 4 * b:4 * b + 4], a, AX.X, ALU.add))
                    if parts[1]:
                        v_.tensor_sub(XTl[:, 4 * b:4 * b + 4, t], a, XTh[:, 4 * b:4 * b + 4, t].bitcast(f32))\
                          .then_inc(s_Tlo, 1)

            def feature(m, a, p, n_, full, hi_, lo_):
                s = m % 2
                dve.wait_ge(*full)
                v_.tensor_scalar(elm[0:p, s, 0:n_], a, 0.0, None, ALU.min).then_inc(s_elm, 1)
                dve.wait_ge(s_ele, m + 1)
                ins = v_.scalar_tensor_tensor(elf[0:p, s, 0:n_], a, 0.0, elm[0:p, s, 0:n_], ALU.max, ALU.add)
                ins.then_inc(s_elf, 1)
                dve.wait_ge(s_elh, m + 1)
                v_.tensor_sub(lo_, elf[0:p, s, 0:n_], hi_.bitcast(f32)).then_inc(s_ell, 1)

            def x_stats(t):
                dve.wait_ge(s_x[t % 2], 16 * (t // 2 + 1))
                tile_stats(t, xs[:, t % 2, :], t % 2)

            def x_normal(t):
                if t >= 2:
                    dve.wait_ge(s_T, 2 * (t - 1))
                normalise(t, xs[:, t % 2, :], xn[:, t % 2, :], s_xn)

            def m_lows(j0):
                for j in range(j0, j0 + 2):
                    mh, ml = ((Mqh, Mql), (Mkh, Mkl))[j // 8]
                    dve.wait_ge(s_hi, j + 1)
                    v_.tensor_sub(ml[:, j % 8, :], bank(j % 4, 128, PF_), mh[:, j % 8, :].bitcast(f32))\
                      .then_inc(s_done, 1)

            for t in range(2):
                x_stats(t)
            inverse_roots(0, 2)
            for t in range(2):
                x_normal(t)
            for t in range(NT):
                if t < 8:
                    m_lows(2 * t)
                transposed_lo(slice(t * T, (t + 1) * T), lambda b: 2 * t + b + 1)
                if t + 2 < NT:
                    if t % 2 == 0:
                        x_stats(t + 2)
                        x_stats(t + 3)
                        inverse_roots(t + 2, 2)
                    x_normal(t + 2)
            sf, df, hf, bf_, slf, kf = (ef[:, k, :] for k in range(6))

            def edges(t):
                if t == 0:
                    dve.wait_ge(s_edges, 32)
                    tick(v_.tensor_copy(sf, raw[:, 0, :]))
                    tick(v_.tensor_copy(df, raw[:, 1, :]))
                    order(v_.tensor_scalar(dhi_i[:, :], raw[:, 1, :], 5, None, ALU.logical_shift_right))
                    tick(v_.tensor_copy(hf, dhi_i[:, :]))
                    order(v_.tensor_scalar(bf_, sf, float(T), None, ALU.is_ge))
                elif t < NT - 1:
                    order(v_.scalar_tensor_tensor(bf_, sf, float(T * (t + 1)), bf_, ALU.is_ge, ALU.add))
                elif t == NT - 1:
                    v_.scalar_tensor_tensor(slf, bf_, -float(T), sf, ALU.mult, ALU.add).then_inc(s_idx, 1)
                    order(v_.scalar_tensor_tensor(kf, bf_, float(DW), df, ALU.mult, ALU.add))
                    v_.scalar_tensor_tensor(kf, hf, float(KW - DW), kf, ALU.mult, ALU.add).then_inc(s_idx, 1)
                else:
                    order(v_.tensor_reduce(gmm[:, 0:1], hf, AX.X, ALU.min))
                    order(v_.tensor_reduce(gmm[:, 1:2], hf, AX.X, ALU.max))
                    order(v_.tensor_scalar(cond[:, 0, :], iotw[0:NG, :], gmm[:, 0:1], None, ALU.is_ge))
                    order(v_.scalar_tensor_tensor(cond[:, 0, :], iotw[0:NG, :], gmm[:, 1:2], cond[:, 0, :],
                                                  ALU.is_le, ALU.mult))
                    for a in range(2):
                        v_.tensor_scalar(cond[:, 1 + a, :], cond[:, 0, :], pcol[0:NG, a:a + 1], None, ALU.mult)\
                          .then_inc(s_idx, 1)

            def edge_bounds():
                dve.wait_ge(s_idxT, 1)
                tick(v_.tensor_copy(slo[:, :].rearrange("e (p g) -> e g p", g=GE),
                                    bank(4, T, ET).rearrange("e (g p) -> e g p", g=GE)))
                dve.wait_ge(s_idxT, 2)
                tick(v_.tensor_copy(key[:, :].rearrange("e (p g) -> e g p", g=GE),
                                    bank(5, T, ET).rearrange("e (g p) -> e g p", g=GE)))
                dve.wait_ge(s_idxT, 3)
                for a in range(2):
                    v_.tensor_reduce(bnd[:, a:a + 1], bank(6, NW, NG, a * NG), AX.X, ALU.max).then_inc(s_idx, 1)

            def window_bounds():
                dve.wait_ge(s_idxT, 4)
                order(v_.tensor_scalar(brow[:, 0, :], bank(7, 1, NW), -1.0, float(NG), ALU.mult, ALU.add))
                order(v_.tensor_sub(brow[:, 1, :], bank(7, 1, NW, NW), brow[:, 0, :]))
                order(v_.tensor_scalar(brow[:, 2, :], brow[:, 0, :], float(NG - 1), None, ALU.min))
                order(v_.tensor_scalar(brow[:, 3, :], brow[:, 1, :], 1.0, None, ALU.max))
                v_.tensor_copy(bint[:, :, :], brow[:, 2:4, :]).then_inc(s_bnd, 1)

            for t in range(NT + 1):
                if t < NT:
                    dve.wait_ge(s_x[t % 2], 16 * ((NT + t) // 2 + 1))
                    if t < 2:
                        dve.wait_ge(s_T, 2 * NT)
                    else:
                        dve.wait_ge(s_xl, t - 1)
                    v_.tensor_scalar(xn[:, t % 2, :], xs[:, t % 2, :], stat[:, t, 0:1], stat[:, t, 2:3],
                                     ALU.subtract, ALU.mult).then_inc(s_xg, 1)
                if t >= 1:
                    m = t - 1
                    feature(m, bank(6 + m % 2, T, PF_), T, PF_, (s_kp, m + 1), kph[:, m % 2, :], kpl[:, m % 2, :])
                edges(t)
            for j in range(4):
                dve.wait_ge(s_hi, HI["GT"] + j + 1)
                v_.tensor_sub(flat(GTl[:, 2 * j:2 * j + 2, :]), bank(j), flat(GTh[:, 2 * j:2 * j + 2, :]).bitcast(f32))\
                  .then_inc(s_done, 1)
            for j in range(PB * 3):
                c0, cn = CH[j % 3]
                feature(NT + j, bank((N["QP"] + j) % 4, 128, cn), 128, cn, (s_acc, N["QP"] + j + 1),
                        qph[:, j // 3, c0:c0 + cn], qpl[:, j // 3, c0:c0 + cn])
                dve.wait_ge(s_elf, NT + j + 1)
                dve.sem_inc(s_done, 1)
                if j == 1:
                    edge_bounds()
                if j == 3:
                    window_bounds()
            for j in range(4):
                for b in range(4):
                    dve.wait_ge(s_wthi, 4 * j + b + 1)
                    v_.tensor_sub(flat(Wl[j % 2][:, 2 * b:2 * b + 2, :]), bank(4 + b),
                                  flat(Wh[j % 2][:, 2 * b:2 * b + 2, :]).bitcast(f32)).then_inc(s_wtlo, 1)
                for b in range(PB):
                    m = PB * j + b
                    dve.wait_ge(s_hi, HI["KV"] + m + 1)
                    v_.tensor_sub(kvl[:, b, j * WQ:(j + 1) * WQ], bank((N["KV"] + m) % 4, 128, WQ),
                                  kvh[:, b, j * WQ:(j + 1) * WQ].bitcast(f32)).then_inc(s_done, 1)
            dve.wait_ge(s_b1, 16)
            for t in range(NT):
                dve.wait_ge(s_xr[t % 3], 16 * (t // 3 + 1))
                order(v_.tensor_add(xr[:, t % 3, :], xr[:, t % 3, :], b1B[:, :]))
                dve.wait_ge(s_z, t + 1)
                order(v_.tensor_scalar(zcol[:, 0:1], bank(4 + t % 2, T, 1), 1e-8, None, ALU.add))
                order(v_.reciprocal(zcol[:, 1:2], zcol[:, 0:1]))
                for c in range(2):
                    m = N["NUM"] + 2 * t + c
                    dve.wait_ge(s_acc, m + 1)
                    if t >= 2:
                        dve.wait_ge(s_bt[t % 2 * 2 + c], 16 * (t // 2))
                    v_.scalar_tensor_tensor(bt2[:, t % 2 * 2 + c, :], bank(m % 4, T, 512), zcol[:, 1:2],
                                            xr[:, t % 3, 512 * c:512 * c + 512], ALU.mult, ALU.add).then_inc(s_done, 1)
            def y0_windows(i, j):
                if j + 2 in WIN_Y0:
                    window_onehots(dve.snap(i * len(WIN_Y0) + WIN_Y0.index(j + 2)))

            lows("Y0", 2, 2 * NT, lambda i, j: y0t[0][0:T, (N["Y0"] + j) % 4, 0:WQ],
                 lambda i, j: y0t[1][0:T, (N["Y0"] + j) % 4, 0:WQ].bitcast(f32r), p=T, cols=lambda j: WQ,
                 before=y0_windows)
            def column_sums(c0, n_):
                v_.tensor_reduce(degp[:, ds(c0, n_)], adjr[:, :, ds(c0, n_)].bitcast(f32).rearrange("p b d -> p d b"),
                                 AX.X, ALU.add).then_inc(s_degp, 1)

            dve.wait_ge(s_winev, 2 + 2 * len(WIN_Y0) - 1)
            column_sums(0, DW * (2 * len(WIN_Y0) - 1))
            with dve.Fori(0, 2) as i:
                for k in range(NS0):
                    w = dve.snap(i * NS0 + (2 * len(WIN_Y0) + k))
                    window_onehots(w)
                    dve.wait_ge(s_winev, i * NS0 + (2 + 2 * len(WIN_Y0) + k))
                    column_sums(dve.snap(i * (NS0 * DW) + (2 * len(WIN_Y0) + k - 1) * DW), DW)
            dve.wait_ge(s_winev, 2 + NW)
            column_sums((NW - 1) * DW, R - (NW - 1) * DW)
            for c, (c0, cn) in enumerate(CH):
                dve.wait_ge(s_deg, c + 1)
                v_.tensor_scalar(deginvB[:, c0:c0 + cn], bank((6, 7, 4)[c], 128, cn), 1.0, None, ALU.max)\
                  .then_inc(s_dve, 1)
                last = own.add()
            dve.wait_ge(s_dve, last)
            order(v_.tensor_reduce(degmax[:, 0:1], deginvB[0:1, :], AX.X, ALU.max))
            order(v_.tensor_scalar(degmax[:, 1:2], degmax[:, 0:1], FAST_MAX, None, ALU.is_gt))
            v_.tensor_copy(slow[:, :], degmax[:, 1:2]).then_inc(s_slow, 1)
            for c0, cn in CH:
                v_.reciprocal(deginvB[:, c0:c0 + cn], deginvB[:, c0:c0 + cn]).then_inc(s_dinv, 1)
            for m in range(3 * KB):
                c0, cn = CH[m % 3]
                z = zt[:, m % 2, 0:cn]
                if m < 3:
                    dve.wait_ge(s_dinv, m + 1)
                dve.wait_ge(s_acc, N["HT"] + m + 1)
                order(v_.tensor_mul(z, bank((N["HT"] + m) % 4, 128, cn), deginvB[:, c0:c0 + cn]))
                dve.wait_ge(s_s0[m % 2], 16 * (m // 2 + 1))
                order(v_.tensor_add(z, z, s0c[:, m % 2, 0:cn]))
                v_.tensor_scalar(z, z, b0c[:, m // 3:m // 3 + 1], 0.0, ALU.add, ALU.max).then_inc(s_zt, 1)
                dve.wait_ge(s_hh, m + 1)
                v_.tensor_sub(XTl[:, m // 3, c0:c0 + cn], z, XTh[:, m // 3, c0:c0 + cn].bitcast(f32)).then_inc(s_done, 1)
            lows("Y1", 2, 2 * NT, lambda i, j: y1h[:, j % NT, ds(i * 512 + j // NT * WQ, WQ)].bitcast(f32),
                 lambda i, j: y1l[:, j % NT, ds(i * 512 + j // NT * WQ, WQ)], p=T, cols=lambda j: WQ)
            with dve.Fori(0, 2) as i:
                for j in range(2 * NT):
                    slot = (N["S1"] + j) % 4
                    dve.wait_ge(s_acc, i * (2 * NT) + (N["S1"] + j + 1))
                    dve.wait_ge(s_bs[slot], i * 80 + 16 * (j // 4 + 1))
                    v_.tensor_add(bs[:, slot, :], bank(slot, T, WQ), bs[:, slot, :]).then_inc(s_done, 1)
            dve.wait_ge(s_row, 32)
            for t in range(NT + 1):
                if t < NT:
                    s = t % 2
                    dve.wait_ge(s_b2[s], 16 * (t // 2 + 1))
                    if t >= 2:
                        dve.wait_ge(s_x2[s], 16 * (t // 2))
                        dve.wait_ge(s_T, 2 * (NT + t - 1))
                    for c in range(2):
                        m = N["X2"] + 2 * t + c
                        dve.wait_ge(s_acc, m + 1)
                        v_.scalar_tensor_tensor(x2s[:, s, 512 * c:512 * c + 512], bank(m % 4, T, 512), deginv[:, t:t + 1],
                                                b2[:, s, 512 * c:512 * c + 512], ALU.mult, ALU.add).then_inc(s_done, 1)
                    dve.wait_ge(s_done, 4 + N["X2"] + 2 * t + 2)
                    tile_stats(t, x2s[:, s, :])
                    inverse_roots(t, 1)
                    normalise(t, x2s[:, s, :], x2n[:, s, :], s_x2n)
                if t >= 1:
                    transposed_lo(slice((t - 1) * T, t * T), lambda b: 2 * (NT + t - 1) + b + 1, sums=t - 1,
                                  parts=(True, t < NT))
            def combine(q4, kh, q):
                sa, sb_ = wst2[:, kh, 0, :, :], wst2[:, kh, 1, :, :]
                if isinstance(q4, int) and q4 + q == 0:
                    dve.wait_ge(s_we_first[kh], 32)
                else:
                    dve.wait_ge(s_we[kh], q4 * 32 + 32 * q)
                order(v_.tensor_scalar(sa, sa, wsel[:, 0:1], None, ALU.mult))
                v_.scalar_tensor_tensor(sa, sb_, wsel[:, 1:2], sa, ALU.mult, ALU.add).then_inc(s_comb, 1)

            dve.wait_ge(s_dve, own.n)
            order(v_.tensor_reduce(pool8[:, :], pooled[:, :, :].rearrange("p t k -> p k t"), AX.X, ALU.add))
            v_.tensor_scalar(pool8[:, :], pool8[:, :], 1.0 / R, None, ALU.mult).then_inc(s_pool, 1)
            transposed_lo(slice((NT - 1) * T, R), None, parts=(False, True))
            order(v_.memset(gate[:, :], -3.0e38))
            dve.wait_ge(s_gw, 16 * 4)
            dve.wait_ge(s_gmm, 2)
            order(v_.tensor_add(gate[:, 0:NE], bank(7, 1, NE), bgr[:, 0:NE]))
            order(v_.max(gate[:, 8:16], gate[:, 0:8]))
            v_.max_index(gidx[:, :], gate[:, 8:16], gate[:, 0:8]).then_inc(s_top, 1)
            dve.wait_ge(s_top, 1)
            order(v_.tensor_copy(gidxf[:, :], gidx[:, :]))
            v_.tensor_sub(gate[:, 32:33], gate[:, 9:10], gate[:, 8:9]).then_inc(s_pool, 1)
            dve.wait_ge(s_ghid, 2)
            order(v_.tensor_scalar(gate[:, 34:35], gate[:, 33:34], 1.0, None, ALU.add))
            order(v_.reciprocal(gate[:, 40:41], gate[:, 34:35]))
            order(v_.tensor_mul(gate[:, 41:42], gate[:, 33:34], gate[:, 40:41]))
            for e in range(2):
                order(v_.tensor_scalar(gate[:, 44 + 4 * e:48 + 4 * e], iot4[:, :], gidxf[:, e:e + 1],
                                       gate[:, 40 + e:41 + e], ALU.is_equal, ALU.mult))
            v_.tensor_add(gate[:, 52:56], gate[:, 44:48], gate[:, 48:52]).then_inc(s_pool, 1)
            dve.wait_ge(s_gmm, 3)
            order(v_.tensor_copy(w4[:, :], bank(6, NE, 128)))
            v_.tensor_copy(wsel[:, :], bank(7, 128, 2)).then_inc(s_gate, 1)
            dve.wait_ge(s_gate, 1)
            for kh in range(2):
                combine(0, kh, 0)
            for kh in range(2):
                dve.wait_ge(s_whi, 16 + kh + 1)
                v_.tensor_sub(Wl[0][:, 4 * kh:4 * kh + 4, :], wst2[:, kh, 0, :, :],
                              Wh[0][:, 4 * kh:4 * kh + 4, :].bitcast(f32)).then_inc(s_wready, 1)
            dve.wait_ge(s_gmm, 4)
            v_.tensor_copy(qkvb[:, :], bank(6, 128, 3 * KB)).then_inc(s_gate, 1)
            for a, ph in enumerate(("Q", "K")):
                def next_quarter(i, j):
                    if j % 6 in (1, 2):
                        combine(i * 2, j % 6 - 1, 4 * a + j // 6 + 1)
                lows(ph, 2, 12, lambda i, j: ot2[0][:, (N[ph] + j) % 4, 0:CH[j % 3][1]],
                     lambda i, j: ot2[1][:, (N[ph] + j) % 4, 0:CH[j % 3][1]].bitcast(f32r),
                     bias_of=lambda i, j: qkvb[:, ds(i * 4 + (KB * a + j // 3), 1)], cols=lambda j: CH[j % 3][1],
                     before=next_quarter, own=own, own_per=4)
            for q in range(4):
                for t in range(NT):
                    if t in (1, 2) and q < 3:
                        combine(0, t - 1, 8 + q + 1)
                    j = q * NT + t
                    slot = (N["V"] + j) % 4
                    dve.wait_ge(s_hi, HI["V"] + j + 1)
                    v_.tensor_sub(ot2[1][0:T, slot, 0:WQ].bitcast(f32r), bank(slot, T, WQ), ot2[0][0:T, slot, 0:WQ])\
                      .then_inc(s_done, 1)

            def maxima(i, m, first_bank=0):
                n = i * (HB * NT) + m
                dve.wait_ge(s_s, n + 1)
                v_.tensor_reduce(att_m[:, m % 2:m % 2 + 1], ps[0:T, 512 * first_bank:512 * first_bank + R], AX.X, ALU.max)\
                  .then_inc(s_mx, 1)
                dve.wait_ge(s_mx, n + 1)
                if m >= 2:
                    dve.wait_ge(s_mt, n - 1)
                order(v_.tensor_scalar(MB[:, m % 2, HD:HD + 1], att_m[:, m % 2:m % 2 + 1], -1.0, None, ALU.mult))
                v_.scalar_tensor_tensor(MB[:, m % 2, HD + 1:HD + 2], att_m[:, m % 2:m % 2 + 1], -1.0,
                                        MB[:, m % 2, HD:HD + 1].bitcast(f32), ALU.mult, ALU.subtract).then_inc(s_mb, 1)

            def output(i, k, part):
                h, cn = k // 3, CH[k % 3][1]
                rows = slice(HD * (h % 2), HD * (h % 2) + HD)
                if part == 0:
                    dve.wait_ge(s_pv, i * (HB * UN) + (NT * (k + 1) + 4))
                if part < 3:
                    a, b = cn * part // 3, cn * (part + 1) // 3
                    order(v_.reciprocal(RB[:, a:b], ps[HD:128, 2560 + 512 * (k % 2) + a:2560 + 512 * (k % 2) + b]))
                    return
                v_.tensor_mul(OB[k % 2][rows, 0:cn], bank(5 + k % 2, HD, cn), RB[:, 0:cn]).then_inc(s_ob, 1)

            def output_lo(i, k):
                h, (c0, cn) = k // 3, CH[k % 3]
                rows = slice(HD * (h % 2), HD * (h % 2) + HD)
                blk = i * (HB // 2) + h // 2
                dve.wait_ge(s_ao, i * (3 * HB) + (k + 1))
                v_.scalar_tensor_tensor(XTl[rows, ds(blk, 1), c0:c0 + cn].rearrange("p a n -> p (a n)"),
                                        OB[k % 2][rows, 0:cn], qkvb[rows, ds(blk + 2 * KB, 1)],
                                        XTh[rows, ds(blk, 1), c0:c0 + cn].rearrange("p a n -> p (a n)").bitcast(f32),
                                        ALU.add, ALU.subtract).then_inc(s_aol, 1)

            def outputs(i, n, first, last):
                for k, part in output_steps(n, first, last):
                    if part < 4:
                        output(i, k, part)
                    elif part == 5:
                        output_lo(i, k)

            def heads(i, first, last):
                for n in range(HB * UN):
                    h, q = n // UN, n % UN
                    cn = CH[q // NT][1]
                    last_head = last and h == HB - 1
                    if q in SCORES_AT and not last_head:
                        maxima(i, (h + 1) * NT + SCORES_AT.index(q))
                    if n % 3 == 2 or last_head:
                        dve.wait_ge(s_ex, i * (HB * UN) + (n + 1 + 2))
                        v_.tensor_sub(EL[n % 4][:, 0:cn], EX[n % 3][:, 0:cn], EH[n % 4][:, 0:cn].bitcast(f32))\
                          .then_inc(low_written(i, n, last)[0], 1)
                    outputs(i, n, first, last)
                if last:
                    outputs(i, HB * UN, first, last)

            dve.wait_ge(s_fill, 1)
            for t in range(NT):
                maxima(0, t, 3 * (t % 2))
            heads(0, True, False)
            with dve.Fori(0, H // HB - 2) as i:
                own.enter(i, HB * (NT + 3 * 3))
                heads(dve.snap(i + 1), False, False)
            own.leave(H // HB - 2)
            heads(H // HB - 1, False, True)
            dve.wait_ge(s_bo, 16)
            with dve.Fori(0, 2) as i:
                own.enter(i, 2 * NT)
                for j in range(2 * NT):
                    slot, u, t = (N["O"] + j) % 4, j // NT, j % NT
                    dve.wait_ge(s_acc, i * (2 * NT) + (N["O"] + j + 1))
                    dve.wait_ge(s_x2r[slot], i * 80 + 16 * (j // 4 + 1))
                    dve.wait_ge(s_st[slot], i * 80 + (STORED["O"] + 16 * (j // 4)))
                    order(v_.tensor_add(ot[:, slot, :], bank(slot, T, WQ), x2r[:, slot, :]))
                    v_.tensor_add(ot[:, slot, :], ot[:, slot, :], boB[:, ds(i * 512 + u * WQ, WQ)]).then_inc(s_done, 1)
            own.leave(2)

        @block.tensor
        def _(pe):
            mm, tr = nc.tensor.matmul, nc.tensor.transpose
            pe.sem_inc(s_pv, 4)
            pe.sem_inc(s_ohfree, RING // GE)
            pe.wait_ge(s_const, 10)

            def three(dst_, ah, al, bh, bl, start, stop):
                mm(dst_, ah, bh, start=start, stop=False)
                mm(dst_, ah, bl, start=False, stop=False)
                return mm(dst_, al, bh, start=False, stop=stop)

            def wait_weights(i, ph, u):
                pe.wait_ge(s_wready, i * 4 + (2 * (WRDY[ph] + u + 1) + 2))

            def weights_stationary(ph, bh, bl, chunks, after=None):
                per = 4 * len(chunks)
                with pe.Fori(0, 2) as i:
                    for u in range(2):
                        wait_weights(i, ph, u)
                        for b in range(2):
                            for c, (c0, cn) in enumerate(chunks):
                                j = (2 * u + b) * len(chunks) + c
                                slot = (N[ph] + j) % 4
                                pe.wait_ge(s_done, i * per + (N[ph] + j + 1))
                                for k in range(KB):
                                    ins = three(bank(slot, 128, cn), Wh[u][:, k, b * 128:(b + 1) * 128],
                                                Wl[u][:, k, b * 128:(b + 1) * 128], bh[:, k, c0:c0 + cn],
                                                bl[:, k, c0:c0 + cn], k == 0, k == KB - 1)
                                ins.then_inc(s_acc, 1)
                                if after:
                                    after(i, j)

            def weights_moving(ph, ah, al, rows, count, after=None, before=None):
                per = 2 * count
                with pe.Fori(0, 2) as i:
                    for u in range(2):
                        wait_weights(i, ph, u)
                        for t in range(count):
                            j = u * count + t
                            slot = (N[ph] + j) % 4
                            pe.wait_ge(s_done, i * per + (N[ph] + j + 1))
                            if before:
                                before(t)
                            for k in range(KB):
                                ins = three(bank(slot, rows, WQ), ah[:, k, t * rows:(t + 1) * rows],
                                            al[:, k, t * rows:(t + 1) * rows], Wh[u][:, k, :], Wl[u][:, k, :],
                                            k == 0, k == KB - 1)
                            ins.then_inc(s_acc, 1)
                            if after:
                                after(i, j)

            tot = pe.alloc_register("groups_pe")
            pe.reg_mov(tot, 0)

            def window(w, u):
                cnt = pe.value_load(bint[0:1, 1, ds(w, 1)], min_val=1, max_val=NG)
                before = pe.snap(tot, min_val=0, max_val=NW * NG)
                pe.wait_ge(s_winev, w + 1)
                acc = bank(4 + u, 128, KW)
                mm(acc, zw[:, :], iot[0:T, :], start=True, stop=False)
                with pe.Fori(0, cnt) as k:
                    r = pe.snap(((before + k) & (RING // GE - 1)) * GE, min_val=0, max_val=RING - GE)
                    pe.wait_ge(s_oh, (before + k) + 1)
                    ohs_, ohk_ = ohs[:, ds(r, GE), :], ohk[:, ds(r, GE), :]
                    for m in range(GE):
                        ins = mm(acc, ohs_[:, m, :], ohk_[:, m, :], start=False, stop=False)
                    ins.then_inc(s_ohfree, 1)
                mm(acc, zw[:, :], iot[0:T, :], start=False, stop=True).then_inc(s_win, 1)
                pe.reg_add(tot, tot, cnt)

            def transposes(src_, sem_):
                for b in range(2):
                    for k in range(4):
                        c0 = (4 * b + k) * 128
                        ins = tr(bank(4 + b, 128, T, k * T), src_[:, c0:c0 + 128], ident[0:T, 0:T])
                    ins.then_inc(sem_, 1)

            pe.wait_ge(s_proj, 17)

            for t in range(NT):
                if t < 8:
                    for b in range(2):
                        j = 2 * t + b
                        pe.wait_ge(s_done, j + 1)
                        for k in range(KB):
                            if b == 0 and k % (KB // 2) == 0:
                                pe.wait_ge(s_wready, 2 * t + 2 + k // (KB // 2) + 1)
                            ins = three(bank(j % 4, 128, PF_), Wh[t % 2][:, k, b * 128:(b + 1) * 128],
                                        Wl[t % 2][:, k, b * 128:(b + 1) * 128], prh[:, k, :], prl[:, k, :],
                                        k == 0, k == KB - 1)
                        ins.then_inc(s_acc, 1)
                pe.wait_ge(s_xn, t + 1)
                if t:
                    pe.wait_ge(s_Tlo, 2 * t)
                transposes(xn[:, t % 2, :], s_T)
            pe.wait_ge(s_done, 4 + N["GT"])
            pe.wait_ge(s_Tlo, 2 * NT)
            for t in range(1, NT + 2):
                if t <= NT:
                    m = t - 1
                    if m >= 2:
                        pe.wait_ge(s_elf, m - 1)
                    for k in range(KB):
                        ins = three(bank(6 + m % 2, T, PF_), XTh[:, k, m * T:t * T], XTl[:, k, m * T:t * T],
                                    Mkh[:, k, :], Mkl[:, k, :], k == 0, k == KB - 1)
                    ins.then_inc(s_kp, 1)
                if t >= 2:
                    m = t - 2
                    pe.wait_ge(s_ell, m + 1)
                    pe.wait_ge(s_xl, m + 1)
                    for k in range(KB):
                        dst_ = bank(k // 2, 128, PF_, PF_ * (k % 2))
                        ah, al = (a[m % 2][:, k * 128:(k + 1) * 128] for a in (xnh, xnl))
                        bh, bl = kph[:, m % 2, :], kpl[:, m % 2, :]
                        mm(dst_, ah, bh, start=m == 0 and k % 2 == 0, stop=False, skip_group_check=True)
                        mm(dst_, ah, bl, start=False, stop=False, skip_group_check=True)
                        ins = mm(dst_, al, bh, start=False, stop=m == NT - 1, skip_group_check=True)
                        if m == NT - 1 and k % 2:
                            ins.then_inc(s_acc, 1)
                            if k == KB - 1:
                                pe.wait_ge(s_acc, N["GT"] + 4)
                                pe.sem_inc(s_G, 1)
                    if m < NT - 1:
                        ins.then_inc(s_G, 1)
            pe.wait_ge(s_elf, NT)
            for a in range(2):
                pe.wait_ge(s_idx, a + 1)
                for e in range(GE):
                    ins = tr(bank(4 + a, T, NG, e * NG), ef[:, 4 + a, e * T:(e + 1) * T], ident[0:NG, 0:NG])
                ins.then_inc(s_idxT, 1)
            for j in range(PB * 3):
                if j == 1:
                    pe.wait_ge(s_idx, 4)
                    for a in range(2):
                        ins = tr(bank(6, NW, NG, a * NG), cond[:, 1 + a, :], ident[0:NG, 0:NG])
                    ins.then_inc(s_idxT, 1)
                if j == 3:
                    pe.wait_ge(s_idx, 6)
                    for a in range(2):
                        ins = tr(bank(7, 1, NW, a * NW), bnd[:, a:a + 1], ident[0:NW, 0:NW])
                    ins.then_inc(s_idxT, 1)
                n_ = N["QP"] + j
                c0, cn = CH[j % 3]
                pb = j // 3
                pe.wait_ge(s_done, n_ + 1)
                for k in range(KB):
                    ins = three(bank(n_ % 4, 128, cn), Mqh[:, k, pb * 128:(pb + 1) * 128],
                                Mql[:, k, pb * 128:(pb + 1) * 128], XTh[:, k, c0:c0 + cn], XTl[:, k, c0:c0 + cn],
                                k == 0, k == KB - 1)
                ins.then_inc(s_acc, 1)
            wst_rows = Wst[:, :, :, :].rearrange("p a b c -> p (a b c)").rearrange("p (e n) -> p e n", e=2)
            pe.wait_ge(s_bnd, 1)
            for j in range(4):
                pe.wait_ge(s_wv, 16 * (j + 1))
                for b in range(4):
                    if j:
                        pe.wait_ge(s_wtlo, 4 * (j - 1) + b + 1)
                    for k in range(2):
                        for e in range(2):
                            c0 = (2 * b + k) * 128
                            ins = tr(bank(4 + b, 128, 128, k * WQ + e * 128), wst_rows[:, e, c0:c0 + 128], ident[:, :])
                    ins.then_inc(s_wt, 1)
                pe.wait_ge(s_wtlo, 4 * j + 4)
                for b in range(PB):
                    n_ = N["KV"] + PB * j + b
                    pe.wait_ge(s_done, n_ + 1)
                    for k in range(KB):
                        ins = three(bank(n_ % 4, 128, WQ), GTh[:, k, b * 128:(b + 1) * 128],
                                    GTl[:, k, b * 128:(b + 1) * 128], Wh[j % 2][:, k, :], Wl[j % 2][:, k, :],
                                    k == 0, k == KB - 1)
                    ins.then_inc(s_acc, 1)
            pe.wait_ge(s_ell, NT + PB * 3)
            pe.wait_ge(s_done, 4 + N["NUM"])
            for t in range(NT):
                rows = slice(t * T, (t + 1) * T)
                if t >= 2:
                    pe.wait_ge(s_done, 4 + N["NUM"] + 2 * (t - 2) + 1)
                for b in range(PB):
                    mm(bank(4 + t % 2, T, 2), qph[:, b, rows], onesr[:, :], start=b == 0, stop=False)
                    ins = mm(bank(4 + t % 2, T, 2), qpl[:, b, rows], onesr[:, :], start=False, stop=b == PB - 1)
                ins.then_inc(s_z, 1)
                for c in range(2):
                    n_ = N["NUM"] + 2 * t + c
                    pe.wait_ge(s_done, n_ + 1)
                    for b in range(PB):
                        ins = three(bank(n_ % 4, T, 512), qph[:, b, rows], qpl[:, b, rows],
                                    kvh[:, b, 512 * c:512 * c + 512], kvl[:, b, 512 * c:512 * c + 512],
                                    b == 0, b == PB - 1)
                    ins.then_inc(s_acc, 1)
            def y0_windows(i, j):
                if j in WIN_Y0:
                    k = WIN_Y0.index(j)
                    window(pe.snap(i * len(WIN_Y0) + k), k % 2)

            weights_moving("Y0", XTh, XTl, T, NT, after=y0_windows)
            def s0_windows(i, j):
                for k in WIN_S0[j]:
                    window(pe.snap(i * NS0 + (2 * len(WIN_Y0) + k)), k % 2)

            weights_stationary("S0", XTh, XTl, CH, after=s0_windows)
            pe.wait_ge(s_degp, 2 + 2 * NS0)
            for c, (c0, cn) in enumerate(CH):
                mm(bank((6, 7, 4)[c], 128, cn), ones[0:T, :], degp[:, c0:c0 + cn], start=True, stop=True)\
                    .then_inc(s_deg, 1)
            pe.wait_ge(s_slow, 1)
            slow_ = pe.value_load(slow[0:1, 0:1], min_val=0, max_val=1)

            def counts_product(dst_, ys, a, exact_first):
                n_s = len(ys)
                for s_i in range(n_s):
                    yh, yl, ad = ys[s_i]
                    for part, y_ in enumerate((yh, yl)):
                        y_, ad_ = (y_, ad) if exact_first else (y_.bitcast(f32), ad.bitcast(f32))
                        l_, r_ = (y_, ad_) if a else (ad_, y_)
                        ins = mm(dst_, l_, r_, start=s_i == 0 and part == 0, stop=s_i == n_s - 1 and part == 1)
                return ins


            def aggregate_cols(fast):
                for blk in range(KB):
                    for c, (c0, cn) in enumerate(CH):
                        m = 3 * blk + c
                        if c == 0:
                            pe.wait_ge(s_y0[blk % 2], 32 * (blk // 2 + 1))
                        pe.wait_ge(s_done, N["HT"] + m + 1)
                        ins = counts_product(bank((N["HT"] + m) % 4, 128, cn),
                                             [(y0sh[blk % 2][:, s, :], y0sl[blk % 2][:, s, :], adjr[:, s, c0:c0 + cn])
                                              for s in range(NT)], True, fast)
                        ins.then_inc(s_acc, 1)

            with pe.If(slow_ == 0):
                aggregate_cols(True)
            with pe.Else():
                aggregate_cols(False)
            pe.wait_ge(s_done, 4 + N["Y1"])
            weights_moving("Y1", XTh, XTl, T, NT)
            weights_moving("S1", XTh, XTl, T, NT)
            pe.wait_ge(s_done, 4 + N["S1"])

            def aggregate_rows(fast):
                for t in range(NT + 1):
                    if t < NT:
                        pe.wait_ge(s_at[t % 2], 16 * (t // 2 + 1))
                        for c in range(2):
                            n_ = N["X2"] + 2 * t + c
                            cols = slice(512 * c, 512 * c + 512)
                            pe.wait_ge(s_done, n_ + 1)
                            ins = counts_product(bank(n_ % 4, T, 512),
                                                 [(y1h[:, s, cols], y1l[:, s, cols], adt[t % 2][:, s, 0:T])
                                                  for s in range(NT)], False, fast)
                            ins.then_inc(s_acc, 1)
                    if t:
                        pe.wait_ge(s_x2n, t)
                        if t > 1:
                            pe.wait_ge(s_Tlo, 2 * (NT + t - 1))
                        transposes(x2n[:, (t - 1) % 2, :], s_T)

            with pe.If(slow_ == 0):
                aggregate_rows(True)
            with pe.Else():
                aggregate_rows(False)
            pe.wait_ge(s_pool, 1)
            pe.wait_ge(s_gw, 64)
            for k in range(KB):
                ins = mm(bank(6, 128, 1), wg1[:, k, :], pool8[:, k:k + 1], start=k == 0, stop=k == KB - 1)
            ins.then_inc(s_gmm, 1)
            pe.wait_ge(s_ghid, 1)
            mm(bank(7, 1, NE), hid[:, :], wg2[:, :], start=True, stop=True).then_inc(s_gmm, 1)
            pe.wait_ge(s_pool, 3)
            mm(bank(6, NE, 128), gate[:, 52:56], ones[0:1, :], start=True, stop=True)
            mm(bank(7, 128, 2), ones[0:1, :], gate[:, 40:42], start=True, stop=True).then_inc(s_gmm, 1)
            pe.wait_ge(s_gate, 1)
            pe.wait_ge(s_eb, 16 * 3)
            pe.wait_ge(s_Tlo, 4 * NT)
            for a in range(3):
                for k in range(KB):
                    ins = mm(bank(6, 128, 1, a * KB + k), b3[:, a, k * 128:(k + 1) * 128], w4[:, 0:1], start=True, stop=True)
            ins.then_inc(s_gmm, 1)
            pe.wait_ge(s_gate, 2)
            weights_stationary("Q", XTh, XTl, CH)
            weights_stationary("K", XTh, XTl, CH)
            weights_moving("V", XTh, XTl, T, NT)

            def query_scores(i, m, first_bank=0):
                n, t, k = i * (HB * NT) + m, m % NT, m // NT % HB
                if m:
                    if first_bank == 0 or m >= 2:
                        pe.wait_ge(s_mx, n if m >= NT else m - 1)
                if m == 0:
                    pe.wait_ge(s_qk_first, 96)
                elif t == 0:
                    pe.wait_ge(s_qk[k], i * 96 + 96 * (m // NT // HB + (1 if k else 0)))
                for c0, cn in SCH:
                    dst_ = ps[0:T, 512 * first_bank + c0:512 * first_bank + c0 + cn]
                    mm(dst_, QS[k][:, t * T:(t + 1) * T], KH[k][:, c0:c0 + cn], start=True, stop=False)
                    ins = mm(dst_, QS[k][0:HD, t * T:(t + 1) * T], KM[k][0:HD, c0:c0 + cn], start=False, stop=True)
                ins.then_inc(s_s, 1)

            def maxima_row(i, m):
                t = m % NT
                grp = [t in range(a, b) for a, b in MG].index(True)
                pe.wait_ge(s_mb, i * (HB * NT) + (m + 1))
                if t == MG[grp][0] and m:
                    pe.wait_ge(s_mr, i * (3 * HB) + (m // NT * 3 + grp))
                tr(bank(7, HD + 2, T, (t - MG[grp][0]) * T), MB[:, m % 2, :].bitcast(f32), ident[0:T, 0:T])\
                    .then_inc(s_mt, 1)

            def key_scores(i, n):
                k, q = n // UN, n % UN
                (c0, cn), j = CH[q // NT], q % NT
                keys = slice(j * T, (j + 1) * T)
                if q == 0:
                    pe.wait_ge(s_mr, i * (3 * HB) + 3 * (k + 1))
                pe.wait_ge(s_ex, i * (HB * UN) + (n + 1))
                mm(bank(3 + n % 2, T, cn), KH[k][:, keys], QS[k][:, c0:c0 + cn], start=True, stop=False)
                mm(bank(3 + n % 2, T, cn), KM[k][:, keys], QM[k][:, c0:c0 + cn], start=False, stop=True)\
                    .then_inc(s_sc, 1)

            def values(i, n, last):
                h, q = n // UN, n % UN
                cn, j = CH[q // NT][1], q % NT
                chunk = 3 * h + q // NT
                out_ = 5 + chunk % 2
                if q == 0:
                    pe.wait_ge(s_v[h % 2], i * (16 * HB) + 32 * (h // 2 + 1))
                if j == 0:
                    pe.wait_ge(s_ob, i * (3 * HB) + (chunk + 1))
                pe.wait_ge(s_eh, i * (HB * UN) + (n + 1))
                mm(bank(out_, 128, cn), VS[h % 2][:, j, :], EH[n % 4][:, 0:cn], start=j == 0, stop=False)
                mm(bank(out_, HD, cn), VL[h % 2][:, j, :], EH[n % 4][:, 0:cn], start=False, stop=False)
                pe.wait_ge(*low_written(i, n, last))
                mm(bank(out_, 128, cn), VS[h % 2][:, j, :], EL[n % 4][:, 0:cn], start=False, stop=j == NT - 1)\
                    .then_inc(s_pv, 1)

            def heads(i, first, last):
                for n in range(HB * UN + (LAG if last else 0)):
                    h, q = n // UN, n % UN
                    ahead = not (last and h == HB - 1) and n < HB * UN
                    if q in SCORES_AT and ahead:
                        query_scores(i, (h + 1) * NT + SCORES_AT.index(q))
                    if n < HB * UN:
                        key_scores(i, n)
                    if n >= LAG or not first:
                        values(i, n - LAG, last)
                    if q in ROWS_AT and ahead:
                        maxima_row(i, (h + 1) * NT + ROWS_AT.index(q))

            pe.wait_ge(s_done, 4 + N["O"])
            for t in range(NT):
                query_scores(0, t, 3 * (t % 2))
                if t:
                    maxima_row(0, t - 1)
            maxima_row(0, NT - 1)
            pe.wait_ge(s_fill, HB + 3)
            heads(0, True, False)
            with pe.Fori(0, H // HB - 2) as i:
                heads(pe.snap(i + 1), False, False)
            heads(H // HB - 1, False, True)
            def chunks_written(t):
                pe.wait_ge(s_aol, 3 * (H - 1) + [(t + 1) * T <= c0 + cn for c0, cn in CH].index(True) + 1)

            weights_moving("O", XTh, XTl, T, NT, before=chunks_written)


_INS = ['x', 'src', 'dst', 'L0_gnn_W_self0', 'L0_gnn_W_neigh0', 'L0_gnn_b0', 'L0_gnn_W_self1', 'L0_gnn_W_neigh1',
        'L0_gnn_b1', 'L0_mix_Wq', 'L0_mix_Wk', 'L0_mix_Wv', 'L0_mix_proj', 'L0_ffn_Wq', 'L0_ffn_bq', 'L0_ffn_Wk',
        'L0_ffn_bk', 'L0_ffn_Wv', 'L0_ffn_bv', 'L0_ffn_Wg1', 'L0_ffn_bg1', 'L0_ffn_Wg2', 'L0_ffn_bg2', 'L0_ffn_Wo',
        'L0_ffn_bo']
_OUTS = [((1250, 1024), 'float32')]
_SCRATCH = [("adj", (1250, 1280)), ("base", (1250, 1024)), ("y0hi", (1250, 1024)), ("y0lo", (1250, 1024)),
            ("s0T", (1024, 1250)), ("x2d", (1250, 1024)),
            ("qhi", (1024, 1250)), ("qlo", (1024, 1250)), ("khi", (1024, 1250)), ("klo", (1024, 1250)), ("vhi", (1250, 1024)), ("vlo", (1250, 1024)),
            ("degrow", (1250,))]


def kernel(**inputs):
    import numpy as _np
    import concourse.bacc as _bacc
    from concourse import mybir as _mybir
    from concourse.bass_utils import run_bass_kernel_spmd as _run

    nc = _bacc.Bacc("TRN2", target_bir_lowering=False, num_devices=1)
    arrays, args = {}, []
    for name in _INS:
        a = _np.ascontiguousarray(inputs[name])
        arrays[f"in_{name}_dram"] = a
        args.append(nc.dram_tensor(f"in_{name}_dram", a.shape, _mybir.dt.from_np(a.dtype), kind="ExternalInput").ap())
    for i, (shape, dtype) in enumerate(_OUTS):
        dt = _mybir.dt.from_np(_np.dtype(dtype))
        args.append(nc.dram_tensor(f"out_{i}_dram", shape, dt, kind="ExternalOutput").ap())
    for name, shape in _SCRATCH:
        args.append(nc.dram_tensor(f"scratch_{name}", shape, _mybir.dt.float32, kind="Internal").ap())
    gps_layer_kernel(nc, *args)
    r = _run(nc, [arrays], core_ids=[0])
    got = tuple(r.results[0][f"out_{i}_dram"] for i in range(len(_OUTS)))
    return got[0]
```
